# Optimizing a Trainium2 kernel written in Bass

```python
import numpy as np
import jax
import jax.numpy as jnp

def _softmax(x, axis=-1):
    return jax.nn.softmax(x, axis=axis)

def _gelu(x):
    return jax.nn.gelu(x, approximate=True)

def _silu(x):
    return jax.nn.silu(x)

def _sigmoid(x):
    return jax.nn.sigmoid(x)

def _layernorm(x, axis=-1, eps=1e-05):
    m = jnp.mean(x, axis=axis, keepdims=True)
    v = jnp.var(x, axis=axis, keepdims=True)
    return (x - m) / jnp.sqrt(v + eps)

def _scatter_add(tgt, idx, src, axis=0):
    return tgt.at[idx].add(src)

def _segment_sum(src, seg, n):
    return jax.ops.segment_sum(src, seg, n)
kernel_name = 'mk_gps_d1_gnn_r32_9541a4'

def setup_inputs(seed: int=0):
    np.random.seed(seed)
    _w = jnp.asarray

    def _rec_inputs():
        import jax
        import jax.numpy as jnp
        _gk = jax.random.key(seed)
        x = -0.0002117 + 1 * jax.random.normal(jax.random.fold_in(_gk, 1), (3125, 256), jnp.float32)
        src = jax.random.randint(jax.random.fold_in(_gk, 2), (50000,), 0, 3125, jnp.int32)
        dst = jax.random.randint(jax.random.fold_in(_gk, 3), (50000,), 0, 3125, jnp.int32)
        _o = jnp.argsort(dst, stable=True)
        src = src[_o]
        dst = dst[_o]
        edge_weight = jax.random.uniform(jax.random.fold_in(_gk, 12), (50000,), jnp.float32, 0.0, 1)
        return (x, src, dst, edge_weight)
    x, src, dst, edge_weight = _rec_inputs()

    def _L0_gnn_setup():
        import jax, jax.numpy as jnp
        import numpy as np
        N = 3125
        D_IN = 256
        D_OUT = 256
        E = 100000
        key = jax.random.key(seed)
        ks = jax.random.split(key, 9)
        x = jax.random.normal(ks[0], (N, D_IN), dtype=jnp.float32)
        edge_src = jax.random.randint(ks[1], (E,), 0, N, dtype=jnp.int32)
        edge_dst = jax.random.randint(ks[2], (E,), 0, N, dtype=jnp.int32)
        edge_weight = jax.random.uniform(ks[3], (E,), dtype=jnp.float32)
        eps = jnp.zeros((1,), dtype=jnp.float32)
        lim1 = 1.0 / np.sqrt(D_IN)
        w1 = jax.random.uniform(ks[4], (D_IN, D_OUT), minval=-lim1, maxval=lim1, dtype=jnp.float32)
        b1 = jax.random.uniform(ks[5], (D_OUT,), minval=-lim1, maxval=lim1, dtype=jnp.float32)
        lim2 = 1.0 / np.sqrt(D_OUT)
        w2 = jax.random.uniform(ks[6], (D_OUT, D_OUT), minval=-lim2, maxval=lim2, dtype=jnp.float32)
        b2 = jax.random.uniform(ks[7], (D_OUT,), minval=-lim2, maxval=lim2, dtype=jnp.float32)
        return {'x': x, 'edge_src': edge_src, 'edge_dst': edge_dst, 'edge_weight': edge_weight, 'eps': eps, 'w1': w1, 'b1': b1, 'w2': w2, 'b2': b2}
    _L0_gnn_all = _L0_gnn_setup()
    _L0_gnn_in = {k: v for k, v in _L0_gnn_all.items() if k in ('eps', 'w1', 'b1', 'w2', 'b2')}
    del _L0_gnn_all

    def _L0_mix_setup():
        import jax, jax.numpy as jnp
        import numpy as np
        NHEAD = 8
        ATT_EPS = 1e-06
        LN_EPS = 1e-05

        def _layernorm(x, g, b):
            mu = jnp.mean(x, axis=-1, keepdims=True)
            var = jnp.mean(jnp.square(x - mu), axis=-1, keepdims=True)
            return (x - mu) * jax.lax.rsqrt(var + LN_EPS) * g + b
        key = jax.random.key(seed)
        ks = jax.random.split(key, 7)
        N, L, C = (4, 512, 256)
        s = 1.0 / np.sqrt(C)
        return {'x': jax.random.normal(ks[0], (N, L, C), jnp.float32), 'Wq': jax.random.normal(ks[1], (C, C), jnp.float32) * s, 'Wk': jax.random.normal(ks[2], (C, C), jnp.float32) * s, 'Wv': jax.random.normal(ks[3], (C, C), jnp.float32) * s, 'Wm': jax.random.normal(ks[4], (C, C), jnp.float32) * s, 'W1': jax.random.normal(ks[5], (2 * C, 2 * C), jnp.float32) * (1.0 / np.sqrt(2 * C)), 'W2': jax.random.normal(ks[6], (2 * C, C), jnp.float32) * (1.0 / np.sqrt(2 * C)), 'g1': jnp.ones((C,), jnp.float32), 'b1': jnp.zeros((C,), jnp.float32), 'g2': jnp.ones((C,), jnp.float32), 'b2': jnp.zeros((C,), jnp.float32)}
    _L0_mix_all = _L0_mix_setup()
    _L0_mix_in = {k: v for k, v in _L0_mix_all.items() if k in ('Wq', 'Wk', 'Wv', 'Wm', 'W1', 'W2', 'g1', 'b1', 'g2', 'b2')}
    del _L0_mix_all

    def _L0_ffn_setup():
        import jax, jax.numpy as jnp
        import numpy as np
        B, T, D, H, E = (16, 128, 256, 512, 8)
        key = jax.random.key(seed)
        ks = jax.random.split(key, 5)
        x = jax.random.normal(ks[0], (B, T, D), dtype=jnp.float32)
        gate_w = jax.random.normal(ks[1], (D, E), dtype=jnp.float32) * 0.02
        gate_b = jnp.zeros((E,), dtype=jnp.float32)
        W1 = jax.random.normal(ks[2], (E, D, H), dtype=jnp.float32) * 0.02
        b1 = jnp.zeros((E, H), dtype=jnp.float32)
        W2 = jax.random.normal(ks[3], (E, H, D), dtype=jnp.float32) * 0.02
        b2 = jnp.zeros((E, D), dtype=jnp.float32)
        return {'x': x, 'gate_w': gate_w, 'gate_b': gate_b, 'W1': W1, 'b1': b1, 'W2': W2, 'b2': b2}
    _L0_ffn_all = _L0_ffn_setup()
    _L0_ffn_in = {k: v for k, v in _L0_ffn_all.items() if k in ('gate_w', 'gate_b', 'W1', 'b1', 'W2', 'b2')}
    del _L0_ffn_all
    return {'x': x, 'src': src, 'dst': dst, 'edge_weight': edge_weight, 'L0_gnn_eps': _L0_gnn_in['eps'], 'L0_gnn_w1': _L0_gnn_in['w1'], 'L0_gnn_b1': _L0_gnn_in['b1'], 'L0_gnn_w2': _L0_gnn_in['w2'], 'L0_gnn_b2': _L0_gnn_in['b2'], 'L0_mix_Wq': _L0_mix_in['Wq'], 'L0_mix_Wk': _L0_mix_in['Wk'], 'L0_mix_Wv': _L0_mix_in['Wv'], 'L0_mix_Wm': _L0_mix_in['Wm'], 'L0_mix_W1': _L0_mix_in['W1'], 'L0_mix_W2': _L0_mix_in['W2'], 'L0_mix_g1': _L0_mix_in['g1'], 'L0_mix_b1': _L0_mix_in['b1'], 'L0_mix_g2': _L0_mix_in['g2'], 'L0_mix_b2': _L0_mix_in['b2'], 'L0_ffn_gate_w': _L0_ffn_in['gate_w'], 'L0_ffn_gate_b': _L0_ffn_in['gate_b'], 'L0_ffn_W1': _L0_ffn_in['W1'], 'L0_ffn_b1': _L0_ffn_in['b1'], 'L0_ffn_W2': _L0_ffn_in['W2'], 'L0_ffn_b2': _L0_ffn_in['b2']}

def reference(x, src, dst, edge_weight, L0_gnn_eps, L0_gnn_w1, L0_gnn_b1, L0_gnn_w2, L0_gnn_b2, L0_mix_Wq, L0_mix_Wk, L0_mix_Wv, L0_mix_Wm, L0_mix_W1, L0_mix_W2, L0_mix_g1, L0_mix_b1, L0_mix_g2, L0_mix_b2, L0_ffn_gate_w, L0_ffn_gate_b, L0_ffn_W1, L0_ffn_b1, L0_ffn_W2, L0_ffn_b2):
    import jax
    import jax.numpy as jnp

    def _L0_gnn_ref(x, edge_src, edge_dst, edge_weight, eps, w1, b1, w2, b2):
        import jax, jax.numpy as jnp
        import numpy as np
        N = 3125
        D_IN = 256
        D_OUT = 256
        E = 100000
        msgs = edge_weight[:, None] * x[edge_src]
        agg = jax.ops.segment_sum(msgs, edge_dst, num_segments=N)
        h = (1.0 + eps[0]) * x + agg
        h = jax.nn.relu(h @ w1 + b1)
        return h @ w2 + b2

    def _L0_mix_ref(x, Wq, Wk, Wv, Wm, W1, W2, g1, b1, g2, b2):
        import jax, jax.numpy as jnp
        import numpy as np
        NHEAD = 8
        ATT_EPS = 1e-06
        LN_EPS = 1e-05

        def _layernorm(x, g, b):
            mu = jnp.mean(x, axis=-1, keepdims=True)
            var = jnp.mean(jnp.square(x - mu), axis=-1, keepdims=True)
            return (x - mu) * jax.lax.rsqrt(var + LN_EPS) * g + b
        N, L, C = x.shape
        H = NHEAD
        D = C // H
        q = (x @ Wq).reshape(N, L, H, D)
        k = (x @ Wk).reshape(N, L, H, D)
        v = (x @ Wv).reshape(N, L, H, D)
        Q = jax.nn.elu(q) + 1.0
        K = jax.nn.elu(k) + 1.0
        v = v / L
        KV = jnp.einsum('nshd,nshv->nhdv', K, v)
        Z = 1.0 / (jnp.einsum('nlhd,nhd->nlh', Q, K.sum(axis=1)) + ATT_EPS)
        msg = jnp.einsum('nlhd,nhdv,nlh->nlhv', Q, KV, Z) * L
        msg = msg.reshape(N, L, C) @ Wm
        msg = _layernorm(msg, g1, b1)
        h = jnp.concatenate([x, msg], axis=-1) @ W1
        h = jax.nn.relu(h) @ W2
        msg = _layernorm(h, g2, b2)
        return x + msg

    def _L0_ffn_ref(x, gate_w, gate_b, W1, b1, W2, b2):
        import jax, jax.numpy as jnp
        import numpy as np
        B, T, D, H, E = (16, 128, 256, 512, 8)
        Bb, Tt, Dd = x.shape
        Ee = gate_w.shape[1]
        xf = x.reshape(-1, Dd)
        N = xf.shape[0]
        logits = xf @ gate_w + gate_b
        probs = jax.nn.softmax(logits, axis=-1)
        top2_vals, top2_idx = jax.lax.top_k(probs, 2)
        cw = jnp.zeros((N, Ee), dtype=xf.dtype).at[jnp.arange(N)[:, None], top2_idx].add(top2_vals)

        def step(acc, params):
            w1, bb1, w2, bb2, we = params
            h = jax.nn.gelu(xf @ w1 + bb1, approximate=False)
            y = h @ w2 + bb2
            return (acc + we[:, None] * y, None)
        out, _ = jax.lax.scan(step, jnp.zeros_like(xf), (W1, b1, W2, b2, cw.T))
        return out.reshape(Bb, Tt, Dd)
    xn = _layernorm(x, axis=-1)
    x = x + _L0_gnn_ref(xn, src, dst, edge_weight, L0_gnn_eps, L0_gnn_w1, L0_gnn_b1, L0_gnn_w2, L0_gnn_b2) + _L0_mix_ref(xn[None], L0_mix_Wq, L0_mix_Wk, L0_mix_Wv, L0_mix_Wm, L0_mix_W1, L0_mix_W2, L0_mix_g1, L0_mix_b1, L0_mix_g2, L0_mix_b2)[0]
    x = x + _L0_ffn_ref(_layernorm(x, axis=-1)[None], L0_ffn_gate_w, L0_ffn_gate_b, L0_ffn_W1, L0_ffn_b1, L0_ffn_W2, L0_ffn_b2)[0]
    return x

_drawn_inputs = setup_inputs


def setup_inputs(seed=0):
    import zlib

    import numpy as np

    out = dict(_drawn_inputs(seed))
    spreads = {'L0_mix_g1': (1.0, 0.2),
     'L0_mix_b1': (0.0, 0.275),
     'L0_mix_g2': (1.0, 0.2),
     'L0_mix_b2': (0.0, 0.1),
     'L0_ffn_gate_b': (0.0, 0.8),
     'L0_ffn_b1': (0.0, 0.8),
     'L0_ffn_b2': (0.0, 0.737)}
    factors = {'L0_gnn_b1': 8.0,
     'L0_gnn_b2': 3.653,
     'L0_ffn_gate_w': 4.847,
     'L0_ffn_W1': 6.842,
     'L0_ffn_W2': 6.451}
    for name, (base, spread) in spreads.items():
        noise = np.random.default_rng([zlib.crc32(name.encode()), seed]).standard_normal(out[name].shape)
        drawn = base * np.exp(spread * noise) if base else spread * noise
        out[name] = jnp.asarray(drawn.astype(out[name].dtype))
    for name, factor in factors.items():
        out[name] = (out[name] * factor).astype(out[name].dtype)
    return out
```

```python
from contextlib import ExitStack

import concourse.bass as bass
from concourse import mybir

F32 = mybir.dt.float32
I32 = mybir.dt.int32
ALU = mybir.AluOpType
ACT = mybir.ActivationFunctionType
AX = mybir.AxisListType

P = 128
WIN = 64
WIDE = 400
LN_EPS = 1e-5
ATT_EPS = 1e-6


class Steps:

    def __init__(self, sem):
        self.sem, self.before, self.here, self.loop = sem, 0, 0, 0

    def enter(self, i, per):
        self.before, self.here, self.loop, self.per = self.before + self.here, 0, i * per, per

    def leave(self, n):
        assert self.here == self.per, (self.here, self.per)
        self.before, self.here, self.loop = self.before + n * self.per, 0, 0

    def mark(self, ins):
        ins.then_inc(self.sem, 1)
        self.here += 1
        return self.loop + (self.before + self.here)


def graph_layer(nc, a, out):
    N, D = a["x"].shape
    E = a["src"].shape[0]
    NT = -(-N // P)
    NP = NT * P
    LAST = N - (NT - 1) * P
    KH = D // P
    EW = 2 * P
    GROUPS = 2 * NT * 4
    GI = 4
    SLOTS = 2 * GI
    GFULL, GREST = E // EW, E % EW
    GB = GFULL - P
    assert KH == 2 and E <= GROUPS * EW and 0 < GB < P and GROUPS <= 2 * P
    H1 = a["L0_mix_W1"].shape[1]
    NE, _, HE = a["L0_ffn_W1"].shape
    HC = HE // P
    HEADS = 8
    DH = D // HEADS
    PAIRS = 2 * N
    XT_TILES = (PAIRS + NE * (P - 1)) // P
    XT_TILES += XT_TILES % 2

    ctx = ExitStack()
    sb = lambda n, s, d=F32: ctx.enter_context(nc.sbuf_tensor(n, s, d))
    sem = lambda n: ctx.enter_context(nc.semaphore(n))
    bank = [ctx.enter_context(nc.psum_tensor(f"bank{i}", [P, 512], F32)) for i in range(8)]
    ds = bass.ds

    xn_rows = nc.dram_tensor("xn_rows", [NP, D], F32, kind="Internal").ap()
    lists = nc.dram_tensor("expert_lists", [XT_TILES * P, D], F32, kind="Internal").ap()
    results = nc.dram_tensor("expert_results", [XT_TILES * P, D], F32, kind="Internal").ap()

    w_kv = sb("w_kv", [P, KH, 2 * D]); w_q = sb("w_q", [P, KH, D]); w_m = sb("w_m", [P, KH, D])
    w_1 = sb("w_1", [P, 2 * KH, H1]); w_2 = sb("w_2", [P, H1 // P, D])
    g_w1 = sb("g_w1", [P, KH, D]); g_w2 = sb("g_w2", [P, KH, D]); gate_w = sb("gate_w", [P, KH, NE])
    g_b1 = sb("g_b1", [P, KH]); m_g1 = sb("m_g1", [P, KH]); m_b1 = sb("m_b1", [P, KH])
    eps1 = sb("eps1", [P, 1])
    row_g2 = sb("row_g2", [P, D]); row_b2 = sb("row_b2", [P, D]); row_gb2 = sb("row_gb2", [P, D])
    gate_b = sb("gate_b_rows", [P, NE])
    e_w1 = sb("e_w1", [P, KH, NE * HE])
    e_b1 = sb("e_b1", [P, NE * HC]); e_b2 = sb("e_b2", [P, NE * D])

    xres = sb("xres", [P, NT, D])
    xT = sb("xT", [P, KH, NP])
    aggT = sb("aggT", [P, KH, NP])
    q_w2 = sb("q_w2", [P, NE * HC * D])
    qT = q_w2[:, 0:KH * NP].rearrange("p (h n) -> p h n", h=KH)
    e_w2 = q_w2[:, :].rearrange("p (c n) -> p c n", c=HC)

    ident = sb("ident", [P, P]); before = sb("before", [P, P]); ones = sb("ones", [P, P])
    heads = sb("heads", [P, P]); iota_w = sb("iota_w", [P, WIDE]); valid = sb("valid", [P, NT])
    epsln = sb("epsln", [P, 1]); zeros = sb("zeros", [P, D])

    early = e_w1[:, :, :].rearrange("p k n -> p (k n)")
    r_int = early[:, 0:4 * EW].bitcast(I32).rearrange("p (a b e) -> p a b e", a=2, b=2)
    r_f = early[:, 4 * EW:10 * EW].rearrange("p (a b e) -> p a b e", a=3, b=2)
    r_dst = early[:, 10 * EW:12 * EW].rearrange("p (b e) -> p b e", b=2)
    r_stat = sb("r_stat", [P, 2, 2])
    c_loc = sb("c_loc", [P, 2, GROUPS + GI]); c_w = sb("c_w", [P, 2, GROUPS + GI])
    c_dst = sb("c_dst", [P, 2, GROUPS]); c_src = sb("c_src", [P, 2, GROUPS], I32)
    base = sb("base", [1, 2 * P], I32); far = sb("far", [1, 4]); flag = sb("flag", [1, 1], I32)
    onehot = sb("onehot", [P, SLOTS, WIN])
    gath = sb("gath", [P, SLOTS, D]); idx = sb("idx", [P, SLOTS], I32)

    NB = 5
    xs = early[:, 12 * EW:12 * EW + NB * D].rearrange("p (j d) -> p j d", j=NB)
    stats = sb("stats", [P, NT, 6]); mv = sb("mv", [P, NT, 2])
    std = sb("std", [P, NT]); rstd = sb("rstd", [P, NT])
    space = [12 * EW + NB * D]

    def carve(n):
        space[0] += n
        assert space[0] <= KH * NE * HE
        return early[:, space[0] - n:space[0]]

    halves = lambda t: t.rearrange("p (h n) -> p h n", h=KH)
    xTs = halves(carve(D)); kqe = carve(2 * D); k_t = carve(D); v_t = halves(carve(KH * (P + 1)))
    kv_bd = halves(carve(D)); ks_bd = halves(carve(D)); den = carve(D); mT = halves(carve(D)); z1 = carve(D)
    mzT = halves(carve(D)); hT = carve(H1).rearrange("p (h n) -> p h n", n=P); z2 = carve(D)
    ks = sb("ks", [P, KH]); b2sum = sb("b2sum", [P, D])
    st2 = sb("st2", [P, 6]); mv2 = sb("mv2", [P, 2]); sd2 = sb("sd2", [P, 1]); rs2 = sb("rs2", [P, 1])

    ctr = {}
    S = {n: sem(n) for n in (
        "loaded", "edges_loaded", "pads", "consts", "masks", "dve", "edge_rows", "edge_cols", "edge_done",
        "xn_store", "ln_std", "xs_ready", "xs_T", "xT_done", "x_loaded",
        "xTs_ready", "pe_qkv", "kq_min", "kq_exp", "kq_ready", "v_ready", "kv_acc",
        "onehots", "win_ready", "win_added", "idx_ready", "pool_past", "dve_past", "act_past", "pe_past",
        "bd_ready", "nd_ready", "mT_ready", "m_ready", "mv_ready", "sd_ready", "z1_ready", "zT_ready",
        "mzT_ready", "h_ready", "hT_ready", "m2_ready", "mv2_ready", "sd2_ready", "mix_done", "kv_zero", "zeroed")}
    assert XT_TILES % 8 == 0
    gath_done = [sem(f"gath_done{s}") for s in range(SLOTS)]
    dve_steps = Steps(S["dve"])

    def dve_link(eng, ins):
        eng.wait_ge(S["dve"], dve_steps.mark(ins))

    def bc(ap, shape):
        return ap.to_broadcast(shape)

    rows = lambda w: w.rearrange("(c p) n -> p c n", p=P)
    cols = lambda v: v.rearrange("(c p) -> p c", p=P)
    spread = lambda v: v.partition_broadcast(P)

    with nc.Block() as block:
        n_loads = 0

        @block.sync
        def _(sp):
            sp.wait_ge(S["pads"], 6)
            d_rows = [a["dst"][0:GFULL * EW].rearrange("(g e) -> g e", e=EW), a["src"][0:GFULL * EW].rearrange("(g e) -> g e", e=EW),
                      a["edge_weight"][0:GFULL * EW].rearrange("(g e) -> g e", e=EW)]
            tails = [v[GFULL * EW:E].rearrange("(a e) -> a e", a=1) for v in (a["dst"], a["src"], a["edge_weight"])]
            for j in range(3):
                t = r_int[:, j] if j < 2 else r_f[:, 1]
                sp.dma_start(t[:, 0, :], d_rows[j][0:P, :]).then_inc(S["edges_loaded"], 16)
                sp.dma_start(t[0:GB, 1, :], d_rows[j][P:GFULL, :]).then_inc(S["edges_loaded"], 16)
                sp.dma_start(t[GB:GB + 1, 1, 0:GREST], tails[j]).then_inc(S["edges_loaded"], 16)
            for b in range(5):
                lo, hi = b * NB, min((b + 1) * NB, NT - 1)
                sp.dma_start(xres[:, lo:hi, :], a["x"][lo * P:hi * P, :].rearrange("(t p) d -> p t d", p=P)).then_inc(S["x_loaded"], 16)
            sp.dma_start(xres[0:LAST, NT - 1, :], a["x"][(NT - 1) * P:N, :]).then_inc(S["x_loaded"], 16)
            for j in range(XT_TILES // 8):
                sp.dma_start(lists[j * 8 * P:(j + 1) * 8 * P, :].rearrange("(p r) d -> p r d", r=8), zeros[:, :].unsqueeze(1).to_broadcast([P, 8, D])).then_inc(S["zeroed"], 16)
            with sp.Fori(0, NT // NB) as i:
                sp.wait_ge(S["xs_ready"], i * NB + NB)
                for j in range(NB):
                    sp.dma_start(xn_rows[ds(i * (NB * P) + j * P, P), :], xs[:, j, :]).then_inc(S["xn_store"], 16)
            sp.wait_ge(S["xn_store"], 16 * NT)
            sp.wait_ge(S["zeroed"], 16 * (XT_TILES // 8))

        @block.gpsimd
        def _(pool):
            pool.memset(r_int[:, 0, 1, :], N).then_inc(S["pads"], 1)
            pool.memset(r_int[:, 1, 1, :], 0).then_inc(S["pads"], 1)
            pool.memset(r_f[:, 1, 1, :], 0.0).then_inc(S["pads"], 1)
            pool.memset(xres[:, NT - 1, :], 0.0).then_inc(S["pads"], 1)
            pool.memset(epsln[:, :], LN_EPS).then_inc(S["pads"], 1)
            pool.memset(zeros[:, :], 0.0).then_inc(S["pads"], 1)
            pool.memset(ident[:, :], 0.0)
            for m in (before, ones, heads, valid):
                pool.memset(m[:, :], 1.0)
            pool.memset(c_loc[:, :, :], 0.0)
            pool.memset(c_w[:, :, :], 0.0)
            pool.iota(iota_w[:, :], pattern=[[1, WIDE]], base=0, channel_multiplier=0,
                      allow_small_or_imprecise_dtypes=True).then_inc(S["consts"], 1)
            pool.wait_ge(S["consts"], 1)
            pool.affine_select(out=ident[:, :], in_=ident[:, :], compare_op=ALU.not_equal, fill=1.0, base=0,
                               pattern=[[-1, P]], channel_multiplier=1).then_inc(S["masks"], 1)
            pool.affine_select(out=before[:, :], in_=before[:, :], compare_op=ALU.is_gt, fill=0.0, base=0,
                               pattern=[[1, P]], channel_multiplier=-1).then_inc(S["masks"], 1)
            pool.affine_select(out=valid[:, :], in_=valid[:, :], compare_op=ALU.is_gt, fill=0.0, base=N,
                               pattern=[[-P, NT]], channel_multiplier=-1).then_inc(S["masks"], 1)
            hv = heads[:, :].rearrange("p (b c) -> p b c", c=DH)
            pool.affine_select(out=hv, in_=hv, compare_op=ALU.is_ge, fill=0.0, base=0,
                               pattern=[[-DH, P // DH], [0, DH]], channel_multiplier=1).then_inc(S["masks"], 1)
            pool.wait_ge(S["masks"], 4)
            pool.affine_select(out=hv, in_=hv, compare_op=ALU.is_ge, fill=0.0, base=DH - 1,
                               pattern=[[DH, P // DH], [0, DH]], channel_multiplier=-1).then_inc(S["masks"], 1)

        @block.scalar
        def _(act):
            for t, v in ((w_kv[:, :, 0:D], rows(a["L0_mix_Wk"])), (w_kv[:, :, D:2 * D], rows(a["L0_mix_Wv"])), (w_q[:, :, :], rows(a["L0_mix_Wq"])),
                         (w_m[:, :, :], rows(a["L0_mix_Wm"])), (w_1[:, :, :], rows(a["L0_mix_W1"])), (w_2[:, :, :], rows(a["L0_mix_W2"])),
                         (g_w1[:, :, :], rows(a["L0_gnn_w1"])), (g_w2[:, :, :], rows(a["L0_gnn_w2"])), (gate_w[:, :, :], rows(a["L0_ffn_gate_w"])),
                         (g_b1[:, :], cols(a["L0_gnn_b1"])), (m_g1[:, :], cols(a["L0_mix_g1"])), (m_b1[:, :], cols(a["L0_mix_b1"])),
                         (eps1[:, :], spread(a["L0_gnn_eps"])),
                         (row_g2[:, :], spread(a["L0_mix_g2"])), (row_b2[:, :], spread(a["L0_mix_b2"])), (row_gb2[:, :], spread(a["L0_gnn_b2"])),
                         (gate_b[:, :], spread(a["L0_ffn_gate_b"]))):
                act.dma_start(t, v, allow_slow_non_contiguous=True).then_inc(S["loaded"], 16)
            act.wait_ge(S["loaded"], 16 * 17)
            act.wait_ge(S["pads"], 6)
            act.wait_ge(S["ln_std"], 1)
            act.activation(std[:, :], mv[:, :, 1], ACT.Sqrt, bias=epsln[:, 0:1]).then_inc(S["ln_std"], 1)
            with act.Fori(0, NT // NB) as i:
                for j in range(NB):
                    act.wait_ge(S["xs_T"], i * NB + j + 1)
                    act.sem_inc(S["act_past"], 1)
                    act.activation(xT[:, :, ds(i * (NB * P) + j * P, P)], bank[j % 2][:, 0:D].rearrange("p (h n) -> p h n", h=KH), ACT.Copy).then_inc(S["xT_done"], 1)

        @block.vector
        def _(dve):
            dve.memset(aggT[:, :, :], 0.0)
            dve.wait_ge(S["x_loaded"], 96)
            for t in range(NT):
                ins = dve.bn_stats(stats[:, t, :], xres[:, t, :])
            dve_link(dve, ins)
            for t in range(NT):
                ins = dve.bn_aggr(mv[:, t, :], stats[:, t, :])
            ins.then_inc(S["ln_std"], 1)
            dve.wait_ge(S["ln_std"], 2)
            dve_link(dve, dve.reciprocal(rstd[:, :], std[:, :]))
            with dve.Fori(0, NT // NB) as i:
                dve_steps.enter(i, 1)
                for j in range(NB):
                    t = i * NB + j
                    dve.tensor_scalar(xs[:, j, :], xres[:, ds(t, 1), :].rearrange("p a d -> p (a d)"), mv[:, ds(t, 1), 0:1].rearrange("p a d -> p (a d)"),
                                      rstd[:, ds(t, 1)], ALU.subtract, ALU.mult).then_inc(S["xs_ready"], 1)
                dve.wait_ge(S["xs_ready"], i * NB + NB)
                for j in range(NB):
                    t = i * NB + j
                    v = xres[:, ds(t, 1), :].rearrange("p a d -> p (a d)")
                    ins = dve.tensor_tensor(v, v, xs[:, j, :], ALU.add)
                dve_link(dve, ins)
                dve.wait_ge(S["xn_store"], (i + 1) * (NB * 16))
                dve.wait_ge(S["xs_T"], (i + 1) * NB)
            dve_steps.leave(NT // NB)
            dve.wait_ge(S["edges_loaded"], 144)
            dve_link(dve, dve.tensor_copy(r_dst[:, :, :], r_int[:, 0, :, :]))
            dve.tensor_copy(r_f[:, 2, :, :], r_int[:, 1, :, :])
            dve_link(dve, dve.tensor_reduce(r_stat[:, 0, :], r_dst[:, :, :], AX.X, ALU.min))
            for b in range(2):
                ins = dve.tensor_scalar(r_f[:, 0, b, :], r_dst[:, b, :], r_stat[:, 0, b:b + 1], None, ALU.subtract)
            dve_link(dve, ins)
            dve_link(dve, dve.scalar_tensor_tensor(out=xs[:, 0:2, :], in0=r_dst[:, :, :], scalar=float(N), in1=r_f[:, 0, :, :],
                                                   op0=ALU.is_lt, op1=ALU.mult))
            dve.tensor_reduce(r_stat[:, 1, :], xs[:, 0:2, :], AX.X, ALU.max).then_inc(S["edge_rows"], 1)
            for n, dst in enumerate((c_loc, c_w, c_src, c_dst)):
                dve.wait_ge(S["edge_cols"], n + 1)
                ps = bank[2 + n][:, :].rearrange("p (h g) -> p h g", h=2)
                dve.tensor_copy(dst[:, :, 0:GROUPS], ps[:, :, 0:GROUPS]).then_inc(S["edge_done"], 1)
            dve.wait_ge(S["edge_cols"], 5)
            dve.tensor_copy(base[:, :], bank[6][0:1, 0:2 * P]).then_inc(S["edge_done"], 1)
            dve_link(dve, dve.tensor_reduce(far[:, 0:1], bank[6][0:1, 2 * P:4 * P], AX.X, ALU.max))
            dve.tensor_scalar(flag[:, :], far[:, 0:1], float(WIN), None, ALU.is_ge).then_inc(S["edge_done"], 1)

        @block.tensor
        def _(pe):
            pe.wait_ge(S["masks"], 1)
            with pe.Fori(0, NT // NB) as i:
                for j in range(NB):
                    pe.wait_ge(S["xs_ready"], i * NB + j + 1)
                    if j >= 2:
                        pe.wait_ge(S["xT_done"], i * NB + j - 1)
                    for h in range(KH):
                        ins = pe.transpose(bank[j % 2][:, h * P:(h + 1) * P], xs[:, j, h * P:(h + 1) * P], ident[:, :])
                    ins.then_inc(S["xs_T"], 1)
                pe.wait_ge(S["xT_done"], (i + 1) * NB)
                pe.sem_inc(S["pe_past"], 1)
            pe.wait_ge(S["edge_rows"], 1)
            for n in range(4):
                for h in range(2):
                    for b in range(2):
                        t = r_f[:, n, b, h * P:(h + 1) * P] if n < 3 else r_dst[:, b, h * P:(h + 1) * P]
                        ins = pe.transpose(bank[2 + n][:, h * 256 + b * P:h * 256 + (b + 1) * P], t, ident[:, :])
                ins.then_inc(S["edge_cols"], 1)
            for s in range(2):
                for b in range(2):
                    ins = pe.matmul(bank[6][0:1, s * 256 + b * P:s * 256 + (b + 1) * P], r_stat[:, s, b:b + 1], ident[:, :], start=True, stop=True)
            ins.then_inc(S["edge_cols"], 1)


    ps_k, ps_v, ps_q, ps_sum = bank[0], bank[5], bank[1], bank[2]
    ps_win = [bank[3], bank[4]]
    ps_nd, ps_tok, ps_hid, ps_zT = bank[0], bank[1], bank[5], bank[6]

    with nc.Block() as block:

        @block.gpsimd
        def _(pool):
            pool.wait_ge(S["edge_done"], 3)
            with pool.Fori(0, 2 * NT) as i:
                for half in range(2):
                    pool.wait_ge(S["win_ready"], i * GI + (2 * half + 2))
                    pool.sem_inc(S["pool_past"], 1)
                    pool.tensor_copy(idx[:, 4 * half:4 * half + 4].rearrange("p (g h) -> p h g", h=2),
                                     c_src[:, :, ds(i * GI + 2 * half, 2)]).then_inc(S["idx_ready"], 1)
                    pool.wait_ge(S["idx_ready"], i * 2 + (half + 1))
                    pool.sem_inc(S["pool_past"], 1)
                    for s in range(4 * half, 4 * half + 4):
                        pool.indirect_dma_start(out=gath[:, s, :], out_offset=None, in_=xn_rows[:, :],
                                                in_offset=bass.IndirectOffsetOnAxis(ap=idx[:, s:s + 1], axis=0)).then_inc(gath_done[s], 16)

        @block.tensor
        def _(pe):
            def group(i, g):
                pe.wait_ge(S["win_added"], i * GI + (g + 1))
                for h in range(2):
                    s = 2 * g + h
                    pe.wait_ge(gath_done[s], i * 16 + 16)
                    pe.wait_ge(S["onehots"], i * SLOTS + (s + 1))
                    for m in range(KH):
                        ins = pe.matmul(ps_win[g % 2][:, m * WIN:(m + 1) * WIN], gath[:, s, m * P:(m + 1) * P], onehot[:, s, :],
                                        start=(h == 0 and m == 0), stop=(h == 1), skip_group_check=True)
                ins.then_inc(S["win_ready"], 1)

            pe.sem_inc(S["win_ready"], GI)
            pe.wait_ge(S["kv_zero"], 1)
            pe.matmul(ps_sum[:, 0:KH * (P + 1)], ident[:, :], kqe[:, 0:KH * (P + 1)], start=True, stop=True, skip_group_check=True).then_inc(S["kv_acc"], 1)
            with pe.Fori(0, NT) as i:
                pe.wait_ge(S["xTs_ready"], i + 1)
                pe.wait_ge(S["kq_ready"], i + 1)
                pe.wait_ge(S["v_ready"], i + 1)
                for dst, w in ((ps_k, w_kv[:, :, 0:D]), (ps_v, w_kv[:, :, D:2 * D])):
                    for k in range(KH):
                        pe.matmul(dst[:, 0:D], xTs[:, k, :], w[:, k, :], start=(k == 0), stop=(k == KH - 1))
                for m in range(KH):
                    for k in range(KH):
                        ins = pe.matmul(ps_q[:, m * P:(m + 1) * P], w_q[:, k, m * P:(m + 1) * P], xTs[:, k, :], start=(k == 0), stop=(k == KH - 1))
                ins.then_inc(S["pe_qkv"], 1)
                group(i, 0)
                group(i, 1)
                pe.wait_ge(S["kq_ready"], i + 2)
                pe.wait_ge(S["v_ready"], i + 2)
                for m in range(KH):
                    ins = pe.matmul(ps_sum[:, m * (P + 1):(m + 1) * (P + 1)], k_t[:, m * P:(m + 1) * P], v_t[:, m, :],
                                    start=False, stop=True, skip_group_check=True)
                ins.then_inc(S["kv_acc"], 1)
                group(i, 2)
                group(i, 3)
            pe.wait_ge(S["bd_ready"], 1)
            with pe.Fori(NT, 2 * NT) as i:
                t = i - NT
                tile = ds(t * P, P)
                for m in range(KH):
                    pe.matmul(ps_nd[:, m * P:(m + 1) * P], kv_bd[:, m, :], qT[:, m, tile], start=True, stop=True)
                for m in range(KH):
                    ins = pe.matmul(ps_nd[:, D + m * P:D + (m + 1) * P], ks_bd[:, m, :], qT[:, m, tile], start=True, stop=True)
                ins.then_inc(S["nd_ready"], 1)
                group(i, 0)
                pe.wait_ge(S["mT_ready"], t + 1)
                for k in range(KH):
                    ins = pe.matmul(ps_tok[:, 0:D], mT[:, k, :], w_m[:, k, :], start=(k == 0), stop=(k == KH - 1))
                ins.then_inc(S["m_ready"], 1)
                group(i, 1)
                pe.wait_ge(S["z1_ready"], t + 1)
                for m in range(KH):
                    ins = pe.transpose(ps_zT[:, m * P:(m + 1) * P], z1[:, m * P:(m + 1) * P], ident[:, :])
                ins.then_inc(S["zT_ready"], 1)
                group(i, 2)
                pe.wait_ge(S["mzT_ready"], t + 1)
                for o in range(H1 // P):
                    for k in range(2 * KH):
                        rhs = xT[:, k, tile] if k < KH else mzT[:, k - KH, :]
                        ins = pe.matmul(ps_hid[:, o * P:(o + 1) * P], w_1[:, k, o * P:(o + 1) * P], rhs, start=(k == 0), stop=(k == 2 * KH - 1))
                ins.then_inc(S["h_ready"], 1)
                group(i, 3)
                pe.wait_ge(S["hT_ready"], t + 1)
                for k in range(H1 // P):
                    ins = pe.matmul(ps_tok[:, 0:D], hT[:, k, :], w_2[:, k, :], start=(k == 0), stop=(k == H1 // P - 1))
                ins.then_inc(S["m2_ready"], 1)

        @block.vector
        def _(dve):
            def build(s, g):
                dve.tensor_scalar(onehot[:, s, :], iota_w[:, 0:WIN], c_loc[:, s % 2, ds(g, 1)], c_w[:, s % 2, ds(g, 1)],
                                        ALU.is_equal, ALU.mult).then_inc(S["onehots"], 1)

            def add(i, g, first):
                dve.wait_ge(S["win_ready"], i * GI + (GI + g + 1))
                dve.sem_inc(S["dve_past"], 1)
                v = aggT[:, :, ds(first, WIN)]
                dve.tensor_tensor(v, v, ps_win[g % 2][:, 0:KH * WIN].rearrange("p (h n) -> p h n", h=KH), ALU.add).then_inc(S["win_added"], 1)
                dve.wait_ge(S["win_added"], i * GI + (g + 3))

            def firsts(i):
                return [dve.value_load(base[0:1, ds(i * GI + g, 1)], min_val=0, max_val=N) for g in range(GI)]

            dve.memset(kqe[:, :], 0.0).then_inc(S["kv_zero"], 1)
            dve.sem_inc(S["win_added"], 2)
            dve.sem_inc(S["kq_ready"], 1)
            dve.wait_ge(S["edge_done"], 5)
            for s in range(SLOTS):
                build(s, s // 2)
            with dve.Fori(0, NT) as i:
                dve.wait_ge(S["pe_qkv"], i + 1)
                dve.wait_ge(S["kv_acc"], i + 1)
                dve.tensor_scalar(kqe[:, 0:D], ps_k[:, 0:D], 0.0, None, ALU.min)
                dve.tensor_scalar(kqe[:, D:2 * D], ps_q[:, 0:D], 0.0, None, ALU.min).then_inc(S["kq_min"], 1)
                r = firsts(i)
                add(i, 0, r[0])
                dve.wait_ge(S["kq_exp"], i + 1)
                dve.scalar_tensor_tensor(out=k_t[:, :], in0=ps_k[:, 0:D], scalar=0.0, in1=kqe[:, 0:D], op0=ALU.max, op1=ALU.add)
                ins = dve.scalar_tensor_tensor(out=qT[:, :, ds(i * P, P)], in0=halves(ps_q[:, 0:D]), scalar=0.0, in1=halves(kqe[:, D:2 * D]),
                                               op0=ALU.max, op1=ALU.add)
                ins.then_inc(S["kq_ready"], 1)
                for g in range(1, GI):
                    add(i, g, r[g])
                for s in range(SLOTS):
                    build(s, i * GI + (GI + s // 2))
            dve.wait_ge(S["kv_acc"], NT + 1)
            for m in range(KH):
                dve.tensor_tensor(kv_bd[:, m, :], heads[:, :], ps_sum[:, m * (P + 1):m * (P + 1) + P], ALU.mult)
                ins = dve.tensor_copy(ks[:, m:m + 1], ps_sum[:, m * (P + 1) + P:(m + 1) * (P + 1)])
            dve_link(dve, ins)
            for m in range(KH):
                ins = dve.tensor_scalar(ks_bd[:, m, :], heads[:, :], ks[:, m:m + 1], None, ALU.mult)
            ins.then_inc(S["bd_ready"], 1)
            dve_link(dve, dve.tensor_tensor(b2sum[:, :], row_b2[:, :], row_gb2[:, :], ALU.add))

            def normalise(src, t, dst, ready, deviation, done):
                dve_link(dve, dve.bn_stats(st2[:, :], src))
                dve.sem_inc(S["dve_past"], 1)
                dve.bn_aggr(mv2[:, :], st2[:, :]).then_inc(S[ready], 1)
                dve.wait_ge(S[deviation], t + 1)
                dve_link(dve, dve.reciprocal(rs2[:, :], sd2[:, :]))
                ins = dve.tensor_scalar(dst, src, mv2[:, 0:1], rs2[:, 0:1], ALU.subtract, ALU.mult)
                if done:
                    ins.then_inc(S[done], 1)
                return ins

            with dve.Fori(NT, 2 * NT) as i:
                t = i - NT
                dve_steps.enter(t, 10)
                r = firsts(i)
                dve.wait_ge(S["nd_ready"], t + 1)
                dve_link(dve, dve.tensor_scalar(den[:, :], ps_nd[:, D:2 * D], ATT_EPS, None, ALU.add))
                dve_link(dve, dve.reciprocal(z1[:, :], den[:, :]))
                dve.scalar_tensor_tensor(out=mT[:, :, :], in0=halves(ps_nd[:, 0:D]), scalar=float(N), in1=halves(z1[:, :]),
                                         op0=ALU.mult, op1=ALU.mult).then_inc(S["mT_ready"], 1)
                add(i, 0, r[0])
                dve.wait_ge(S["mT_ready"], t + 1)
                dve.wait_ge(S["m_ready"], t + 1)
                normalise(ps_tok[:, 0:D], t, z1[:, :], "mv_ready", "sd_ready", "z1_ready")
                for g in range(1, GI):
                    add(i, g, r[g])
                for s in range(SLOTS):
                    build(s, i * GI + (GI + s // 2))
                dve.wait_ge(S["m2_ready"], t + 1)
                dve.wait_ge(S["z1_ready"], t + 1)
                dve_link(dve, normalise(ps_tok[:, 0:D], t, z2[:, :], "mv2_ready", "sd2_ready", None))
                dve_link(dve, dve.tensor_tensor(z2[:, :], z2[:, :], row_g2[:, :], ALU.mult))
                dve_link(dve, dve.tensor_tensor(z2[:, :], z2[:, :], b2sum[:, :], ALU.add))
                v = xres[:, ds(t, 1), :].rearrange("p a d -> p (a d)")
                dve_link(dve, dve.tensor_tensor(v, v, z2[:, :], ALU.add))
            dve_steps.leave(NT)

        @block.scalar
        def _(act):
            act.sem_inc(S["v_ready"], 1)
            with act.Fori(0, NT) as i:
                act.wait_ge(S["kq_ready"], i + 1)
                act.sem_inc(S["act_past"], 1)
                act.activation(xTs[:, :, :], xT[:, :, ds(i * P, P)], ACT.Copy).then_inc(S["xTs_ready"], 1)
                act.wait_ge(S["kv_acc"], i + 1)
                act.sem_inc(S["act_past"], 1)
                act.activation(v_t[:, :, P:P + 1], bc(valid[:, ds(i, 1)].unsqueeze(1), [P, KH, 1]), ACT.Copy)
                act.wait_ge(S["kq_min"], i + 1)
                act.activation(kqe[:, :], kqe[:, :], ACT.Exp).then_inc(S["kq_exp"], 1)
                act.activation(v_t[:, :, 0:P], halves(ps_v[:, 0:D]), ACT.Copy, scale=1.0 / N).then_inc(S["v_ready"], 1)
            with act.Fori(NT, 2 * NT) as i:
                t = i - NT
                act.wait_ge(S["mv_ready"], t + 1)
                act.activation(sd2[:, :], mv2[:, 1:2], ACT.Sqrt, bias=epsln[:, 0:1]).then_inc(S["sd_ready"], 1)
                act.wait_ge(S["zT_ready"], t + 1)
                for m in range(KH):
                    ins = act.activation(mzT[:, m, :], ps_zT[:, m * P:(m + 1) * P], ACT.Identity, scale=m_g1[:, m:m + 1], bias=m_b1[:, m:m + 1])
                ins.then_inc(S["mzT_ready"], 1)
                act.wait_ge(S["h_ready"], t + 1)
                act.activation(hT[:, :, :], ps_hid[:, :].rearrange("p (o n) -> p o n", n=P), ACT.Relu).then_inc(S["hT_ready"], 1)
                act.wait_ge(S["mv2_ready"], t + 1)
                act.activation(sd2[:, :], mv2[:, 1:2], ACT.Sqrt, bias=epsln[:, 0:1]).then_inc(S["sd2_ready"], 1)

    for n in ("far_left", "far_free", "far_idx", "far_got", "far_scaled", "far_onehot", "far_sums", "far_added"):
        S[n] = sem(n)
    WIDES = NP // WIDE
    assert NP % WIDE == 0
    far_hot = early[:, 0:WIDE]
    with nc.Block() as block:

        @block.gpsimd
        def _(pool):
            taken = pool.value_load(flag[0:1, 0:1], min_val=0, max_val=1)
            with pool.If(taken == 1):
                with pool.Fori(0, GROUPS) as g:
                    for h in range(2):
                        pool.wait_ge(S["far_free"], g * 2 + (h + 1))
                        pool.sem_inc(S["pool_past"], 1)
                        pool.tensor_copy(idx[:, 0:1], c_src[:, h, ds(g, 1)]).then_inc(S["far_idx"], 1)
                        pool.wait_ge(S["far_idx"], g * 2 + (h + 1))
                        pool.sem_inc(S["pool_past"], 1)
                        pool.indirect_dma_start(out=gath[:, 0, :], out_offset=None, in_=xn_rows[:, :],
                                                in_offset=bass.IndirectOffsetOnAxis(ap=idx[:, 0:1], axis=0)).then_inc(S["far_got"], 16)

        @block.vector
        def _(dve):
            taken = dve.value_load(flag[0:1, 0:1], min_val=0, max_val=1)
            with dve.If(taken == 1):
                v = c_w[:, :, :]
                dve.scalar_tensor_tensor(out=v, in0=c_loc[:, :, :], scalar=float(WIN), in1=v, op0=ALU.is_ge, op1=ALU.mult).then_inc(S["far_left"], 1)
                dve.wait_ge(S["far_left"], 1)
                dve.sem_inc(S["far_free"], 1)
                with dve.Fori(0, GROUPS) as g:
                    for h in range(2):
                        c = g * 2 + h
                        dve.wait_ge(S["far_got"], c * 16 + 16)
                        dve.sem_inc(S["dve_past"], 1)
                        dve.tensor_scalar(gath[:, 0, :], gath[:, 0, :], c_w[:, h, ds(g, 1)], None, ALU.mult).then_inc(S["far_scaled"], 1)
                        for w in range(WIDES):
                            k = c * WIDES + w
                            dve.tensor_scalar(far_hot[:, :], iota_w[:, :], c_dst[:, h, ds(g, 1)], float(-w * WIDE),
                                              ALU.subtract, ALU.is_equal).then_inc(S["far_onehot"], 1)
                            dve.wait_ge(S["far_sums"], k + 1)
                            for m in range(KH):
                                v = aggT[:, m, w * WIDE:(w + 1) * WIDE]
                                ins = dve.tensor_tensor(v, v, bank[m][:, 0:WIDE], ALU.add)
                            ins.then_inc(S["far_added"], 1)
                            dve.wait_ge(S["far_added"], k + 1)
                        dve.sem_inc(S["far_free"], 1)

        @block.tensor
        def _(pe):
            taken = pe.value_load(flag[0:1, 0:1], min_val=0, max_val=1)
            with pe.If(taken == 1):
                with pe.Fori(0, 2 * GROUPS) as c:
                    pe.wait_ge(S["far_scaled"], c + 1)
                    pe.sem_inc(S["pe_past"], 1)
                    for w in range(WIDES):
                        pe.wait_ge(S["far_onehot"], c * WIDES + (w + 1))
                        for m in range(KH):
                            ins = pe.matmul(bank[m][:, 0:WIDE], gath[:, 0, m * P:(m + 1) * P], far_hot[:, :], start=True, stop=True)
                        ins.then_inc(S["far_sums"], 1)

    gflat = gath[:, :, :].rearrange("p s d -> p (s d)")
    NB_TOK = NB * P
    PIECE = NB_TOK // 2
    g1T = gflat[:, 0:KH * NB_TOK].rearrange("p (h n) -> p h n", h=KH)
    xn2 = gflat[:, 0:NB * D].rearrange("p (j d) -> p j d", j=NB)
    xn2T = gflat[:, NB * D:NB * D + 2 * D].rearrange("p (b h n) -> p b h n", b=2, h=KH)
    xf = xT[:, :, :].rearrange("p h n -> p (h n)").rearrange("p (t d) -> p t d", d=D)
    TN = NT * NE
    TT = XT_TILES
    agg_flat = aggT[:, :, :].rearrange("p h n -> p (h n)")
    taken = [0]

    def late(*shape):
        n = 1
        for d in shape:
            n *= d
        taken[0] += n
        v = agg_flat[:, KH * NP - taken[0]:KH * NP - taken[0] + n]
        return v if len(shape) == 1 else v.rearrange("p (a b) -> p a b", b=shape[-1])

    logits, probs, rtmp, chosen = (late(NT, NE) for _ in range(4))
    picks2 = late(2 * NT, NE)
    picks = picks2.rearrange("p (k t) e -> p k t e", k=2)
    run_in, run = late(NE, NT), late(NE, NT)
    past = late(TT, NE - 1)
    rev = sb("rev", [P, NE]); rmax = sb("rmax", [P, NT]); wts = sb("wts", [P, 2, NT]); slots = sb("slots", [P, 2, NT], I32)
    slot_f = sb("slot_f", [P, 2, NT]);
    count = sb("count", [P, NE]); count_i = sb("count_i", [P, NE], I32); ntile = sb("ntile", [P, NE]); until = sb("until", [P, NE])
    shift = sb("shift", [P, NE])
    jt = sb("jt", [P, TT]); t_exp = sb("t_exp", [P, TT])
    ti_exp = sb("ti_exp", [P, TT], I32)
    for n in ("h0_ready", "g1_ready", "g1T_ready", "g2_ready", "g2_done", "experts_loaded", "std2", "n2_ready", "n2_copied", "n2_T", "n2T_ready",
              "logit_ready", "logits_done", "soft", "chosen_ready", "ranks_ready", "slots_ready", "tables_ready", "scattered", "tails", "pool_consts",
              "xg_T", "xgT_ready", "he_ready", "hs_ready", "heT_ready", "gelu_ready", "ye_ready", "y_ready", "y_free", "sp_past", "t_done"):
        S[n] = sem(n)
    xg_loaded = [sem(f"xg_loaded{b}") for b in range(2)]
    y_stored = [sem(f"y_stored{b}") for b in range(2)]

    with nc.Block() as block:

        @block.sync
        def _(sp):
            for k in range(KH):
                sp.dma_start(e_w1[:, k, :].rearrange("p (e n) -> p e n", e=NE), a["L0_ffn_W1"][:, k * P:(k + 1) * P, :].rearrange("e p n -> p e n")).then_inc(S["experts_loaded"], 16)
            for c in range(HC):
                sp.dma_start(e_w2[:, c, :].rearrange("p (e n) -> p e n", e=NE), a["L0_ffn_W2"][:, c * P:(c + 1) * P, :].rearrange("e p n -> p e n")).then_inc(S["experts_loaded"], 16)
            sp.dma_start(e_b1[:, :], a["L0_ffn_b1"].rearrange("e (c p) -> p (e c)", p=P), allow_slow_non_contiguous=True).then_inc(S["experts_loaded"], 16)
            sp.dma_start(e_b2[:, :], a["L0_ffn_b2"].rearrange("e n -> (e n)").partition_broadcast(P)).then_inc(S["experts_loaded"], 16)
            sp.wait_ge(S["experts_loaded"], 16 * (KH + HC + 2))

        @block.vector
        def _(dve):
            dve_link(dve, dve.tensor_scalar(eps1[:, :], eps1[:, :], 1.0, None, ALU.add))
            for i in range(NT // NB):
                v = aggT[:, :, i * NB_TOK:(i + 1) * NB_TOK]
                dve.scalar_tensor_tensor(out=v, in0=xT[:, :, i * NB_TOK:(i + 1) * NB_TOK], scalar=eps1[:, 0:1], in1=v,
                                         op0=ALU.mult, op1=ALU.add).then_inc(S["h0_ready"], 1)
            with dve.Fori(0, NT // NB) as i:
                dve_steps.enter(i, 2 * NB)
                for j in range(NB):
                    t = i * NB + j
                    v = xres[:, ds(t, 1), :].rearrange("p a d -> p (a d)")
                    dve.wait_ge(S["g2_ready"], i * NB + (j + 1))
                    dve_link(dve, dve.tensor_tensor(v, v, bank[4 + j % 4][:, 0:D], ALU.add))
                    dve.sem_inc(S["g2_done"], 1)
                    dve_link(dve, dve.bn_stats(stats[:, ds(t, 1), :].rearrange("p a d -> p (a d)"), v))
            dve_steps.leave(NT // NB)
            for t in range(NT):
                ins = dve.bn_aggr(mv[:, t, :], stats[:, t, :])
            ins.then_inc(S["std2"], 1)
            dve.wait_ge(S["std2"], 2)
            dve_link(dve, dve.reciprocal(rstd[:, :], std[:, :]))
            with dve.Fori(0, NT // NB) as i:
                for j in range(NB):
                    t = i * NB + j
                    dve.tensor_scalar(xn2[:, j, :], xres[:, ds(t, 1), :].rearrange("p a d -> p (a d)"), mv[:, ds(t, 1), 0:1].rearrange("p a d -> p (a d)"),
                                      rstd[:, ds(t, 1)], ALU.subtract, ALU.mult).then_inc(S["n2_ready"], 1)
                for j in range(NB):
                    t = i * NB + j
                    dve.wait_ge(S["logit_ready"], i * NB + (j + 1))
                    dve.tensor_tensor(logits[:, ds(t, 1), :].rearrange("p a e -> p (a e)"), bank[2 + j % 2][:, 0:NE], gate_b[:, :], ALU.add).then_inc(S["logits_done"], 1)
                dve.wait_ge(S["n2_copied"], (i + 1) * NB)

        @block.tensor
        def _(pe):
            with pe.Fori(0, NT // NB) as i:
                pe.wait_ge(S["h0_ready"], i + 1)
                for n in range(2):
                    for m in range(KH):
                        for k in range(KH):
                            ins = pe.matmul(bank[2 * n + m][:, 0:PIECE], g_w1[:, k, m * P:(m + 1) * P], aggT[:, k, ds(i * NB_TOK + n * PIECE, PIECE)],
                                            start=(k == 0), stop=(k == KH - 1))
                        ins.then_inc(S["g1_ready"], 1)
                for j in range(NB):
                    pe.wait_ge(S["g1T_ready"], i * 4 + (2 if (j + 1) * P <= PIECE else 4))
                    if j >= 4:
                        pe.wait_ge(S["g2_done"], i * NB + (j - 3))
                    for k in range(KH):
                        ins = pe.matmul(bank[4 + j % 4][:, 0:D], g1T[:, k, j * P:(j + 1) * P], g_w2[:, k, :], start=(k == 0), stop=(k == KH - 1))
                    ins.then_inc(S["g2_ready"], 1)
                pe.wait_ge(S["g2_done"], (i + 1) * NB)
                pe.sem_inc(S["pe_past"], 1)
            with pe.Fori(0, NT // NB) as i:
                for j in range(NB):
                    pe.wait_ge(S["n2_ready"], i * NB + (j + 1))
                    for h in range(KH):
                        ins = pe.transpose(bank[j % 2][:, h * P:(h + 1) * P], xn2[:, j, h * P:(h + 1) * P], ident[:, :])
                    ins.then_inc(S["n2_T"], 1)
                    pe.wait_ge(S["n2T_ready"], i * NB + (j + 1))
                    if j >= 2:
                        pe.wait_ge(S["logits_done"], i * NB + (j - 1))
                    for k in range(KH):
                        ins = pe.matmul(bank[2 + j % 2][:, 0:NE], xn2T[:, j % 2, k, :], gate_w[:, k, :], start=(k == 0), stop=(k == KH - 1))
                    ins.then_inc(S["logit_ready"], 1)
                pe.wait_ge(S["logits_done"], (i + 1) * NB)
                pe.sem_inc(S["pe_past"], 1)

        @block.scalar
        def _(act):
            with act.Fori(0, NT // NB) as i:
                for n in range(2):
                    for m in range(KH):
                        act.wait_ge(S["g1_ready"], i * 4 + (2 * n + m + 1))
                        act.activation(g1T[:, m, n * PIECE:(n + 1) * PIECE], bank[2 * n + m][:, 0:PIECE], ACT.Relu, bias=g_b1[:, m:m + 1]).then_inc(S["g1T_ready"], 1)
            act.wait_ge(S["std2"], 1)
            act.activation(std[:, :], mv[:, :, 1], ACT.Sqrt, bias=epsln[:, 0:1]).then_inc(S["std2"], 1)
            with act.Fori(0, NT // NB) as i:
                for j in range(NB):
                    act.wait_ge(S["n2_T"], i * NB + (j + 1))
                    act.activation(xn2T[:, j % 2, :, :], halves(bank[j % 2][:, 0:D]), ACT.Copy).then_inc(S["n2T_ready"], 1)

        @block.gpsimd
        def _(pool):
            pool.iota(rev[:, :], pattern=[[-1, NE]], base=NE, channel_multiplier=0, allow_small_or_imprecise_dtypes=True).then_inc(S["pool_consts"], 1)
            pool.iota(jt[:, :], pattern=[[1, TT]], base=0, channel_multiplier=0, allow_small_or_imprecise_dtypes=True).then_inc(S["pool_consts"], 1)
            with pool.Fori(0, NT // NB) as i:
                for j in range(NB):
                    pool.wait_ge(S["n2_ready"], i * NB + (j + 1))
                    pool.sem_inc(S["pool_past"], 1)
                    pool.tensor_copy(xf[:, ds(i * NB + j, 1), :].rearrange("p a d -> p (a d)"), xn2[:, j, :]).then_inc(S["n2_copied"], 1)

    per_e = lambda v, n=NT: v.unsqueeze(2).to_broadcast([P, n, NE])
    per_t = lambda v, n=NT: v.unsqueeze(1).to_broadcast([P, n, NE])
    by_e = lambda v: v.rearrange("p (t e) -> p t e", e=NE)

    with nc.Block() as block:

        @block.vector
        def _(dve):
            L = lambda ins: dve_link(dve, ins)
            tt, red = dve.tensor_tensor, dve.tensor_reduce
            L(red(rmax[:, :], logits[:, :, :], AX.X, ALU.max))
            tt(rtmp[:, :, :], logits[:, :, :], per_e(rmax[:, :]), ALU.subtract).then_inc(S["soft"], 1)
            dve.wait_ge(S["soft"], 2)
            L(red(rmax[:, :], probs[:, :, :], AX.X, ALU.add))
            L(dve.reciprocal(rmax[:, :], rmax[:, :]))
            L(tt(probs[:, :, :], probs[:, :, :], per_e(rmax[:, :]), ALU.mult))
            for k in range(2):
                L(red(wts[:, k, :], probs[:, :, :], AX.X, ALU.max))
                L(tt(rtmp[:, :, :], probs[:, :, :], per_e(wts[:, k, :]), ALU.is_equal))
                L(tt(rtmp[:, :, :], rtmp[:, :, :], per_t(rev[:, :]), ALU.mult))
                L(red(rmax[:, :], rtmp[:, :, :], AX.X, ALU.max))
                L(tt(picks[:, k, :, :], per_t(rev[:, :]), per_e(rmax[:, :]), ALU.is_equal))
                if k == 0:
                    L(dve.scalar_tensor_tensor(out=probs[:, :, :], in0=picks[:, 0, :, :], scalar=-2.0, in1=probs[:, :, :], op0=ALU.mult, op1=ALU.add))
            L(tt(chosen[:, :, :], picks[:, 0, :, :], picks[:, 1, :, :], ALU.add))
            tt(chosen[:, :, :], chosen[:, :, :], per_e(valid[:, :]), ALU.mult).then_inc(S["chosen_ready"], 1)
            dve.wait_ge(S["ranks_ready"], 1)
            L(dve.tensor_copy(run_in[:, :, :].rearrange("p e t -> p t e"), by_e(bank[1][:, 0:TN])))
            flat = lambda v: v[:, :, :].rearrange("p e t -> p (e t)")
            L(dve.tensor_tensor_scan(flat(run), flat(run_in), flat(run_in), 0.0, ALU.add, ALU.bypass))
            L(dve.tensor_copy(count[:, 0:1], run[:, 0, NT - 1:NT]))
            L(tt(count[:, 1:NE], run[:, 1:NE, NT - 1], run[:, 0:NE - 1, NT - 1], ALU.subtract))
            L(tt(run_in[:, :, :], run[:, :, :], run_in[:, :, :], ALU.subtract))
            L(tt(shift[:, :], run[:, :, NT - 1], count[:, :], ALU.subtract))
            L(dve.tensor_scalar(count[:, :], count[:, :], float(P - 1), None, ALU.add))
            L(dve.tensor_copy(count_i[:, :], count[:, :]))
            L(dve.tensor_scalar(count_i[:, :], count_i[:, :], 7, None, ALU.logical_shift_right))
            L(dve.tensor_copy(ntile[:, :], count_i[:, :]))
            L(dve.tensor_tensor_scan(until[:, :], ntile[:, :], ntile[:, :], 0.0, ALU.add, ALU.bypass))
            L(tt(ntile[:, :], until[:, :], ntile[:, :], ALU.subtract))
            L(dve.scalar_tensor_tensor(out=shift[:, :], in0=ntile[:, :], scalar=float(P), in1=shift[:, :], op0=ALU.mult, op1=ALU.subtract))
            L(tt(rtmp[:, :, :], by_e(bank[0][:, 0:TN]), run_in[:, :, :].rearrange("p e t -> p t e"), ALU.add))
            L(tt(rtmp[:, :, :], rtmp[:, :, :], per_t(shift[:, :]), ALU.add))
            for k in range(2):
                L(tt(probs[:, :, :], picks[:, k, :, :], rtmp[:, :, :], ALU.mult))
                L(red(slot_f[:, k, :], probs[:, :, :], AX.X, ALU.add))
            dve.tensor_copy(slots[:, :, :], slot_f[:, :, :]).then_inc(S["slots_ready"], 1)
            L(tt(past[:, :, :], jt[:, :].unsqueeze(2).to_broadcast([P, TT, NE - 1]), until[:, 0:NE - 1].unsqueeze(1).to_broadcast([P, TT, NE - 1]), ALU.is_ge))
            L(red(t_exp[:, :], past[:, :, :], AX.X, ALU.add))
            dve.tensor_copy(ti_exp[:, :], t_exp[:, :]).then_inc(S["slots_ready"], 1)

        @block.scalar
        def _(act):
            act.wait_ge(S["soft"], 1)
            act.activation(probs[:, :, :], rtmp[:, :, :], ACT.Exp).then_inc(S["soft"], 1)

        @block.tensor
        def _(pe):
            pe.wait_ge(S["chosen_ready"], 1)
            c = chosen[:, :, :].rearrange("p t e -> p (t e)")
            pe.matmul(bank[0][:, 0:TN], before[:, :], c, start=True, stop=True)
            pe.matmul(bank[1][:, 0:TN], ones[:, :], c, start=True, stop=True).then_inc(S["ranks_ready"], 1)

        @block.gpsimd
        def _(pool):
            pool.wait_ge(S["slots_ready"], 1)
            for t in range(NT):
                n = P if t < NT - 1 else LAST
                for k in range(2):
                    pool.indirect_dma_start(out=lists[:, :], out_offset=bass.IndirectOffsetOnAxis(ap=slots[0:n, k, t:t + 1], axis=0),
                                            in_=xf[0:n, t, :], in_offset=None).then_inc(S["scattered"], 16)
            pool.wait_ge(S["scattered"], 16 * 2 * NT)

    work = aggT[:, :, :].rearrange("p h n -> p (h n)")
    cut = [0]

    def piece(n):
        cut[0] += 2 * n
        return work[:, cut[0] - 2 * n:cut[0]].rearrange("p (b n) -> p b n", b=2)

    xg, xgT, hs, heT, ye = piece(D), piece(D), piece(HE), piece(HE), piece(D)

    with nc.Block() as block:

        @block.sync
        def _(sp):
            for b in range(2):
                sp.dma_start(xg[:, b, :], lists[b * P:(b + 1) * P, :]).then_inc(xg_loaded[b], 16)

            def store(i):
                for b in range(2):
                    sp.wait_ge(S["y_ready"], i * 2 + (b + 1))
                    sp.sem_inc(S["sp_past"], 1)
                    sp.dma_start(results[ds(i * (2 * P) + b * P, P), :], ye[:, b, :]).then_inc(y_stored[b], 16)

            with sp.Fori(0, XT_TILES // 2 - 1) as i:
                for b in range(2):
                    sp.wait_ge(S["xg_T"], i * 2 + (b + 1))
                    sp.sem_inc(S["sp_past"], 1)
                    sp.dma_start(xg[:, b, :], lists[ds(i * (2 * P) + (2 + b) * P, P), :]).then_inc(xg_loaded[b], 16)
                store(i)
                for b in range(2):
                    sp.wait_ge(y_stored[b], i * 16 + 16)
                    sp.sem_inc(S["y_free"], 1)
            for b in range(2):
                sp.wait_ge(S["y_ready"], XT_TILES - 1 + b)
                sp.dma_start(results[(XT_TILES - 2 + b) * P:(XT_TILES - 1 + b) * P, :], ye[:, b, :]).then_inc(y_stored[b], 16)
            for b in range(2):
                sp.wait_ge(y_stored[b], 16 * (XT_TILES // 2))

        @block.tensor
        def _(pe):
            with pe.Fori(0, XT_TILES // 2) as i:
                e = [pe.value_load(ti_exp[0:1, ds(i * 2 + b, 1)], min_val=0, max_val=NE - 1) for b in range(2)]
                for b in range(2):
                    pe.wait_ge(xg_loaded[b], i * 16 + 16)
                    for h in range(KH):
                        ins = pe.transpose(bank[b][:, h * P:(h + 1) * P], xg[:, b, h * P:(h + 1) * P], ident[:, :])
                    ins.then_inc(S["xg_T"], 1)
                for b in range(2):
                    pe.wait_ge(S["xgT_ready"], i * 2 + (b + 1))
                    for k in range(KH):
                        ins = pe.matmul(bank[2 + b][:, 0:HE], xgT[:, b, k * P:(k + 1) * P], e_w1[:, k, ds(e[b] * HE, HE)], start=(k == 0), stop=(k == KH - 1))
                    ins.then_inc(S["he_ready"], 1)
                for b in range(2):
                    pe.wait_ge(S["hs_ready"], i * 2 + (b + 1))
                    for c in range(HC):
                        ins = pe.transpose(bank[4 + b][:, c * P:(c + 1) * P], hs[:, b, c * P:(c + 1) * P], ident[:, :])
                    ins.then_inc(S["heT_ready"], 1)
                for b in range(2):
                    pe.wait_ge(S["gelu_ready"], i * 2 + (b + 1))
                    for c in range(HC):
                        ins = pe.matmul(bank[6 + b][:, 0:D], heT[:, b, c * P:(c + 1) * P], e_w2[:, c, ds(e[b] * D, D)], start=(c == 0), stop=(c == HC - 1))
                    ins.then_inc(S["ye_ready"], 1)

        @block.scalar
        def _(act):
            with act.Fori(0, XT_TILES // 2) as i:
                e = [act.value_load(ti_exp[0:1, ds(i * 2 + b, 1)], min_val=0, max_val=NE - 1) for b in range(2)]
                for b in range(2):
                    act.wait_ge(S["xg_T"], i * 2 + (b + 1))
                    act.activation(xgT[:, b, :], bank[b][:, 0:D], ACT.Copy).then_inc(S["xgT_ready"], 1)
                for b in range(2):
                    act.wait_ge(S["heT_ready"], i * 2 + (b + 1))
                    act.sem_inc(S["act_past"], 1)
                    for c in range(HC):
                        ins = act.activation(heT[:, b, c * P:(c + 1) * P], bank[4 + b][:, c * P:(c + 1) * P], ACT.Gelu, bias=e_b1[:, ds(e[b] * HC + c, 1)])
                    ins.then_inc(S["gelu_ready"], 1)

        @block.vector
        def _(dve):
            dve.sem_inc(S["y_free"], 2)
            with dve.Fori(0, XT_TILES // 2) as i:
                e = [dve.value_load(ti_exp[0:1, ds(i * 2 + b, 1)], min_val=0, max_val=NE - 1) for b in range(2)]
                for b in range(2):
                    dve.wait_ge(S["he_ready"], i * 2 + (b + 1))
                    dve.tensor_copy(hs[:, b, :], bank[2 + b][:, 0:HE]).then_inc(S["hs_ready"], 1)
                for b in range(2):
                    dve.wait_ge(S["y_free"], i * 2 + (b + 1))
                    dve.wait_ge(S["ye_ready"], i * 2 + (b + 1))
                    dve.tensor_tensor(ye[:, b, :], bank[6 + b][:, 0:D], e_b2[:, ds(e[b] * D, D)], ALU.add).then_inc(S["y_ready"], 1)

    NC = 6
    cflat = work[:, 0:3 * NC * D].rearrange("p (k j d) -> p k j d", k=3, j=NC)
    y_in, o_t = cflat[:, 0:2], cflat[:, 2]
    cidx = sb("cidx", [P, 2, NC], I32)
    for n in ("cidx_ready", "o_ready", "o_stored", "comb"):
        S[n] = sem(n)
    y_got = [sem(f"y_got{j}") for j in range(NC)]
    assert (NT - 1) % NC == 0

    with nc.Block() as block:

        @block.gpsimd
        def _(pool):
            pool.sem_inc(S["comb"], NC)
            with pool.Fori(0, (NT - 1) // NC) as i:
                pool.wait_ge(S["comb"], (i + 1) * NC)
                pool.sem_inc(S["pool_past"], 1)
                pool.tensor_copy(cidx[:, :, :], slots[:, :, ds(i * NC, NC)]).then_inc(S["cidx_ready"], 1)
                pool.wait_ge(S["cidx_ready"], i + 1)
                pool.sem_inc(S["pool_past"], 1)
                for j in range(NC):
                    for k in range(2):
                        pool.indirect_dma_start(out=y_in[:, k, j, :], out_offset=None, in_=results[:, :],
                                                in_offset=bass.IndirectOffsetOnAxis(ap=cidx[:, k, j:j + 1], axis=0)).then_inc(y_got[j], 16)
            pool.wait_ge(S["comb"], NT - 1 + NC)
            for k in range(2):
                pool.indirect_dma_start(out=y_in[0:LAST, k, 0, :], out_offset=None, in_=results[:, :],
                                        in_offset=bass.IndirectOffsetOnAxis(ap=slots[0:LAST, k, NT - 1:NT], axis=0)).then_inc(y_got[0], 16)

        @block.vector
        def _(dve):
            def combine(n, j, res, w, out_):
                dve_link(dve, dve.scalar_tensor_tensor(out=y_in[0:n, 0, j, :], in0=y_in[0:n, 0, j, :], scalar=w[0], in1=res, op0=ALU.mult, op1=ALU.add))
                dve.scalar_tensor_tensor(out=out_, in0=y_in[0:n, 1, j, :], scalar=w[1], in1=y_in[0:n, 0, j, :], op0=ALU.mult, op1=ALU.add).then_inc(S["o_ready"], 1)

            with dve.Fori(0, (NT - 1) // NC) as i:
                dve_steps.enter(i, NC)
                for j in range(NC):
                    t = i * NC + j
                    dve.wait_ge(y_got[j], i * 32 + 32)
                    combine(P, j, xres[:, ds(t, 1), :].rearrange("p a d -> p (a d)"), [wts[:, k, ds(t, 1)] for k in range(2)], o_t[:, j, :])
                    dve.wait_ge(S["o_ready"], i * NC + (j + 1))
                    dve.sem_inc(S["comb"], 1)
                dve.wait_ge(S["o_stored"], (i + 1) * (16 * NC))
            dve_steps.leave((NT - 1) // NC)
            dve.wait_ge(y_got[0], 32 * ((NT - 1) // NC + 1))
            combine(LAST, 0, xres[0:LAST, NT - 1, :], [wts[0:LAST, k, NT - 1:NT] for k in range(2)], o_t[0:LAST, 0, :])

        @block.sync
        def _(sp):
            with sp.Fori(0, (NT - 1) // NC) as i:
                for j in range(NC):
                    sp.wait_ge(S["o_ready"], i * NC + (j + 1))
                    sp.sem_inc(S["sp_past"], 1)
                    sp.dma_start(out[ds(i * (NC * P) + j * P, P), :], o_t[:, j, :]).then_inc(S["o_stored"], 16)
            sp.wait_ge(S["o_ready"], NT)
            sp.dma_start(out[(NT - 1) * P:N, :], o_t[0:LAST, 0, :]).then_inc(S["o_stored"], 16)
            sp.wait_ge(S["o_stored"], 16 * NT)

    ctx.close()


_OUTS = [((3125, 256), "float32")]


def kernel(**inputs):
    import numpy as _np
    import concourse.bacc as _bacc
    from concourse.bass_utils import run_bass_kernel_spmd as _run

    nc = _bacc.Bacc("TRN2", target_bir_lowering=False, num_devices=1)
    arrays, args = {}, {}
    for name, value in inputs.items():
        v = _np.ascontiguousarray(value)
        arrays[f"in_{name}"] = v
        args[name] = nc.dram_tensor(f"in_{name}", v.shape, mybir.dt.from_np(v.dtype), kind="ExternalInput").ap()
    shape, dtype = _OUTS[0]
    out = nc.dram_tensor("out_0", shape, mybir.dt.from_np(_np.dtype(dtype)), kind="ExternalOutput").ap()
    graph_layer(nc, args, out)
    r = _run(nc, [arrays], core_ids=[0])
    return r.results[0]["out_0"]
```

```python
from contextlib import ExitStack

import concourse.bass as bass
from concourse import mybir

F32 = mybir.dt.float32
I32 = mybir.dt.int32
ALU = mybir.AluOpType
ACT = mybir.ActivationFunctionType
AX = mybir.AxisListType

P = 128
WIN = 64
WIDE = 400
LN_EPS = 1e-5
ATT_EPS = 1e-6


class Steps:

    def __init__(self, sem):
        self.sem, self.before, self.here, self.loop = sem, 0, 0, 0

    def enter(self, i, per):
        self.before, self.here, self.loop, self.per = self.before + self.here, 0, i * per, per

    def leave(self, n):
        assert self.here == self.per, (self.here, self.per)
        self.before, self.here, self.loop = self.before + n * self.per, 0, 0

    def mark(self, ins):
        ins.then_inc(self.sem, 1)
        self.here += 1
        return self.loop + (self.before + self.here)


def graph_layer(nc, a, out):
    N, D = a["x"].shape
    E = a["src"].shape[0]
    NT = -(-N // P)
    NP = NT * P
    LAST = N - (NT - 1) * P
    KH = D // P
    EW = 2 * P
    GA, GM = 2, 6
    GROUPS = NT * (GA + GM)
    NB = 5
    SLOTS = 2 * NB * GA
    GFULL, GREST = E // EW, E % EW
    GB = GFULL - P
    assert KH == 2 and E <= GROUPS * EW and 0 < GB < P and GROUPS <= 2 * P
    H1 = a["L0_mix_W1"].shape[1]
    NE, _, HE = a["L0_ffn_W1"].shape
    HC = HE // P
    HEADS = 8
    DH = D // HEADS
    PAIRS = 2 * N
    XT_TILES = (PAIRS + NE * (P - 1)) // P
    XT_TILES += XT_TILES % 2

    ctx = ExitStack()
    sb = lambda n, s, d=F32: ctx.enter_context(nc.sbuf_tensor(n, s, d))
    sem = lambda n: ctx.enter_context(nc.semaphore(n))
    bank = [ctx.enter_context(nc.psum_tensor(f"bank{i}", [P, 512], F32)) for i in range(8)]
    ds = bass.ds

    xn_rows = nc.dram_tensor("xn_rows", [NP, D], F32, kind="Internal").ap()
    lists = nc.dram_tensor("expert_lists", [XT_TILES * P, D], F32, kind="Internal").ap()
    results = nc.dram_tensor("expert_results", [XT_TILES * P, D], F32, kind="Internal").ap()

    w_kv = sb("w_kv", [P, KH, 2 * D]); w_q = sb("w_q", [P, KH, D]); w_m = sb("w_m", [P, KH, D])
    w_1 = sb("w_1", [P, 2 * KH, H1]); w_2 = sb("w_2", [P, H1 // P, D])
    g_w1 = sb("g_w1", [P, KH, D]); g_w2 = sb("g_w2", [P, KH, D]); gate_w = sb("gate_w", [P, KH, NE])
    g_b1 = sb("g_b1", [P, KH]); m_g1 = sb("m_g1", [P, KH]); m_b1 = sb("m_b1", [P, KH])
    eps1 = sb("eps1", [P, 1])
    row_g2 = sb("row_g2", [P, D]); row_b2 = sb("row_b2", [P, D]); row_gb2 = sb("row_gb2", [P, D])
    gate_b = sb("gate_b_rows", [P, NE])
    e_w1 = sb("e_w1", [P, KH, NE * HE])
    e_b1 = sb("e_b1", [P, NE * HC]); e_b2 = sb("e_b2", [P, NE * D])

    xres = sb("xres", [P, NT, D])
    xT = sb("xT", [P, KH, NP])
    aggT = sb("aggT", [P, KH, NP])
    q_w2 = sb("q_w2", [P, NE * HC * D])
    qT = q_w2[:, 0:KH * NP].rearrange("p (h n) -> p h n", h=KH)
    e_w2 = q_w2[:, :].rearrange("p (c n) -> p c n", c=HC)

    ident = sb("ident", [P, P]); before = sb("before", [P, P]); ones = sb("ones", [P, P])
    heads = sb("heads", [P, P]); iota_w = sb("iota_w", [P, WIDE]); valid = sb("valid", [P, NT])
    epsln = sb("epsln", [P, 1]); zeros = sb("zeros", [P, D])

    early = e_w1[:, :, :].rearrange("p k n -> p (k n)")
    r_int = early[:, 0:4 * EW].bitcast(I32).rearrange("p (a b e) -> p a b e", a=2, b=2)
    r_f = early[:, 4 * EW:10 * EW].rearrange("p (a b e) -> p a b e", a=3, b=2)
    r_dst = early[:, 10 * EW:12 * EW].rearrange("p (b e) -> p b e", b=2)
    r_stat = sb("r_stat", [P, 2, 2])
    c_loc = sb("c_loc", [P, 2, GROUPS + GM]); c_w = sb("c_w", [P, 2, GROUPS + GM])
    c_dst = sb("c_dst", [P, 2, GROUPS]); c_src = sb("c_src", [P, 2, GROUPS], I32)
    RROW, MROW = -(-NB * GA // 4) * 4, -(-GM // 4) * 4
    base_a = sb("base_a", [1, NT // NB * RROW], I32); base_m = sb("base_m", [1, NT * MROW], I32)
    far = sb("far", [1, 4]); flag = sb("flag", [1, 1], I32)
    idx = sb("idx", [P, SLOTS], I32)
    spare = sb("spare", [P, 8 * D])
    gath = [early[:, s * D:(s + 1) * D] for s in range(12 * EW // D)] + [spare[:, s * D:(s + 1) * D] for s in range(8)]
    assert len(gath) == SLOTS

    xs = early[:, 12 * EW:12 * EW + NB * D].rearrange("p (j d) -> p j d", j=NB)
    onehot = early[:, 12 * EW:12 * EW + SLOTS * WIN].rearrange("p (s n) -> p s n", n=WIN)
    assert SLOTS * WIN <= NB * D
    stats = sb("stats", [P, NT, 6]); mv = sb("mv", [P, NT, 2])
    std = sb("std", [P, NT]); rstd = sb("rstd", [P, NT])
    space = [12 * EW + NB * D]

    def carve(n):
        space[0] += n
        assert space[0] <= KH * NE * HE
        return early[:, space[0] - n:space[0]]

    halves = lambda t: t.rearrange("p (h n) -> p h n", h=KH)
    xTs0 = halves(carve(D)); kqe = carve(2 * D); k_t = carve(D); v_t = halves(carve(KH * (P + 1)))
    kv_bd = halves(carve(D)); ks_bd = halves(carve(D)); den = carve(D); mT = halves(carve(D)); z1 = carve(D)
    mzT = halves(carve(D)); hT = carve(H1).rearrange("p (h n) -> p h n", n=P); z2 = carve(D)
    xTs = [xTs0, hT[:, 0:KH, :]]
    ks = sb("ks", [P, KH]); b2sum = sb("b2sum", [P, D])
    st2 = sb("st2", [P, 2, 6]); mv2 = sb("mv2", [P, 2, 2]); sd2 = sb("sd2", [P, 2]); rs2 = sb("rs2", [P, 2])
    LINKS = 9

    S = {n: sem(n) for n in (
        "loaded", "edges_loaded", "pads", "consts", "masks", "dve", "edge_rows", "edge_cols", "edge_done",
        "xn_store", "ln_std", "xs_ready", "xs_T", "xT_done", "x_loaded",
        "xTs_ready", "pe_qkv", "kq_min", "kq_exp", "kq_ready", "v_ready", "kv_acc",
        "onehots", "win_ready", "win_added", "idx_ready", "pool_past", "dve_past", "act_past", "pe_past",
        "bd_ready", "nd_ready", "mT_ready", "m_ready", "mv_ready", "sd_ready", "z1_ready", "zT_ready",
        "mzT_ready", "h_ready", "hT_ready", "m2_ready", "mv2_ready", "sd2_ready", "m2_free", "kv_zero", "zeroed")}
    assert XT_TILES % 8 == 0
    gath_done = [sem(f"gath_done{s}") for s in range(SLOTS)]
    dve_steps = Steps(S["dve"])

    def dve_link(eng, ins):
        eng.wait_ge(S["dve"], dve_steps.mark(ins))

    def load_values(engine, cells, most, why):
        _, values = nc.values_load_multi_w_load_instructions(cells, engines=[engine], min_val=0, max_val=most, skip_runtime_bounds_check_because=why)
        return values

    def bc(ap, shape):
        return ap.to_broadcast(shape)

    rows = lambda w: w.rearrange("(c p) n -> p c n", p=P)
    cols = lambda v: v.rearrange("(c p) -> p c", p=P)
    spread = lambda v: v.partition_broadcast(P)

    with nc.Block() as block:
        n_loads = 0

        @block.sync
        def _(sp):
            sp.wait_ge(S["pads"], 6)
            d_rows = [a["dst"][0:GFULL * EW].rearrange("(g e) -> g e", e=EW), a["src"][0:GFULL * EW].rearrange("(g e) -> g e", e=EW),
                      a["edge_weight"][0:GFULL * EW].rearrange("(g e) -> g e", e=EW)]
            tails = [v[GFULL * EW:E].rearrange("(a e) -> a e", a=1) for v in (a["dst"], a["src"], a["edge_weight"])]
            for j in range(3):
                t = r_int[:, j] if j < 2 else r_f[:, 1]
                sp.dma_start(t[:, 0, :], d_rows[j][0:P, :]).then_inc(S["edges_loaded"], 16)
                sp.dma_start(t[0:GB, 1, :], d_rows[j][P:GFULL, :]).then_inc(S["edges_loaded"], 16)
                sp.dma_start(t[GB:GB + 1, 1, 0:GREST], tails[j]).then_inc(S["edges_loaded"], 16)
            for b in range(5):
                lo, hi = b * NB, min((b + 1) * NB, NT - 1)
                sp.dma_start(xres[:, lo:hi, :], a["x"][lo * P:hi * P, :].rearrange("(t p) d -> p t d", p=P)).then_inc(S["x_loaded"], 16)
            sp.dma_start(xres[0:LAST, NT - 1, :], a["x"][(NT - 1) * P:N, :]).then_inc(S["x_loaded"], 16)
            for j in range(XT_TILES // 8):
                sp.dma_start(lists[j * 8 * P:(j + 1) * 8 * P, :].rearrange("(p r) d -> p r d", r=8), zeros[:, :].unsqueeze(1).to_broadcast([P, 8, D])).then_inc(S["zeroed"], 16)
            with sp.Fori(0, NT // NB) as i:
                sp.wait_ge(S["xs_ready"], i * NB + NB)
                for j in range(NB):
                    sp.dma_start(xn_rows[ds(i * (NB * P) + j * P, P), :], xs[:, j, :]).then_inc(S["xn_store"], 16)
            sp.wait_ge(S["xn_store"], 16 * NT)
            sp.wait_ge(S["zeroed"], 16 * (XT_TILES // 8))

        @block.gpsimd
        def _(pool):
            pool.memset(r_int[:, 0, 1, :], N).then_inc(S["pads"], 1)
            pool.memset(r_int[:, 1, 1, :], 0).then_inc(S["pads"], 1)
            pool.memset(r_f[:, 1, 1, :], 0.0).then_inc(S["pads"], 1)
            pool.memset(xres[:, NT - 1, :], 0.0).then_inc(S["pads"], 1)
            pool.memset(epsln[:, :], LN_EPS).then_inc(S["pads"], 1)
            pool.memset(zeros[:, :], 0.0).then_inc(S["pads"], 1)
            pool.memset(ident[:, :], 0.0)
            for m in (before, ones, heads, valid):
                pool.memset(m[:, :], 1.0)
            pool.memset(c_loc[:, :, :], 0.0)
            pool.memset(c_w[:, :, :], 0.0)
            pool.iota(iota_w[:, :], pattern=[[1, WIDE]], base=0, channel_multiplier=0,
                      allow_small_or_imprecise_dtypes=True).then_inc(S["consts"], 1)
            pool.wait_ge(S["consts"], 1)
            pool.affine_select(out=ident[:, :], in_=ident[:, :], compare_op=ALU.not_equal, fill=1.0, base=0,
                               pattern=[[-1, P]], channel_multiplier=1).then_inc(S["masks"], 1)
            pool.affine_select(out=before[:, :], in_=before[:, :], compare_op=ALU.is_gt, fill=0.0, base=0,
                               pattern=[[1, P]], channel_multiplier=-1).then_inc(S["masks"], 1)
            pool.affine_select(out=valid[:, :], in_=valid[:, :], compare_op=ALU.is_gt, fill=0.0, base=N,
                               pattern=[[-P, NT]], channel_multiplier=-1).then_inc(S["masks"], 1)
            hv = heads[:, :].rearrange("p (b c) -> p b c", c=DH)
            pool.affine_select(out=hv, in_=hv, compare_op=ALU.is_ge, fill=0.0, base=0,
                               pattern=[[-DH, P // DH], [0, DH]], channel_multiplier=1).then_inc(S["masks"], 1)
            pool.wait_ge(S["masks"], 4)
            pool.affine_select(out=hv, in_=hv, compare_op=ALU.is_ge, fill=0.0, base=DH - 1,
                               pattern=[[DH, P // DH], [0, DH]], channel_multiplier=-1).then_inc(S["masks"], 1)

        @block.scalar
        def _(act):
            for t, v in ((w_kv[:, :, 0:D], rows(a["L0_mix_Wk"])), (w_kv[:, :, D:2 * D], rows(a["L0_mix_Wv"])), (w_q[:, :, :], rows(a["L0_mix_Wq"])),
                         (w_m[:, :, :], rows(a["L0_mix_Wm"])), (w_1[:, :, :], rows(a["L0_mix_W1"])), (w_2[:, :, :], rows(a["L0_mix_W2"])),
                         (g_w1[:, :, :], rows(a["L0_gnn_w1"])), (g_w2[:, :, :], rows(a["L0_gnn_w2"])), (gate_w[:, :, :], rows(a["L0_ffn_gate_w"])),
                         (g_b1[:, :], cols(a["L0_gnn_b1"])), (m_g1[:, :], cols(a["L0_mix_g1"])), (m_b1[:, :], cols(a["L0_mix_b1"])),
                         (eps1[:, :], spread(a["L0_gnn_eps"])),
                         (row_g2[:, :], spread(a["L0_mix_g2"])), (row_b2[:, :], spread(a["L0_mix_b2"])), (row_gb2[:, :], spread(a["L0_gnn_b2"])),
                         (gate_b[:, :], spread(a["L0_ffn_gate_b"]))):
                act.dma_start(t, v, allow_slow_non_contiguous=True).then_inc(S["loaded"], 16)
            act.wait_ge(S["loaded"], 16 * 17)
            act.wait_ge(S["pads"], 6)
            act.wait_ge(S["ln_std"], 1)
            act.activation(std[:, :], mv[:, :, 1], ACT.Sqrt, bias=epsln[:, 0:1]).then_inc(S["ln_std"], 1)
            with act.Fori(0, NT // NB) as i:
                for j in range(NB):
                    act.wait_ge(S["xs_T"], i * NB + j + 1)
                    act.sem_inc(S["act_past"], 1)
                    act.activation(xT[:, :, ds(i * (NB * P) + j * P, P)], bank[j % 2][:, 0:D].rearrange("p (h n) -> p h n", h=KH), ACT.Copy).then_inc(S["xT_done"], 1)

        @block.vector
        def _(dve):
            dve.memset(aggT[:, :, :], 0.0)
            dve.wait_ge(S["x_loaded"], 96)
            for t in range(NT):
                ins = dve.bn_stats(stats[:, t, :], xres[:, t, :])
            dve_link(dve, ins)
            for t in range(NT):
                ins = dve.bn_aggr(mv[:, t, :], stats[:, t, :])
            ins.then_inc(S["ln_std"], 1)
            dve.wait_ge(S["ln_std"], 2)
            dve_link(dve, dve.reciprocal(rstd[:, :], std[:, :]))
            with dve.Fori(0, NT // NB) as i:
                dve_steps.enter(i, 1)
                for j in range(NB):
                    t = i * NB + j
                    dve.tensor_scalar(xs[:, j, :], xres[:, ds(t, 1), :].rearrange("p a d -> p (a d)"), mv[:, ds(t, 1), 0:1].rearrange("p a d -> p (a d)"),
                                      rstd[:, ds(t, 1)], ALU.subtract, ALU.mult).then_inc(S["xs_ready"], 1)
                dve.wait_ge(S["xs_ready"], i * NB + NB)
                for j in range(NB):
                    t = i * NB + j
                    v = xres[:, ds(t, 1), :].rearrange("p a d -> p (a d)")
                    ins = dve.tensor_tensor(v, v, xs[:, j, :], ALU.add)
                dve_link(dve, ins)
                dve.wait_ge(S["xn_store"], (i + 1) * (NB * 16))
                dve.wait_ge(S["xs_T"], (i + 1) * NB)
            dve_steps.leave(NT // NB)
            dve.wait_ge(S["edges_loaded"], 144)
            dve_link(dve, dve.tensor_copy(r_dst[:, :, :], r_int[:, 0, :, :]))
            dve.tensor_copy(r_f[:, 2, :, :], r_int[:, 1, :, :])
            dve_link(dve, dve.tensor_reduce(r_stat[:, 0, :], r_dst[:, :, :], AX.X, ALU.min))
            for b in range(2):
                ins = dve.tensor_scalar(r_f[:, 0, b, :], r_dst[:, b, :], r_stat[:, 0, b:b + 1], None, ALU.subtract)
            dve_link(dve, ins)
            dve_link(dve, dve.scalar_tensor_tensor(out=xs[:, 0:2, :], in0=r_dst[:, :, :], scalar=float(N), in1=r_f[:, 0, :, :],
                                                   op0=ALU.is_lt, op1=ALU.mult))
            dve.tensor_reduce(r_stat[:, 1, :], xs[:, 0:2, :], AX.X, ALU.max).then_inc(S["edge_rows"], 1)
            for n, dst in enumerate((c_loc, c_w, c_src, c_dst)):
                dve.wait_ge(S["edge_cols"], n + 1)
                ps = bank[2 + n][:, :].rearrange("p (h g) -> p h g", h=2)
                dve.tensor_copy(dst[:, :, 0:GROUPS], ps[:, :, 0:GROUPS]).then_inc(S["edge_done"], 1)
            dve.wait_ge(S["edge_cols"], 5)
            dve.tensor_copy(base_a[:, :].rearrange("p (i g) -> p i g", g=RROW)[:, :, 0:NB * GA],
                            bank[6][0:1, 0:NT * GA].rearrange("p (i g) -> p i g", g=NB * GA))
            dve.tensor_copy(base_m[:, :].rearrange("p (i g) -> p i g", g=MROW)[:, :, 0:GM],
                            bank[6][0:1, NT * GA:GROUPS].rearrange("p (i g) -> p i g", g=GM)).then_inc(S["edge_done"], 1)
            dve_link(dve, dve.tensor_reduce(far[:, 0:1], bank[6][0:1, 2 * P:4 * P], AX.X, ALU.max))
            dve.tensor_scalar(flag[:, :], far[:, 0:1], float(WIN), None, ALU.is_ge).then_inc(S["edge_done"], 1)

        @block.tensor
        def _(pe):
            pe.wait_ge(S["masks"], 1)
            with pe.Fori(0, NT // NB) as i:
                for j in range(NB):
                    pe.wait_ge(S["xs_ready"], i * NB + j + 1)
                    if j >= 2:
                        pe.wait_ge(S["xT_done"], i * NB + j - 1)
                    for h in range(KH):
                        ins = pe.transpose(bank[j % 2][:, h * P:(h + 1) * P], xs[:, j, h * P:(h + 1) * P], ident[:, :])
                    ins.then_inc(S["xs_T"], 1)
                pe.wait_ge(S["xT_done"], (i + 1) * NB)
                pe.sem_inc(S["pe_past"], 1)
            pe.wait_ge(S["edge_rows"], 1)
            for n in range(4):
                for h in range(2):
                    for b in range(2):
                        t = r_f[:, n, b, h * P:(h + 1) * P] if n < 3 else r_dst[:, b, h * P:(h + 1) * P]
                        ins = pe.transpose(bank[2 + n][:, h * 256 + b * P:h * 256 + (b + 1) * P], t, ident[:, :])
                ins.then_inc(S["edge_cols"], 1)
            for s in range(2):
                for b in range(2):
                    ins = pe.matmul(bank[6][0:1, s * 256 + b * P:s * 256 + (b + 1) * P], r_stat[:, s, b:b + 1], ident[:, :], start=True, stop=True)
            ins.then_inc(S["edge_cols"], 1)


    RING = NB * GA
    ps_kq, ps_v, ps_sum = [bank[0], bank[1]], [bank[5], bank[6]], bank[2]
    ps_win = [bank[3], bank[4]]
    ps_nd, ps_m, ps_hid, ps_zT, ps_m2 = bank[0], bank[1], bank[5], bank[6], bank[7]
    STAGES = 5

    def active(i, stage):
        return not isinstance(i, int) or 0 <= i - stage < NT

    def second_pass(eng, step, around=None):
        for i in range(STAGES - 1):
            step(i)
        with eng.Fori(STAGES - 1, NT) as i:
            if around:
                around.enter(i - (STAGES - 1), LINKS)
            step(i)
        if around:
            around.leave(NT - (STAGES - 1))
        for i in range(NT, NT + STAGES - 1):
            step(i)

    with nc.Block() as block:

        @block.gpsimd
        def _(pool):
            def fetch(slots, columns, copies):
                lo, hi = slots
                pool.tensor_copy(idx[:, lo:hi].rearrange("p (g h) -> p h g", h=2), c_src[:, :, ds(columns, (hi - lo) // 2)]).then_inc(S["idx_ready"], 1)
                pool.wait_ge(S["idx_ready"], copies)
                pool.sem_inc(S["pool_past"], 1)
                for s in range(lo, hi):
                    pool.indirect_dma_start(out=gath[s], out_offset=None, in_=xn_rows[:, :],
                                            in_offset=bass.IndirectOffsetOnAxis(ap=idx[:, s:s + 1], axis=0)).then_inc(gath_done[s], 16)

            pool.wait_ge(S["edge_done"], 3)
            with pool.Fori(0, NT // NB) as i:
                for half in range(2):
                    n = RING // 2
                    pool.wait_ge(S["win_ready"], i * RING + (half + 1) * n)
                    pool.sem_inc(S["pool_past"], 1)
                    fetch((half * 2 * n, (half + 1) * 2 * n), i * RING + half * n, i * 2 + (half + 1))
            with pool.Fori(0, NT) as i:
                for half in range(2):
                    n = GM // 2
                    pool.wait_ge(S["win_ready"], i * GM + (RING + NT * GA - GM + (half + 1) * n))
                    pool.sem_inc(S["pool_past"], 1)
                    fetch((half * 2 * n, (half + 1) * 2 * n), i * GM + (NT * GA + half * n), i * 2 + (2 * (NT // NB) + half + 1))

        @block.tensor
        def _(pe):
            def group(G, place, rounds, hots):
                pe.wait_ge(S["win_added"], G + 1)
                for h in range(2):
                    s = 2 * place + h
                    pe.wait_ge(gath_done[s], rounds)
                    pe.wait_ge(S["onehots"], hots + (h + 1))
                    for m in range(KH):
                        ins = pe.matmul(ps_win[place % 2][:, m * WIN:(m + 1) * WIN], gath[s][:, m * P:(m + 1) * P], onehot[:, s, :],
                                        start=(h == 0 and m == 0), stop=(h == 1), skip_group_check=True)
                ins.then_inc(S["win_ready"], 1)

            def sum_kv():
                for m in range(KH):
                    ins = pe.matmul(ps_sum[:, m * (P + 1):(m + 1) * (P + 1)], k_t[:, m * P:(m + 1) * P], v_t[:, m, :],
                                    start=False, stop=True, skip_group_check=True)
                ins.then_inc(S["kv_acc"], 1)

            pe.sem_inc(S["win_ready"], RING)
            pe.sem_inc(S["pe_qkv"], 2)
            pe.wait_ge(S["kv_zero"], 1)
            pe.matmul(ps_sum[:, 0:KH * (P + 1)], ident[:, :], kqe[:, 0:KH * (P + 1)], start=True, stop=True, skip_group_check=True).then_inc(S["kv_acc"], 1)
            with pe.Fori(0, NT // NB) as i:
                for j in range(NB):
                    t = i * NB + j
                    first = lambda g: group(i * RING + (j * GA + g), j * GA + g, i * 16 + 16, i * (2 * RING) + 2 * (j * GA + g))
                    pe.wait_ge(S["xTs_ready"], t + 1)
                    pe.wait_ge(S["kq_ready"], t + (2 if j == 0 else 1))
                    pe.wait_ge(S["v_ready"], t + (2 if j == 0 else 1))
                    kq, x = ps_kq[j % 2], xTs[j % 2]
                    for k in range(KH):
                        pe.matmul(kq[:, 0:D], x[:, k, :], w_kv[:, k, 0:D], start=(k == 0), stop=(k == KH - 1))
                    for m in range(KH):
                        for k in range(KH):
                            pe.matmul(kq[:, D + m * P:D + (m + 1) * P], w_q[:, k, m * P:(m + 1) * P], x[:, k, :], start=(k == 0), stop=(k == KH - 1))
                    for k in range(KH):
                        ins = pe.matmul(ps_v[j % 2][:, 0:D], x[:, k, :], w_kv[:, k, D:2 * D], start=(k == 0), stop=(k == KH - 1))
                    ins.then_inc(S["pe_qkv"], 1)
                    first(0)
                    pe.wait_ge(S["kq_ready"], t + 2)
                    pe.wait_ge(S["v_ready"], t + 2)
                    sum_kv()
                    first(1)
            pe.wait_ge(S["kq_ready"], NT + 2)
            pe.wait_ge(S["v_ready"], NT + 2)
            sum_kv()

            def step(i):
                def sums(*gs):
                    if active(i, 0):
                        for g in gs:
                            group(i * GM + (NT * GA + g), g, i * 16 + 16 * (NT // NB + 1), i * (2 * GM) + (2 * RING + 2 * NT * GA - 2 * GM + 2 * g))

                if active(i, 4):
                    pe.wait_ge(S["hT_ready"], i - 3)
                    pe.wait_ge(S["m2_free"], i - 3)
                    for k in range(H1 // P):
                        ins = pe.matmul(ps_m2[:, 0:D], hT[:, k, :], w_2[:, k, :], start=(k == 0), stop=(k == H1 // P - 1))
                    ins.then_inc(S["m2_ready"], 1)
                sums(0)
                if active(i, 3):
                    pe.wait_ge(S["mzT_ready"], i - 2)
                    for o in range(H1 // P):
                        for k in range(2 * KH):
                            rhs = xT[:, k, ds((i - 3) * P, P)] if k < KH else mzT[:, k - KH, :]
                            ins = pe.matmul(ps_hid[:, o * P:(o + 1) * P], w_1[:, k, o * P:(o + 1) * P], rhs, start=(k == 0), stop=(k == 2 * KH - 1))
                    ins.then_inc(S["h_ready"], 1)
                sums(1)
                if active(i, 2):
                    pe.wait_ge(S["z1_ready"], i - 1)
                    for m in range(KH):
                        ins = pe.transpose(ps_zT[:, m * P:(m + 1) * P], z1[:, m * P:(m + 1) * P], ident[:, :])
                    ins.then_inc(S["zT_ready"], 1)
                sums(2)
                if active(i, 1):
                    pe.wait_ge(S["mT_ready"], i)
                    for k in range(KH):
                        ins = pe.matmul(ps_m[:, 0:D], mT[:, k, :], w_m[:, k, :], start=(k == 0), stop=(k == KH - 1))
                    ins.then_inc(S["m_ready"], 1)
                sums(3, 4)
                if active(i, 0):
                    if isinstance(i, int) and i == 0:
                        pe.wait_ge(S["bd_ready"], 1)
                    for m in range(KH):
                        pe.matmul(ps_nd[:, m * P:(m + 1) * P], kv_bd[:, m, :], qT[:, m, ds(i * P, P)], start=True, stop=True)
                    for m in range(KH):
                        ins = pe.matmul(ps_nd[:, D + m * P:D + (m + 1) * P], ks_bd[:, m, :], qT[:, m, ds(i * P, P)], start=True, stop=True)
                    ins.then_inc(S["nd_ready"], 1)
                sums(5)

            second_pass(pe, step)

        @block.vector
        def _(dve):
            def build(place, G):
                for h in range(2):
                    dve.tensor_scalar(onehot[:, 2 * place + h, :], iota_w[:, 0:WIN], c_loc[:, h, ds(G, 1)], c_w[:, h, ds(G, 1)],
                                      ALU.is_equal, ALU.mult).then_inc(S["onehots"], 1)

            def add(G, place, ahead, first):
                dve.wait_ge(S["win_ready"], G + (RING + 1))
                dve.sem_inc(S["dve_past"], 1)
                v = aggT[:, :, ds(first, WIN)]
                dve.tensor_tensor(v, v, ps_win[place % 2][:, 0:KH * WIN].rearrange("p (h n) -> p h n", h=KH), ALU.add).then_inc(S["win_added"], 1)
                build(place, G + ahead)
                dve.wait_ge(S["win_added"], G + 3)


            dve.memset(kqe[:, :], 0.0)
            dve.memset(k_t[:, :], 0.0)
            dve.memset(v_t[:, :, :], 0.0).then_inc(S["kv_zero"], 1)
            for n in ("win_added", "kq_ready"):
                dve.sem_inc(S[n], 2)
            dve.wait_ge(S["edge_done"], 5)
            for g in range(RING):
                build(g, g)
            with dve.Fori(0, NT // NB) as i:
                r = load_values(mybir.EngineType.DVE, base_a[0:1, ds(i * RROW, RING)], N, "a group's first node is a dst, or N where the group is padding")
                for j in range(NB):
                    t = i * NB + j
                    G = i * RING + j * GA
                    dve.wait_ge(S["kv_acc"], t + 1)
                    dve.wait_ge(S["kq_ready"], t + 2)
                    dve.wait_ge(S["pe_qkv"], t + 3)
                    dve.tensor_scalar(kqe[:, :], ps_kq[j % 2][:, :], 0.0, None, ALU.min).then_inc(S["kq_min"], 1)
                    add(G, j * GA, RING, r[j * GA])
                    dve.wait_ge(S["kq_exp"], t + 1)
                    dve.wait_ge(S["kv_acc"], t + 2)
                    dve.scalar_tensor_tensor(out=k_t[:, :], in0=ps_kq[j % 2][:, 0:D], scalar=0.0, in1=kqe[:, 0:D], op0=ALU.max, op1=ALU.add)
                    dve.scalar_tensor_tensor(out=qT[:, :, ds(t * P, P)], in0=halves(ps_kq[j % 2][:, D:2 * D]), scalar=0.0, in1=halves(kqe[:, D:2 * D]),
                                             op0=ALU.max, op1=ALU.add).then_inc(S["kq_ready"], 1)
                    add(G + 1, j * GA + 1, RING, r[j * GA + 1])
            dve.wait_ge(S["kv_acc"], NT + 2)
            for m in range(KH):
                dve.tensor_tensor(kv_bd[:, m, :], heads[:, :], ps_sum[:, m * (P + 1):m * (P + 1) + P], ALU.mult)
                ins = dve.tensor_copy(ks[:, m:m + 1], ps_sum[:, m * (P + 1) + P:(m + 1) * (P + 1)])
            dve_link(dve, ins)
            for m in range(KH):
                ins = dve.tensor_scalar(ks_bd[:, m, :], heads[:, :], ks[:, m:m + 1], None, ALU.mult)
            ins.then_inc(S["bd_ready"], 1)
            dve_link(dve, dve.tensor_tensor(b2sum[:, :], row_b2[:, :], row_gb2[:, :], ALU.add))
            dve.sem_inc(S["m2_free"], 1)

            def moments(src, n, ready):
                dve_link(dve, dve.bn_stats(st2[:, n, :], src))
                dve.sem_inc(S["dve_past"], 1)
                dve.bn_aggr(mv2[:, n, :], st2[:, n, :]).then_inc(S[ready], 1)

            def normalise(src, n, dst):
                dve_link(dve, dve.reciprocal(rs2[:, n:n + 1], sd2[:, n:n + 1]))
                return dve.tensor_scalar(dst, src, mv2[:, n, 0:1], rs2[:, n:n + 1], ALU.subtract, ALU.mult)

            def step(i):
                def sums(*gs):
                    if active(i, 0):
                        for g in gs:
                            add(i * GM + (NT * GA + g), g, GM, r[g])

                if active(i, 0):
                    r = load_values(mybir.EngineType.DVE, base_m[0:1, ds(i * MROW, GM)], N, "a group's first node is a dst, or N where the group is padding")
                if active(i, 4):
                    dve.wait_ge(S["m2_ready"], i - 3)
                    moments(ps_m2[:, 0:D], 1, "mv2_ready")
                sums(0)
                if active(i, 4):
                    t = i - 4
                    dve.wait_ge(S["sd2_ready"], i - 3)
                    normalise(ps_m2[:, 0:D], 1, z2[:, :]).then_inc(S["m2_free"], 1)
                    dve.wait_ge(S["m2_free"], i - 2)
                    dve_link(dve, dve.tensor_tensor(z2[:, :], z2[:, :], row_g2[:, :], ALU.mult))
                    dve_link(dve, dve.tensor_tensor(z2[:, :], z2[:, :], b2sum[:, :], ALU.add))
                    v = xres[:, ds(t, 1), :].rearrange("p a d -> p (a d)")
                    dve_link(dve, dve.tensor_tensor(v, v, z2[:, :], ALU.add))
                sums(1, 2)
                if active(i, 1):
                    dve.wait_ge(S["m_ready"], i)
                    moments(ps_m[:, 0:D], 0, "mv_ready")
                sums(3)
                if active(i, 1):
                    dve.wait_ge(S["sd_ready"], i)
                    normalise(ps_m[:, 0:D], 0, z1[:, :]).then_inc(S["z1_ready"], 1)
                sums(4)
                if active(i, 0):
                    dve.wait_ge(S["nd_ready"], i + 1)
                    dve_link(dve, dve.tensor_scalar(den[:, :], ps_nd[:, D:2 * D], ATT_EPS, None, ALU.add))
                    dve_link(dve, dve.reciprocal(den[:, :], den[:, :]))
                    dve.scalar_tensor_tensor(out=mT[:, :, :], in0=halves(ps_nd[:, 0:D]), scalar=float(N), in1=halves(den[:, :]),
                                             op0=ALU.mult, op1=ALU.mult).then_inc(S["mT_ready"], 1)
                sums(5)
                if active(i, 0):
                    dve.wait_ge(S["mT_ready"], i + 1)
                if active(i, 1):
                    dve.wait_ge(S["z1_ready"], i)

            second_pass(dve, step, dve_steps)

        @block.scalar
        def _(act):
            def prepare(t, b, count):
                act.wait_ge(S["pe_qkv"], count)
                act.sem_inc(S["act_past"], 1)
                act.activation(xTs[b][:, :, :], xT[:, :, ds(t * P, P)], ACT.Copy).then_inc(S["xTs_ready"], 1)

            act.sem_inc(S["v_ready"], 2)
            with act.Fori(0, NT // NB) as i:
                prepare(i * NB, 0, i * NB + 2)
                for j in range(NB):
                    t = i * NB + j
                    if j < NB - 1:
                        prepare(t + 1, (j + 1) % 2, t + 2)
                    act.wait_ge(S["kq_min"], t + 1)
                    act.activation(kqe[:, :], kqe[:, :], ACT.Exp).then_inc(S["kq_exp"], 1)
                    act.wait_ge(S["kv_acc"], t + 2)
                    act.activation(v_t[:, :, P:P + 1], bc(valid[:, ds(t, 1)].unsqueeze(1), [P, KH, 1]), ACT.Copy)
                    act.activation(v_t[:, :, 0:P], halves(ps_v[j % 2][:, 0:D]), ACT.Copy, scale=1.0 / N).then_inc(S["v_ready"], 1)

            def step(i):
                if active(i, 4):
                    act.wait_ge(S["mv2_ready"], i - 3)
                    act.activation(sd2[:, 1:2], mv2[:, 1, 1:2], ACT.Sqrt, bias=epsln[:, 0:1]).then_inc(S["sd2_ready"], 1)
                if active(i, 3):
                    act.wait_ge(S["h_ready"], i - 2)
                    act.activation(hT[:, :, :], ps_hid[:, :].rearrange("p (o n) -> p o n", n=P), ACT.Relu).then_inc(S["hT_ready"], 1)
                if active(i, 2):
                    act.wait_ge(S["zT_ready"], i - 1)
                    for m in range(KH):
                        ins = act.activation(mzT[:, m, :], ps_zT[:, m * P:(m + 1) * P], ACT.Identity, scale=m_g1[:, m:m + 1], bias=m_b1[:, m:m + 1])
                    ins.then_inc(S["mzT_ready"], 1)
                if active(i, 1):
                    act.wait_ge(S["mv_ready"], i)
                    act.activation(sd2[:, 0:1], mv2[:, 0, 1:2], ACT.Sqrt, bias=epsln[:, 0:1]).then_inc(S["sd_ready"], 1)

            second_pass(act, step)

    for n in ("far_left", "far_free", "far_idx", "far_got", "far_scaled", "far_onehot", "far_sums", "far_added"):
        S[n] = sem(n)
    WIDES = NP // WIDE
    assert NP % WIDE == 0
    far_hot = early[:, 0:WIDE]
    with nc.Block() as block:

        @block.gpsimd
        def _(pool):
            taken, = load_values(mybir.EngineType.Pool, flag[0:1, 0:1], 1, "the outcome of a comparison")
            with pool.If(taken == 1):
                with pool.Fori(0, GROUPS) as g:
                    for h in range(2):
                        pool.wait_ge(S["far_free"], g * 2 + (h + 1))
                        pool.sem_inc(S["pool_past"], 1)
                        pool.tensor_copy(idx[:, 0:1], c_src[:, h, ds(g, 1)]).then_inc(S["far_idx"], 1)
                        pool.wait_ge(S["far_idx"], g * 2 + (h + 1))
                        pool.sem_inc(S["pool_past"], 1)
                        pool.indirect_dma_start(out=gath[0], out_offset=None, in_=xn_rows[:, :],
                                                in_offset=bass.IndirectOffsetOnAxis(ap=idx[:, 0:1], axis=0)).then_inc(S["far_got"], 16)

        @block.vector
        def _(dve):
            taken, = load_values(mybir.EngineType.DVE, flag[0:1, 0:1], 1, "the outcome of a comparison")
            with dve.If(taken == 1):
                v = c_w[:, :, :]
                dve.scalar_tensor_tensor(out=v, in0=c_loc[:, :, :], scalar=float(WIN), in1=v, op0=ALU.is_ge, op1=ALU.mult).then_inc(S["far_left"], 1)
                dve.wait_ge(S["far_left"], 1)
                dve.sem_inc(S["far_free"], 1)
                with dve.Fori(0, GROUPS) as g:
                    for h in range(2):
                        c = g * 2 + h
                        dve.wait_ge(S["far_got"], c * 16 + 16)
                        dve.sem_inc(S["dve_past"], 1)
                        dve.tensor_scalar(gath[0], gath[0], c_w[:, h, ds(g, 1)], None, ALU.mult).then_inc(S["far_scaled"], 1)
                        for w in range(WIDES):
                            k = c * WIDES + w
                            dve.tensor_scalar(far_hot[:, :], iota_w[:, :], c_dst[:, h, ds(g, 1)], float(-w * WIDE),
                                              ALU.subtract, ALU.is_equal).then_inc(S["far_onehot"], 1)
                            dve.wait_ge(S["far_sums"], k + 1)
                            for m in range(KH):
                                v = aggT[:, m, w * WIDE:(w + 1) * WIDE]
                                ins = dve.tensor_tensor(v, v, bank[m][:, 0:WIDE], ALU.add)
                            ins.then_inc(S["far_added"], 1)
                            dve.wait_ge(S["far_added"], k + 1)
                        dve.sem_inc(S["far_free"], 1)

        @block.tensor
        def _(pe):
            taken, = load_values(mybir.EngineType.PE, flag[0:1, 0:1], 1, "the outcome of a comparison")
            with pe.If(taken == 1):
                with pe.Fori(0, 2 * GROUPS) as c:
                    pe.wait_ge(S["far_scaled"], c + 1)
                    pe.sem_inc(S["pe_past"], 1)
                    for w in range(WIDES):
                        pe.wait_ge(S["far_onehot"], c * WIDES + (w + 1))
                        for m in range(KH):
                            ins = pe.matmul(bank[m][:, 0:WIDE], gath[0][:, m * P:(m + 1) * P], far_hot[:, :], start=True, stop=True)
                        ins.then_inc(S["far_sums"], 1)

    gflat = spare
    NB_TOK = NB * P
    PIECE = NB_TOK // 2
    g1T = gflat[:, 0:KH * NB_TOK].rearrange("p (h n) -> p h n", h=KH)
    xn2 = gflat[:, 0:NB * D].rearrange("p (j d) -> p j d", j=NB)
    xn2T = gflat[:, NB * D:NB * D + 2 * D].rearrange("p (b h n) -> p b h n", b=2, h=KH)
    xf = xT[:, :, :].rearrange("p h n -> p (h n)").rearrange("p (t d) -> p t d", d=D)
    TN = NT * NE
    TT = XT_TILES
    agg_flat = aggT[:, :, :].rearrange("p h n -> p (h n)")
    taken = [0]

    def late(*shape):
        n = 1
        for d in shape:
            n *= d
        taken[0] += n
        v = agg_flat[:, KH * NP - taken[0]:KH * NP - taken[0] + n]
        return v if len(shape) == 1 else v.rearrange("p (a b) -> p a b", b=shape[-1])

    logits, probs, rtmp, chosen = (late(NT, NE) for _ in range(4))
    picks2 = late(2 * NT, NE)
    picks = picks2.rearrange("p (k t) e -> p k t e", k=2)
    run_in, run = late(NE, NT), late(NE, NT)
    past = late(TT, NE - 1)
    rev = sb("rev", [P, NE]); rmax = sb("rmax", [P, NT]); wts = sb("wts", [P, 2, NT]); slots = sb("slots", [P, 2, NT], I32)
    slot_f = sb("slot_f", [P, 2, NT]);
    count = sb("count", [P, NE]); count_i = sb("count_i", [P, NE], I32); ntile = sb("ntile", [P, NE]); until = sb("until", [P, NE])
    shift = sb("shift", [P, NE])
    jt = sb("jt", [P, TT]); t_exp = sb("t_exp", [P, TT])
    ti_exp = sb("ti_exp", [P, TT], I32)
    for n in ("h0_ready", "g1_ready", "g1T_ready", "g2_ready", "g2_done", "experts_loaded", "std2", "n2_ready", "n2_copied", "n2_T", "n2T_ready",
              "logit_ready", "logits_done", "soft", "chosen_ready", "ranks_ready", "slots_ready", "tables_ready", "scattered", "tails", "pool_consts",
              "xg_T", "xgT_ready", "he_ready", "hs_ready", "heT_ready", "gelu_ready", "ye_ready", "y_ready", "ye_free", "sp_past", "t_done"):
        S[n] = sem(n)
    xg_loaded = [sem(f"xg_loaded{b}") for b in range(2)]
    y_stored = [sem(f"y_stored{b}") for b in range(2)]

    with nc.Block() as block:

        @block.sync
        def _(sp):
            for k in range(KH):
                sp.dma_start(e_w1[:, k, :].rearrange("p (e n) -> p e n", e=NE), a["L0_ffn_W1"][:, k * P:(k + 1) * P, :].rearrange("e p n -> p e n")).then_inc(S["experts_loaded"], 16)
            for c in range(HC):
                sp.dma_start(e_w2[:, c, :].rearrange("p (e n) -> p e n", e=NE), a["L0_ffn_W2"][:, c * P:(c + 1) * P, :].rearrange("e p n -> p e n")).then_inc(S["experts_loaded"], 16)
            sp.dma_start(e_b1[:, :], a["L0_ffn_b1"].rearrange("e (c p) -> p (e c)", p=P), allow_slow_non_contiguous=True).then_inc(S["experts_loaded"], 16)
            sp.dma_start(e_b2[:, :], a["L0_ffn_b2"].rearrange("e n -> (e n)").partition_broadcast(P)).then_inc(S["experts_loaded"], 16)
            sp.wait_ge(S["experts_loaded"], 16 * (KH + HC + 2))

        @block.vector
        def _(dve):
            dve_link(dve, dve.tensor_scalar(eps1[:, :], eps1[:, :], 1.0, None, ALU.add))
            for i in range(NT // NB):
                v = aggT[:, :, i * NB_TOK:(i + 1) * NB_TOK]
                dve.scalar_tensor_tensor(out=v, in0=xT[:, :, i * NB_TOK:(i + 1) * NB_TOK], scalar=eps1[:, 0:1], in1=v,
                                         op0=ALU.mult, op1=ALU.add).then_inc(S["h0_ready"], 1)
            with dve.Fori(0, NT // NB) as i:
                dve_steps.enter(i, 2 * NB)
                for j in range(NB):
                    t = i * NB + j
                    v = xres[:, ds(t, 1), :].rearrange("p a d -> p (a d)")
                    dve.wait_ge(S["g2_ready"], i * NB + (j + 1))
                    dve_link(dve, dve.tensor_tensor(v, v, bank[4 + j % 4][:, 0:D], ALU.add))
                    dve.sem_inc(S["g2_done"], 1)
                    dve_link(dve, dve.bn_stats(stats[:, ds(t, 1), :].rearrange("p a d -> p (a d)"), v))
            dve_steps.leave(NT // NB)
            for t in range(NT):
                ins = dve.bn_aggr(mv[:, t, :], stats[:, t, :])
            ins.then_inc(S["std2"], 1)
            dve.wait_ge(S["std2"], 2)
            dve_link(dve, dve.reciprocal(rstd[:, :], std[:, :]))
            with dve.Fori(0, NT // NB) as i:
                for j in range(NB):
                    t = i * NB + j
                    dve.tensor_scalar(xn2[:, j, :], xres[:, ds(t, 1), :].rearrange("p a d -> p (a d)"), mv[:, ds(t, 1), 0:1].rearrange("p a d -> p (a d)"),
                                      rstd[:, ds(t, 1)], ALU.subtract, ALU.mult).then_inc(S["n2_ready"], 1)
                for j in range(NB):
                    t = i * NB + j
                    dve.wait_ge(S["logit_ready"], i * NB + (j + 1))
                    dve.tensor_tensor(logits[:, ds(t, 1), :].rearrange("p a e -> p (a e)"), bank[2 + j % 2][:, 0:NE], gate_b[:, :], ALU.add).then_inc(S["logits_done"], 1)
                dve.wait_ge(S["n2_copied"], (i + 1) * NB)

        @block.tensor
        def _(pe):
            with pe.Fori(0, NT // NB) as i:
                pe.wait_ge(S["h0_ready"], i + 1)
                for n in range(2):
                    for m in range(KH):
                        for k in range(KH):
                            ins = pe.matmul(bank[2 * n + m][:, 0:PIECE], g_w1[:, k, m * P:(m + 1) * P], aggT[:, k, ds(i * NB_TOK + n * PIECE, PIECE)],
                                            start=(k == 0), stop=(k == KH - 1))
                        ins.then_inc(S["g1_ready"], 1)
                for j in range(NB):
                    pe.wait_ge(S["g1T_ready"], i * 4 + (2 if (j + 1) * P <= PIECE else 4))
                    if j >= 4:
                        pe.wait_ge(S["g2_done"], i * NB + (j - 3))
                    for k in range(KH):
                        ins = pe.matmul(bank[4 + j % 4][:, 0:D], g1T[:, k, j * P:(j + 1) * P], g_w2[:, k, :], start=(k == 0), stop=(k == KH - 1))
                    ins.then_inc(S["g2_ready"], 1)
                pe.wait_ge(S["g2_done"], (i + 1) * NB)
                pe.sem_inc(S["pe_past"], 1)
            with pe.Fori(0, NT // NB) as i:
                for j in range(NB):
                    pe.wait_ge(S["n2_ready"], i * NB + (j + 1))
                    for h in range(KH):
                        ins = pe.transpose(bank[j % 2][:, h * P:(h + 1) * P], xn2[:, j, h * P:(h + 1) * P], ident[:, :])
                    ins.then_inc(S["n2_T"], 1)
                    pe.wait_ge(S["n2T_ready"], i * NB + (j + 1))
                    if j >= 2:
                        pe.wait_ge(S["logits_done"], i * NB + (j - 1))
                    for k in range(KH):
                        ins = pe.matmul(bank[2 + j % 2][:, 0:NE], xn2T[:, j % 2, k, :], gate_w[:, k, :], start=(k == 0), stop=(k == KH - 1))
                    ins.then_inc(S["logit_ready"], 1)
                pe.wait_ge(S["logits_done"], (i + 1) * NB)
                pe.sem_inc(S["pe_past"], 1)

        @block.scalar
        def _(act):
            with act.Fori(0, NT // NB) as i:
                for n in range(2):
                    for m in range(KH):
                        act.wait_ge(S["g1_ready"], i * 4 + (2 * n + m + 1))
                        act.activation(g1T[:, m, n * PIECE:(n + 1) * PIECE], bank[2 * n + m][:, 0:PIECE], ACT.Relu, bias=g_b1[:, m:m + 1]).then_inc(S["g1T_ready"], 1)
            act.wait_ge(S["std2"], 1)
            act.activation(std[:, :], mv[:, :, 1], ACT.Sqrt, bias=epsln[:, 0:1]).then_inc(S["std2"], 1)
            with act.Fori(0, NT // NB) as i:
                for j in range(NB):
                    act.wait_ge(S["n2_T"], i * NB + (j + 1))
                    act.activation(xn2T[:, j % 2, :, :], halves(bank[j % 2][:, 0:D]), ACT.Copy).then_inc(S["n2T_ready"], 1)

        @block.gpsimd
        def _(pool):
            pool.iota(rev[:, :], pattern=[[-1, NE]], base=NE, channel_multiplier=0, allow_small_or_imprecise_dtypes=True).then_inc(S["pool_consts"], 1)
            pool.iota(jt[:, :], pattern=[[1, TT]], base=0, channel_multiplier=0, allow_small_or_imprecise_dtypes=True).then_inc(S["pool_consts"], 1)
            with pool.Fori(0, NT // NB) as i:
                for j in range(NB):
                    pool.wait_ge(S["n2_ready"], i * NB + (j + 1))
                    pool.sem_inc(S["pool_past"], 1)
                    pool.tensor_copy(xf[:, ds(i * NB + j, 1), :].rearrange("p a d -> p (a d)"), xn2[:, j, :]).then_inc(S["n2_copied"], 1)

    per_e = lambda v, n=NT: v.unsqueeze(2).to_broadcast([P, n, NE])
    per_t = lambda v, n=NT: v.unsqueeze(1).to_broadcast([P, n, NE])
    by_e = lambda v: v.rearrange("p (t e) -> p t e", e=NE)

    with nc.Block() as block:

        @block.vector
        def _(dve):
            L = lambda ins: dve_link(dve, ins)
            tt, red = dve.tensor_tensor, dve.tensor_reduce
            L(red(rmax[:, :], logits[:, :, :], AX.X, ALU.max))
            tt(rtmp[:, :, :], logits[:, :, :], per_e(rmax[:, :]), ALU.subtract).then_inc(S["soft"], 1)
            dve.wait_ge(S["soft"], 2)
            L(red(rmax[:, :], probs[:, :, :], AX.X, ALU.add))
            L(dve.reciprocal(rmax[:, :], rmax[:, :]))
            L(tt(probs[:, :, :], probs[:, :, :], per_e(rmax[:, :]), ALU.mult))
            for k in range(2):
                L(red(wts[:, k, :], probs[:, :, :], AX.X, ALU.max))
                L(tt(rtmp[:, :, :], probs[:, :, :], per_e(wts[:, k, :]), ALU.is_equal))
                L(tt(rtmp[:, :, :], rtmp[:, :, :], per_t(rev[:, :]), ALU.mult))
                L(red(rmax[:, :], rtmp[:, :, :], AX.X, ALU.max))
                L(tt(picks[:, k, :, :], per_t(rev[:, :]), per_e(rmax[:, :]), ALU.is_equal))
                if k == 0:
                    L(dve.scalar_tensor_tensor(out=probs[:, :, :], in0=picks[:, 0, :, :], scalar=-2.0, in1=probs[:, :, :], op0=ALU.mult, op1=ALU.add))
            L(tt(chosen[:, :, :], picks[:, 0, :, :], picks[:, 1, :, :], ALU.add))
            tt(chosen[:, :, :], chosen[:, :, :], per_e(valid[:, :]), ALU.mult).then_inc(S["chosen_ready"], 1)
            dve.wait_ge(S["ranks_ready"], 1)
            L(dve.tensor_copy(run_in[:, :, :].rearrange("p e t -> p t e"), by_e(bank[1][:, 0:TN])))
            flat = lambda v: v[:, :, :].rearrange("p e t -> p (e t)")
            L(dve.tensor_tensor_scan(flat(run), flat(run_in), flat(run_in), 0.0, ALU.add, ALU.bypass))
            L(dve.tensor_copy(count[:, 0:1], run[:, 0, NT - 1:NT]))
            L(tt(count[:, 1:NE], run[:, 1:NE, NT - 1], run[:, 0:NE - 1, NT - 1], ALU.subtract))
            L(tt(run_in[:, :, :], run[:, :, :], run_in[:, :, :], ALU.subtract))
            L(tt(shift[:, :], run[:, :, NT - 1], count[:, :], ALU.subtract))
            L(dve.tensor_scalar(count[:, :], count[:, :], float(P - 1), None, ALU.add))
            L(dve.tensor_copy(count_i[:, :], count[:, :]))
            L(dve.tensor_scalar(count_i[:, :], count_i[:, :], 7, None, ALU.logical_shift_right))
            L(dve.tensor_copy(ntile[:, :], count_i[:, :]))
            L(dve.tensor_tensor_scan(until[:, :], ntile[:, :], ntile[:, :], 0.0, ALU.add, ALU.bypass))
            L(tt(ntile[:, :], until[:, :], ntile[:, :], ALU.subtract))
            L(dve.scalar_tensor_tensor(out=shift[:, :], in0=ntile[:, :], scalar=float(P), in1=shift[:, :], op0=ALU.mult, op1=ALU.subtract))
            L(tt(rtmp[:, :, :], by_e(bank[0][:, 0:TN]), run_in[:, :, :].rearrange("p e t -> p t e"), ALU.add))
            L(tt(rtmp[:, :, :], rtmp[:, :, :], per_t(shift[:, :]), ALU.add))
            for k in range(2):
                L(tt(probs[:, :, :], picks[:, k, :, :], rtmp[:, :, :], ALU.mult))
                L(red(slot_f[:, k, :], probs[:, :, :], AX.X, ALU.add))
            dve.tensor_copy(slots[:, :, :], slot_f[:, :, :]).then_inc(S["slots_ready"], 1)
            L(tt(past[:, :, :], jt[:, :].unsqueeze(2).to_broadcast([P, TT, NE - 1]), until[:, 0:NE - 1].unsqueeze(1).to_broadcast([P, TT, NE - 1]), ALU.is_ge))
            L(red(t_exp[:, :], past[:, :, :], AX.X, ALU.add))
            dve.tensor_copy(ti_exp[:, :], t_exp[:, :]).then_inc(S["slots_ready"], 1)

        @block.scalar
        def _(act):
            act.wait_ge(S["soft"], 1)
            act.activation(probs[:, :, :], rtmp[:, :, :], ACT.Exp).then_inc(S["soft"], 1)

        @block.tensor
        def _(pe):
            pe.wait_ge(S["chosen_ready"], 1)
            c = chosen[:, :, :].rearrange("p t e -> p (t e)")
            pe.matmul(bank[0][:, 0:TN], before[:, :], c, start=True, stop=True)
            pe.matmul(bank[1][:, 0:TN], ones[:, :], c, start=True, stop=True).then_inc(S["ranks_ready"], 1)

        @block.gpsimd
        def _(pool):
            pool.wait_ge(S["slots_ready"], 1)
            for t in range(NT):
                n = P if t < NT - 1 else LAST
                for k in range(2):
                    pool.indirect_dma_start(out=lists[:, :], out_offset=bass.IndirectOffsetOnAxis(ap=slots[0:n, k, t:t + 1], axis=0),
                                            in_=xf[0:n, t, :], in_offset=None).then_inc(S["scattered"], 16)
            pool.wait_ge(S["scattered"], 16 * 2 * NT)

    work = aggT[:, :, :].rearrange("p h n -> p (h n)")
    cut = [0]

    def piece(n):
        cut[0] += 2 * n
        return work[:, cut[0] - 2 * n:cut[0]].rearrange("p (b n) -> p b n", b=2)

    xg, xgT, hs, heT, ye = piece(D), piece(D), piece(HE), piece(HE), piece(D)
    STEPS = XT_TILES // 2

    def busy(i, stage):
        return not isinstance(i, int) or 0 <= i - stage < STEPS

    def expert_pass(eng, step):
        for i in range(3):
            step(i)
        with eng.Fori(3, STEPS) as i:
            step(i)
        for i in range(STEPS, STEPS + 3):
            step(i)

    def experts_of(engine, i):
        return load_values(engine, ti_exp[0:1, ds(i * 2, 2)], NE - 1, "a count of NE - 1 comparisons")

    with nc.Block() as block:

        @block.sync
        def _(sp):
            for b in range(2):
                sp.dma_start(xg[:, b, :], lists[b * P:(b + 1) * P, :]).then_inc(xg_loaded[b], 16)

            def step(i):
                if busy(i, 3):
                    for b in range(2):
                        sp.wait_ge(S["y_ready"], (i - 3) * 2 + (b + 1))
                        sp.sem_inc(S["sp_past"], 1)
                        sp.dma_start(results[ds((i - 3) * (2 * P) + b * P, P), :], ye[:, b, :]).then_inc(y_stored[b], 16)
                if not isinstance(i, int) or i < STEPS - 1:
                    for b in range(2):
                        sp.wait_ge(S["xg_T"], i * 2 + (b + 1))
                        sp.sem_inc(S["sp_past"], 1)
                        sp.dma_start(xg[:, b, :], lists[ds(i * (2 * P) + (2 + b) * P, P), :]).then_inc(xg_loaded[b], 16)

            for i in range(3):
                step(i)
            with sp.Fori(3, STEPS - 1) as i:
                step(i)
            for i in range(STEPS - 1, STEPS + 3):
                step(i)
            for b in range(2):
                sp.wait_ge(y_stored[b], 16 * STEPS)

        @block.tensor
        def _(pe):
            def step(i):
                if busy(i, 3):
                    e = experts_of(mybir.EngineType.PE, i - 3)
                    for b in range(2):
                        pe.wait_ge(S["gelu_ready"], (i - 3) * 2 + (b + 1))
                        pe.wait_ge(S["ye_free"], (i - 3) * 2 + (b + 1))
                        for c in range(HC):
                            ins = pe.matmul(bank[6 + b][:, 0:D], heT[:, b, c * P:(c + 1) * P], e_w2[:, c, ds(e[b] * D, D)], start=(c == 0), stop=(c == HC - 1))
                        ins.then_inc(S["ye_ready"], 1)
                if busy(i, 2):
                    for b in range(2):
                        pe.wait_ge(S["hs_ready"], (i - 2) * 2 + (b + 1))
                        for c in range(HC):
                            ins = pe.transpose(bank[4 + b][:, c * P:(c + 1) * P], hs[:, b, c * P:(c + 1) * P], ident[:, :])
                        ins.then_inc(S["heT_ready"], 1)
                if busy(i, 1):
                    e = experts_of(mybir.EngineType.PE, i - 1)
                    for b in range(2):
                        pe.wait_ge(S["xgT_ready"], (i - 1) * 2 + (b + 1))
                        for k in range(KH):
                            ins = pe.matmul(bank[2 + b][:, 0:HE], xgT[:, b, k * P:(k + 1) * P], e_w1[:, k, ds(e[b] * HE, HE)], start=(k == 0), stop=(k == KH - 1))
                        ins.then_inc(S["he_ready"], 1)
                if busy(i, 0):
                    for b in range(2):
                        pe.wait_ge(xg_loaded[b], i * 16 + 16)
                        for h in range(KH):
                            ins = pe.transpose(bank[b][:, h * P:(h + 1) * P], xg[:, b, h * P:(h + 1) * P], ident[:, :])
                        ins.then_inc(S["xg_T"], 1)

            expert_pass(pe, step)

        @block.scalar
        def _(act):
            def step(i):
                if busy(i, 2):
                    e = experts_of(mybir.EngineType.Activation, i - 2)
                    for b in range(2):
                        act.wait_ge(S["heT_ready"], (i - 2) * 2 + (b + 1))
                        act.sem_inc(S["act_past"], 1)
                        for c in range(HC):
                            ins = act.activation(heT[:, b, c * P:(c + 1) * P], bank[4 + b][:, c * P:(c + 1) * P], ACT.Gelu, bias=e_b1[:, ds(e[b] * HC + c, 1)])
                        ins.then_inc(S["gelu_ready"], 1)
                if busy(i, 0):
                    for b in range(2):
                        act.wait_ge(S["xg_T"], i * 2 + (b + 1))
                        act.activation(xgT[:, b, :], bank[b][:, 0:D], ACT.Copy).then_inc(S["xgT_ready"], 1)

            expert_pass(act, step)

        @block.vector
        def _(dve):
            def step(i):
                if busy(i, 3):
                    e = experts_of(mybir.EngineType.DVE, i - 3)
                    for b in range(2):
                        if not isinstance(i, int) or i > 3:
                            dve.wait_ge(y_stored[b], (i - 3) * 16)
                        dve.wait_ge(S["ye_ready"], (i - 3) * 2 + (b + 1))
                        dve.sem_inc(S["dve_past"], 1)
                        dve.tensor_tensor(ye[:, b, :], bank[6 + b][:, 0:D], e_b2[:, ds(e[b] * D, D)], ALU.add).then_inc(S["y_ready"], 1)
                        dve.wait_ge(S["y_ready"], (i - 3) * 2 + (b + 1))
                        dve.sem_inc(S["ye_free"], 1)
                if busy(i, 1):
                    for b in range(2):
                        dve.wait_ge(S["he_ready"], (i - 1) * 2 + (b + 1))
                        dve.tensor_copy(hs[:, b, :], bank[2 + b][:, 0:HE]).then_inc(S["hs_ready"], 1)

            dve.sem_inc(S["ye_free"], 2)
            for i in range(3):
                step(i)
            step(3)
            with dve.Fori(4, STEPS) as i:
                step(i)
            for i in range(STEPS, STEPS + 3):
                step(i)

    NC = 6
    cflat = work[:, 0:3 * NC * D].rearrange("p (k j d) -> p k j d", k=3, j=NC)
    y_in, o_t = cflat[:, 0:2], cflat[:, 2]
    cidx = sb("cidx", [P, 2, NC], I32)
    for n in ("cidx_ready", "o_ready", "o_stored", "comb"):
        S[n] = sem(n)
    y_got = [sem(f"y_got{j}") for j in range(NC)]
    assert (NT - 1) % NC == 0

    with nc.Block() as block:

        @block.gpsimd
        def _(pool):
            pool.sem_inc(S["comb"], NC)
            with pool.Fori(0, (NT - 1) // NC) as i:
                pool.wait_ge(S["comb"], (i + 1) * NC)
                pool.sem_inc(S["pool_past"], 1)
                pool.tensor_copy(cidx[:, :, :], slots[:, :, ds(i * NC, NC)]).then_inc(S["cidx_ready"], 1)
                pool.wait_ge(S["cidx_ready"], i + 1)
                pool.sem_inc(S["pool_past"], 1)
                for j in range(NC):
                    for k in range(2):
                        pool.indirect_dma_start(out=y_in[:, k, j, :], out_offset=None, in_=results[:, :],
                                                in_offset=bass.IndirectOffsetOnAxis(ap=cidx[:, k, j:j + 1], axis=0)).then_inc(y_got[j], 16)
            pool.wait_ge(S["comb"], NT - 1 + NC)
            for k in range(2):
                pool.indirect_dma_start(out=y_in[0:LAST, k, 0, :], out_offset=None, in_=results[:, :],
                                        in_offset=bass.IndirectOffsetOnAxis(ap=slots[0:LAST, k, NT - 1:NT], axis=0)).then_inc(y_got[0], 16)

        @block.vector
        def _(dve):
            def combine(n, j, res, w, out_):
                dve_link(dve, dve.scalar_tensor_tensor(out=y_in[0:n, 0, j, :], in0=y_in[0:n, 0, j, :], scalar=w[0], in1=res, op0=ALU.mult, op1=ALU.add))
                dve.scalar_tensor_tensor(out=out_, in0=y_in[0:n, 1, j, :], scalar=w[1], in1=y_in[0:n, 0, j, :], op0=ALU.mult, op1=ALU.add).then_inc(S["o_ready"], 1)

            with dve.Fori(0, (NT - 1) // NC) as i:
                dve_steps.enter(i, NC)
                for j in range(NC):
                    t = i * NC + j
                    dve.wait_ge(y_got[j], i * 32 + 32)
                    combine(P, j, xres[:, ds(t, 1), :].rearrange("p a d -> p (a d)"), [wts[:, k, ds(t, 1)] for k in range(2)], o_t[:, j, :])
                    dve.wait_ge(S["o_ready"], i * NC + (j + 1))
                    dve.sem_inc(S["comb"], 1)
                dve.wait_ge(S["o_stored"], (i + 1) * (16 * NC))
            dve_steps.leave((NT - 1) // NC)
            dve.wait_ge(y_got[0], 32 * ((NT - 1) // NC + 1))
            combine(LAST, 0, xres[0:LAST, NT - 1, :], [wts[0:LAST, k, NT - 1:NT] for k in range(2)], o_t[0:LAST, 0, :])

        @block.sync
        def _(sp):
            with sp.Fori(0, (NT - 1) // NC) as i:
                for j in range(NC):
                    sp.wait_ge(S["o_ready"], i * NC + (j + 1))
                    sp.sem_inc(S["sp_past"], 1)
                    sp.dma_start(out[ds(i * (NC * P) + j * P, P), :], o_t[:, j, :]).then_inc(S["o_stored"], 16)
            sp.wait_ge(S["o_ready"], NT)
            sp.dma_start(out[(NT - 1) * P:N, :], o_t[0:LAST, 0, :]).then_inc(S["o_stored"], 16)
            sp.wait_ge(S["o_stored"], 16 * NT)

    ctx.close()


_OUTS = [((3125, 256), "float32")]


def kernel(**inputs):
    import numpy as _np
    import concourse.bacc as _bacc
    from concourse.bass_utils import run_bass_kernel_spmd as _run

    nc = _bacc.Bacc("TRN2", target_bir_lowering=False, num_devices=1)
    arrays, args = {}, {}
    for name, value in inputs.items():
        v = _np.ascontiguousarray(value)
        arrays[f"in_{name}"] = v
        args[name] = nc.dram_tensor(f"in_{name}", v.shape, mybir.dt.from_np(v.dtype), kind="ExternalInput").ap()
    shape, dtype = _OUTS[0]
    out = nc.dram_tensor("out_0", shape, mybir.dt.from_np(_np.dtype(dtype)), kind="ExternalOutput").ap()
    graph_layer(nc, args, out)
    r = _run(nc, [arrays], core_ids=[0])
    return r.results[0]["out_0"]
```

```python
from contextlib import ExitStack

import concourse.bass as bass
from concourse import mybir

F32 = mybir.dt.float32
I32 = mybir.dt.int32
F32R = mybir.dt.float32r
ALU = mybir.AluOpType
ACT = mybir.ActivationFunctionType
AX = mybir.AxisListType

P = 128
WIN = 64
WIDE = 400
LN_EPS = 1e-5
ATT_EPS = 1e-6


class Steps:

    def __init__(self, sem):
        self.sem, self.before, self.here, self.loop = sem, 0, 0, 0

    def enter(self, i, per):
        self.before, self.here, self.loop, self.per = self.before + self.here, 0, i * per, per

    def leave(self, n):
        assert self.here == self.per, (self.here, self.per)
        self.before, self.here, self.loop = self.before + n * self.per, 0, 0

    def mark(self, ins):
        ins.then_inc(self.sem, 1)
        self.here += 1
        return self.loop + (self.before + self.here)


def graph_layer(nc, a, out):
    N, D = a["x"].shape
    E = a["src"].shape[0]
    NT = -(-N // P)
    NP = NT * P
    LAST = N - (NT - 1) * P
    KH = D // P
    EW = 2 * P
    GROUPS = -(-E // EW)
    NB = 5
    STAGES = 5
    GA, GM = 2, 5
    MORE = GROUPS - NT * GA - (NT + STAGES - 1) * GM
    SLOTS = 2 * NB * GA
    GFULL, GREST = E // EW, E % EW
    GB = GFULL - P
    assert KH == 2 and 0 < GB < P and GREST and 0 <= MORE <= 1
    H1 = a["L0_mix_W1"].shape[1]
    NE, _, HE = a["L0_ffn_W1"].shape
    HC = HE // P
    HEADS = 8
    DH = D // HEADS
    PAIRS = 2 * N
    XT_TILES = (PAIRS + NE * (P - 1)) // P
    XT_TILES += XT_TILES % 2

    ctx = ExitStack()
    sb = lambda n, s, d=F32: ctx.enter_context(nc.sbuf_tensor(n, s, d))
    sem = lambda n: ctx.enter_context(nc.semaphore(n))
    bank = [ctx.enter_context(nc.psum_tensor(f"bank{i}", [P, 512], F32)) for i in range(8)]
    ds = bass.ds

    xn_rows = nc.dram_tensor("xn_rows", [NP, D], F32, kind="Internal").ap()
    xn2_rows = nc.dram_tensor("xn2_rows", [NP, D], F32, kind="Internal").ap()
    results = nc.dram_tensor("expert_results", [2 * NP + XT_TILES * P, D], F32, kind="Internal").ap()

    SIZES = dict(mix_w=KH * 5 * D + 2 * KH * H1 + H1 // P * D + KH * D, spare=8 * D, xT=KH * NP, aggT=KH * NP, e_w1=KH * NE * HE, q_w2=NE * HC * D)
    with ExitStack() as whole:
        flat = {n: whole.enter_context(nc.sbuf_tensor(n, [P, size], F32)) for n, size in SIZES.items()}
    parts = {n: sb(n + "_parts", [P, size]) for n, size in SIZES.items()}

    mix_w = flat["mix_w"]
    placed = [0]

    def weight(k, n):
        placed[0] += k * n
        return mix_w[:, placed[0] - k * n:placed[0]].rearrange("p (k n) -> p k n", k=k)

    w_kv, w_q, w_m, w_1, w_2 = weight(KH, 2 * D), weight(KH, D), weight(KH, D), weight(2 * KH, H1), weight(H1 // P, D)
    g_w1, g_w2 = weight(KH, D), weight(KH, D)
    gate_w = sb("gate_w", [P, KH, NE])
    g_b1 = sb("g_b1", [P, KH]); m_g1 = sb("m_g1", [P, KH]); m_b1 = sb("m_b1", [P, KH])
    eps1 = sb("eps1", [P, 1])
    row_g2 = sb("row_g2", [P, D]); row_b2 = sb("row_b2", [P, D]); row_gb2 = sb("row_gb2", [P, D])
    gate_b = sb("gate_b_rows", [P, NE])
    e_w1 = flat["e_w1"][:, :].rearrange("p (k n) -> p k n", k=KH)
    e_b1 = sb("e_b1", [P, NE * HC]); e_b2 = sb("e_b2", [P, NE * D])

    xres = sb("xres", [P, NT, D])
    xT = flat["xT"][:, :].rearrange("p (h n) -> p h n", h=KH)
    aggT = flat["aggT"][:, :].rearrange("p (h n) -> p h n", h=KH)
    q_w2 = flat["q_w2"]
    qT = q_w2[:, 0:KH * NP].rearrange("p (h n) -> p h n", h=KH)
    e_w2 = q_w2[:, :].rearrange("p (c n) -> p c n", c=HC)

    ident = sb("ident", [P, P]); before = sb("before", [P, P]); ones = sb("ones", [P, P])
    heads = sb("heads", [P, P]); iota_w = sb("iota_w", [P, WIDE]); valid = sb("valid", [P, NT])
    epsln = sb("epsln", [P, 1]); epsatt = sb("epsatt", [P, 1])

    early = e_w1[:, :, :].rearrange("p k n -> p (k n)")
    r_int = early[:, 0:4 * EW].bitcast(I32).rearrange("p (a b e) -> p a b e", a=2, b=2)
    r_f = early[:, 4 * EW:10 * EW].rearrange("p (a b e) -> p a b e", a=3, b=2)
    r_dst = early[:, 10 * EW:12 * EW].rearrange("p (b e) -> p b e", b=2)
    r_stat = sb("r_stat", [P, 2, 2])
    c_loc = sb("c_loc", [P, 2, GROUPS]); c_w = sb("c_w", [P, 2, GROUPS])
    c_dst = sb("c_dst", [P, 2, GROUPS]); c_src = sb("c_src", [P, 2, GROUPS], I32)
    RROW, MROW = -(-NB * GA // 4) * 4, -(-(GM + MORE) // 4) * 4
    base_a = sb("base_a", [1, NT // NB * RROW], I32); base_m = sb("base_m", [1, (NT + STAGES - 1) * MROW], I32)
    far = sb("far", [1, 4]); flag = sb("flag", [1, 1], I32)
    idx = sb("idx", [P, SLOTS], I32)
    spare = flat["spare"]
    gath = [early[:, s * D:(s + 1) * D] for s in range(12 * EW // D)] + [spare[:, s * D:(s + 1) * D] for s in range(8)]
    assert len(gath) == SLOTS

    xs = [early[:, 12 * EW + b * NB * D:12 * EW + (b + 1) * NB * D].rearrange("p (j d) -> p j d", j=NB) for b in range(2)]
    onehot = early[:, 12 * EW:12 * EW + SLOTS * WIN].rearrange("p (s n) -> p s n", n=WIN)
    assert SLOTS * WIN <= NB * D
    r_tmp = early[:, 12 * EW + 2 * NB * D:14 * EW + 2 * NB * D].rearrange("p (b e) -> p b e", b=2)
    stats = sb("stats", [P, NT, 6]); mv = sb("mv", [P, NT, 2])
    std = sb("std", [P, NT]); rstd = sb("rstd", [P, NT])
    space = [12 * EW + NB * D]

    def carve(n):
        space[0] += n
        assert space[0] <= KH * NE * HE
        return early[:, space[0] - n:space[0]]

    halves = lambda t: t.rearrange("p (h n) -> p h n", h=KH)
    xTs0 = halves(carve(D)); kqe = carve(2 * D)
    first = space[0]
    k_t = carve(D); carve(D + 1)
    ks_bd = halves(carve(D))
    second = space[0]
    den = carve(D); mT = halves(carve(D)); z1 = carve(D)
    mzT = halves(carve(D)); hT = carve(H1).rearrange("p (h n) -> p h n", n=P); z2 = carve(D)
    x_t = [early[:, o:o + D + 1] for o in (first + D, second, second + 2 * D)]
    X_T = (0, 1, 2, 0, 1)
    kvm = early[:, first:first + KH * D].rearrange("p (m n) -> p m n", m=KH)
    xTs = [xTs0, hT[:, 0:KH, :]]
    kx = hT[:, :, :].rearrange("p o n -> p (o n)"); kxT = kqe; kvT = halves(z2)
    ks = sb("ks", [P, KH]); b2sum = sb("b2sum", [P, D])
    st2 = sb("st2", [P, 2, 6]); mv2 = sb("mv2", [P, 2, 2]); sd2 = sb("sd2", [P, 2]); rs2 = sb("rs2", [P, 2])
    LINKS = 6

    S = {n: sem(n) for n in (
        "loaded", "edges_loaded", "pads", "consts", "masks", "dve", "edge_rows", "edge_cols", "edge_done",
        "ln_std", "res_done", "sp_past", "xs_ready", "xs_T", "xT_done",
        "xTs_ready", "pe_kq", "kq_min", "kq_exp", "kq_ready", "marked", "kx_acc", "kx_taken", "kx_T", "kxT_ready", "kvT_sum", "kvT_ready", "kvm_sum", "kvm_ready", "den_sum", "den_ready",
        "onehots", "win_ready", "win_added", "idx_ready", "pool_past", "dve_past", "act_past", "pe_past",
        "bd_ready", "mT_ready", "m_ready", "mv_ready", "sd_ready", "z1_ready", "zT_ready",
        "mzT_ready", "h_ready", "hT_ready", "m2_ready", "mv2_ready", "sd2_ready", "m2_free", "kv_zero")}
    gath_done = [sem(f"gath_done{s}") for s in range(SLOTS)]
    dve_steps = Steps(S["dve"])

    def dve_link(eng, ins):
        eng.wait_ge(S["dve"], dve_steps.mark(ins))

    def load_values(engine, cells, most, why):
        _, values = nc.values_load_multi_w_load_instructions(cells, engines=[engine], min_val=0, max_val=most, skip_runtime_bounds_check_because=why)
        return values

    rows = lambda w: w.rearrange("(c p) n -> p c n", p=P)
    cols = lambda v: v.rearrange("(c p) -> p c", p=P)
    spread = lambda v: v.partition_broadcast(P)

    CHUNKS = NT // NB
    T_BANKS = (bank[0], bank[1], bank[7])
    x_loaded = [sem(f"x_loaded{c}") for c in range(CHUNKS)]
    xn_store = [sem(f"xn_store{b}") for b in range(2)]

    def chunks(eng, chunk):
        with eng.Fori(0, CHUNKS // 2) as g:
            for b in range(2):
                chunk(g * 2 + b, b)
        chunk(CHUNKS - 1, 0)

    with nc.Block() as block:

        @block.sync
        def _(sp):
            for c in range(CHUNKS):
                lo, hi = c * NB, min((c + 1) * NB, NT - 1)
                sp.dma_start(xres[:, lo:hi, :], a["x"][lo * P:hi * P, :].rearrange("(t p) d -> p t d", p=P)).then_inc(x_loaded[c], 16)
            sp.wait_ge(S["pads"], 5)
            sp.dma_start(xres[0:LAST, NT - 1, :], a["x"][(NT - 1) * P:N, :]).then_inc(x_loaded[CHUNKS - 1], 16)
            weights = ((w_kv[:, :, 0:D], rows(a["L0_mix_Wk"])), (w_kv[:, :, D:2 * D], rows(a["L0_mix_Wv"])), (w_q[:, :, :], rows(a["L0_mix_Wq"])),
                       (w_m[:, :, :], rows(a["L0_mix_Wm"])), (w_1[:, :, :], rows(a["L0_mix_W1"])), (w_2[:, :, :], rows(a["L0_mix_W2"])),
                       (g_w1[:, :, :], rows(a["L0_gnn_w1"])), (g_w2[:, :, :], rows(a["L0_gnn_w2"])), (gate_w[:, :, :], rows(a["L0_ffn_gate_w"])),
                       (g_b1[:, :], cols(a["L0_gnn_b1"])), (m_g1[:, :], cols(a["L0_mix_g1"])), (m_b1[:, :], cols(a["L0_mix_b1"])),
                       (eps1[:, :], spread(a["L0_gnn_eps"])),
                       (row_g2[:, :], spread(a["L0_mix_g2"])), (row_b2[:, :], spread(a["L0_mix_b2"])), (row_gb2[:, :], spread(a["L0_gnn_b2"])),
                       (gate_b[:, :], spread(a["L0_ffn_gate_b"])))
            for t, v in weights:
                sp.dma_start(t, v, allow_slow_non_contiguous=True).then_inc(S["loaded"], 16)

            def chunk(c, b):
                sp.wait_ge(S["xs_ready"], c + 1)
                sp.sem_inc(S["sp_past"], 1)
                sp.dma_start(xn_rows[ds(c * (NB * P), NB * P), :].rearrange("(j p) d -> p j d", p=P), xs[b][:, :, :]).then_inc(xn_store[b], 16)

            chunks(sp, chunk)
            sp.wait_ge(S["loaded"], 16 * len(weights))
            for b in range(2):
                sp.wait_ge(xn_store[b], 16 * (1 + (CHUNKS + 1 - b) // 2))

        @block.gpsimd
        def _(pool):
            pool.memset(r_int[:, 0, 1, :], N).then_inc(S["pads"], 1)
            pool.memset(r_int[:, 1, 1, :], 0).then_inc(S["pads"], 1)
            pool.memset(r_f[:, 1, 1, :], 0.0).then_inc(S["pads"], 1)
            pool.memset(xres[:, NT - 1, :], 0.0).then_inc(S["pads"], 1)
            pool.memset(epsln[:, :], LN_EPS).then_inc(S["pads"], 1)
            pool.memset(epsatt[:, :], ATT_EPS)
            pool.memset(ident[:, :], 0.0)
            for m in (before, ones, heads, valid):
                pool.memset(m[:, :], 1.0)
            pool.iota(iota_w[:, :], pattern=[[1, WIDE]], base=0, channel_multiplier=0,
                      allow_small_or_imprecise_dtypes=True).then_inc(S["consts"], 1)
            pool.wait_ge(S["consts"], 1)
            pool.affine_select(out=ident[:, :], in_=ident[:, :], compare_op=ALU.not_equal, fill=1.0, base=0,
                               pattern=[[-1, P]], channel_multiplier=1).then_inc(S["masks"], 1)
            pool.affine_select(out=before[:, :], in_=before[:, :], compare_op=ALU.is_gt, fill=0.0, base=0,
                               pattern=[[1, P]], channel_multiplier=-1).then_inc(S["masks"], 1)
            pool.affine_select(out=valid[:, :], in_=valid[:, :], compare_op=ALU.is_gt, fill=0.0, base=N,
                               pattern=[[-P, NT]], channel_multiplier=-1).then_inc(S["masks"], 1)
            hv = heads[:, :].rearrange("p (b c) -> p b c", c=DH)
            pool.affine_select(out=hv, in_=hv, compare_op=ALU.is_ge, fill=0.0, base=0,
                               pattern=[[-DH, P // DH], [0, DH]], channel_multiplier=1).then_inc(S["masks"], 1)
            pool.wait_ge(S["masks"], 4)
            pool.affine_select(out=hv, in_=hv, compare_op=ALU.is_ge, fill=0.0, base=DH - 1,
                               pattern=[[DH, P // DH], [0, DH]], channel_multiplier=-1).then_inc(S["masks"], 1)
            pool.memset(aggT[:, :, :], 0.0)
            pool.sem_inc(S["res_done"], 2)

            def chunk(c, b):
                pool.wait_ge(S["xs_ready"], c + 1)
                pool.sem_inc(S["pool_past"], 1)
                v = xres[:, ds(c * NB, NB), :]
                pool.tensor_tensor(v, v, xs[b], ALU.add).then_inc(S["res_done"], 1)

            chunks(pool, chunk)

        @block.scalar
        def _(act):
            act.wait_ge(S["pads"], 5)
            d_rows = [v[0:GFULL * EW].rearrange("(g e) -> g e", e=EW) for v in (a["dst"], a["src"], a["edge_weight"])]
            tails = [v[GFULL * EW:E].rearrange("(a e) -> a e", a=1) for v in (a["dst"], a["src"], a["edge_weight"])]
            for j in range(3):
                t = r_int[:, j] if j < 2 else r_f[:, 1]
                act.dma_start(t[:, 0, :], d_rows[j][0:P, :]).then_inc(S["edges_loaded"], 16)
                act.dma_start(t[0:GB, 1, :], d_rows[j][P:GFULL, :]).then_inc(S["edges_loaded"], 16)
                act.dma_start(t[GB:GB + 1, 1, 0:GREST], tails[j]).then_inc(S["edges_loaded"], 16)
            act.activation(sd2[:, 0:1], epsln[:, :], ACT.Sqrt, bias=epsln[:, 0:1])
            act.wait_ge(S["ln_std"], 1)
            act.activation(std[:, :], mv[:, :, 1], ACT.Sqrt, bias=epsln[:, 0:1]).then_inc(S["ln_std"], 1)

            def chunk(c, b):
                for j in range(NB):
                    act.wait_ge(S["xs_T"], c * NB + (2 * NB + j + 1))
                    act.sem_inc(S["act_past"], 1)
                    act.activation(xT[:, :, ds(c * (NB * P) + j * P, P)], halves(T_BANKS[j % 3][:, 0:D]), ACT.Copy).then_inc(S["xT_done"], 1)

            chunks(act, chunk)

        @block.vector
        def _(dve):
            for c in range(CHUNKS):
                dve.wait_ge(x_loaded[c], 32 if c == CHUNKS - 1 else 16)
                for t in range(c * NB, (c + 1) * NB):
                    ins = dve.bn_stats(stats[:, t, :], xres[:, t, :])
            dve_link(dve, ins)
            for t in range(NT):
                ins = dve.bn_aggr(mv[:, t, :], stats[:, t, :])
            ins.then_inc(S["ln_std"], 1)
            dve.wait_ge(S["ln_std"], 2)
            dve_link(dve, dve.reciprocal(rstd[:, :], std[:, :]))
            for b in range(2):
                dve.sem_inc(xn_store[b], 16)

            def chunk(c, b):
                dve.wait_ge(xn_store[b], (c - b) * 8 + 16)
                dve.wait_ge(S["xs_T"], c * NB + NB)
                dve.wait_ge(S["res_done"], c + 1)
                for j in range(NB):
                    t = c * NB + j
                    ins = dve.tensor_scalar(xs[b][:, j, :], xres[:, ds(t, 1), :].rearrange("p a d -> p (a d)"), mv[:, ds(t, 1), 0:1].rearrange("p a d -> p (a d)"),
                                            rstd[:, ds(t, 1)], ALU.subtract, ALU.mult)
                ins.then_inc(S["xs_ready"], 1)

            for c in range(2):
                chunk(c, c)
            dve.wait_ge(S["edges_loaded"], 144)
            dve_link(dve, dve.tensor_copy(r_dst[:, :, :], r_int[:, 0, :, :]))
            dve.tensor_copy(r_f[:, 2, :, :], r_int[:, 1, :, :])
            dve_link(dve, dve.tensor_reduce(r_stat[:, 0, :], r_dst[:, :, :], AX.X, ALU.min))
            for b in range(2):
                ins = dve.tensor_scalar(r_f[:, 0, b, :], r_dst[:, b, :], r_stat[:, 0, b:b + 1], None, ALU.subtract)
            dve_link(dve, ins)
            dve_link(dve, dve.scalar_tensor_tensor(out=r_tmp[:, :, :], in0=r_dst[:, :, :], scalar=float(N), in1=r_f[:, 0, :, :],
                                                   op0=ALU.is_lt, op1=ALU.mult))
            dve_link(dve, dve.tensor_reduce(r_stat[:, 1, :], r_tmp[:, :, :], AX.X, ALU.max))
            dve.sem_inc(S["edge_rows"], 1)
            for c in range(2, CHUNKS):
                chunk(c, c % 2)
            for n, dst in enumerate((c_loc, c_w, c_src, c_dst)):
                dve.wait_ge(S["edge_cols"], n + 1)
                ps = bank[2 + n][:, :].rearrange("p (h g) -> p h g", h=2)
                dve.tensor_copy(dst[:, :, 0:GROUPS], ps[:, :, 0:GROUPS]).then_inc(S["edge_done"], 1)
            dve.wait_ge(S["edge_cols"], 5)
            dve.tensor_copy(base_a[:, :].rearrange("p (i g) -> p i g", g=RROW)[:, :, 0:NB * GA],
                            bank[6][0:1, 0:NT * GA].rearrange("p (i g) -> p i g", g=NB * GA))
            dve.tensor_copy(base_m[:, 0:GM + MORE], bank[6][0:1, NT * GA:NT * GA + GM + MORE])
            dve.tensor_copy(base_m[:, MROW:].rearrange("p (i g) -> p i g", g=MROW)[:, :, 0:GM],
                            bank[6][0:1, NT * GA + GM + MORE:GROUPS].rearrange("p (i g) -> p i g", g=GM)).then_inc(S["edge_done"], 1)
            dve_link(dve, dve.tensor_reduce(far[:, 0:1], bank[6][0:1, 2 * P:4 * P], AX.X, ALU.max))
            dve.tensor_scalar(flag[:, :], far[:, 0:1], float(WIN), None, ALU.is_ge).then_inc(S["edge_done"], 1)

        @block.tensor
        def _(pe):
            pe.wait_ge(S["masks"], 1)
            pe.sem_inc(S["xs_T"], 2 * NB)

            def chunk(c, b):
                pe.wait_ge(S["xs_ready"], c + 1)
                for j in range(NB):
                    pe.wait_ge(S["xT_done"], c * NB + (j + 1))
                    for h in range(KH):
                        ins = pe.transpose(T_BANKS[j % 3][:, h * P:(h + 1) * P], xs[b][:, j, h * P:(h + 1) * P], ident[:, :])
                    ins.then_inc(S["xs_T"], 1)

            pe.sem_inc(S["xT_done"], 2)
            for c in range(2):
                chunk(c, c)
            pe.wait_ge(S["edge_rows"], 1)
            for n in range(4):
                for h in range(2):
                    for b in range(2):
                        t = r_f[:, n, b, h * P:(h + 1) * P] if n < 3 else r_dst[:, b, h * P:(h + 1) * P]
                        ins = pe.transpose(bank[2 + n][:, h * 256 + b * P:h * 256 + (b + 1) * P], t, ident[:, :])
                ins.then_inc(S["edge_cols"], 1)
            for s in range(2):
                for b in range(2):
                    ins = pe.matmul(bank[6][0:1, s * 256 + b * P:s * 256 + (b + 1) * P], r_stat[:, s, b:b + 1], ident[:, :], start=True, stop=True)
            ins.then_inc(S["edge_cols"], 1)
            for c in range(2, CHUNKS):
                chunk(c, c % 2)

    RING = NB * GA
    ps_kq, ps_kx = [bank[0], bank[1]], [bank[2], bank[5]]
    ps_kxT, ps_kvT, ps_kvm = bank[6], bank[7], bank[1]
    ps_win = [bank[3], bank[4]]
    ps_win2 = [bank[3], bank[4], bank[2], bank[3], bank[4], bank[2]]
    ps_nd, ps_m, ps_hid, ps_zT, ps_m2 = bank[0], bank[1], bank[5], bank[6], bank[7]
    LAST_STEP = NT + STAGES - 2

    def groups_at(i):
        return GM + (MORE if isinstance(i, int) and i == 0 else 0)

    def first_group(i):
        return NT * GA if isinstance(i, int) and i == 0 else i * GM + (NT * GA + MORE)

    def active(i, stage):
        return not isinstance(i, int) or 0 <= i - stage < NT

    def second_pass(eng, step, around=None):
        for i in range(STAGES - 1):
            step(i)
        with eng.Fori(STAGES - 1, NT) as i:
            if around:
                around.enter(i - (STAGES - 1), LINKS)
            step(i)
        if around:
            around.leave(NT - (STAGES - 1))
        for i in range(NT, NT + STAGES - 1):
            step(i)

    x_got = [sem(f"x_got{b}") for b in range(3)]

    with nc.Block() as block:

        @block.sync
        def _(sp):
            sp.sem_inc(x_got[1], 16)
            with sp.Fori(0, NT // NB) as i:
                for j in range(NB):
                    t = i * NB + j
                    sp.wait_ge(S["kx_acc"], t + 1)
                    sp.sem_inc(S["sp_past"], 1)
                    sp.dma_start(x_t[X_T[j]][:, 0:D], xn_rows[ds(t * P, P), :]).then_inc(x_got[X_T[j]], 16)
            for b in range(3):
                sp.wait_ge(x_got[b], 16 * ((b == 1) + NT // NB * X_T.count(b)))

        @block.gpsimd
        def _(pool):
            def indices(lo, hi, G):
                pool.tensor_copy(idx[:, 2 * lo:2 * hi].rearrange("p (g h) -> p h g", h=2), c_src[:, :, ds(G, hi - lo)]).then_inc(S["idx_ready"], 1)

            def gathers(slots):
                for s in slots:
                    pool.indirect_dma_start(out=gath[s], out_offset=None, in_=xn_rows[:, :],
                                            in_offset=bass.IndirectOffsetOnAxis(ap=idx[:, s:s + 1], axis=0)).then_inc(gath_done[s], 16)

            def half_step(lo, hi, consumed, copies, prepare):
                pool.wait_ge(S["win_ready"], consumed)
                pool.sem_inc(S["pool_past"], 1)
                pool.wait_ge(S["idx_ready"], copies)
                pool.sem_inc(S["pool_past"], 1)
                gathers(range(2 * lo, 2 * hi - 1))
                if prepare:
                    prepare()
                gathers([2 * hi - 1])

            n = RING // 2
            pool.wait_ge(S["edge_done"], 3)
            indices(0, n, 0)
            with pool.Fori(0, NT // NB) as i:
                for half in range(2):
                    def prepare():
                        pool.wait_ge(S["win_ready"], i * RING + (half + 2) * n)
                        pool.sem_inc(S["pool_past"], 1)
                        indices((1 - half) * n, (2 - half) * n, i * RING + (half + 1) * n)

                    half_step(half * n, (half + 1) * n, i * RING + (half + 1) * n, i * 2 + (half + 1), prepare)

            def step(i):
                cuts = (0, groups_at(i) // 2, groups_at(i))
                for half in range(2):
                    lo, hi = cuts[half:half + 2]
                    before_ = (NT - NB) * GA if isinstance(i, int) and i == 0 else (i - 1) * GM + (NT * GA + MORE)

                    def prepare():
                        to = (cuts[1], cuts[2]) if half == 0 else (0, GM // 2)
                        for s in range(2 * to[0], 2 * to[1]):
                            pool.wait_ge(gath_done[s], i * 16 + 16 * (NT // NB + half))
                        pool.sem_inc(S["pool_past"], 1)
                        indices(*to, first_group(i) + cuts[1] if half == 0 else first_group(i + 1))

                    last = isinstance(i, int) and i == LAST_STEP and half == 1
                    half_step(lo, hi, before_ + (RING + hi), i * 2 + (2 * (NT // NB) + half + 1), None if last else prepare)

            step(0)
            with pool.Fori(1, LAST_STEP) as i:
                step(i)
            step(LAST_STEP)

        @block.tensor
        def _(pe):
            def group(G, place, win, rounds, hots):
                pe.wait_ge(S["win_added"], G + 1)
                for h in range(2):
                    s = 2 * place + h
                    pe.wait_ge(gath_done[s], rounds)
                    pe.wait_ge(S["onehots"], hots + (h + 1))
                    for m in range(KH):
                        ins = pe.matmul(win[:, m * WIN:(m + 1) * WIN], gath[s][:, m * P:(m + 1) * P], onehot[:, s, :],
                                        start=(h == 0 and m == 0), stop=(h == 1), skip_group_check=True)
                ins.then_inc(S["win_ready"], 1)

            def sum_kx(j, tiles, marks):
                b = X_T[j - 1]
                pe.wait_ge(x_got[b], tiles)
                pe.wait_ge(S["marked"], marks)
                for m in range(KH):
                    ins = pe.matmul(ps_kx[m][:, 0:D + 1], k_t[:, m * P:(m + 1) * P], x_t[b], start=False, stop=True, skip_group_check=True)
                ins.then_inc(S["kx_acc"], 1)

            pe.sem_inc(S["win_ready"], RING)
            pe.sem_inc(S["pe_kq"], 2)
            pe.wait_ge(S["kv_zero"], 1)
            for m in range(KH):
                ins = pe.matmul(ps_kx[m][:, 0:D + 1], ident[:, :], kqe[:, 0:D + 1], start=True, stop=True, skip_group_check=True)
            ins.then_inc(S["kx_acc"], 1)
            loads = lambda i, j: i * (16 * X_T.count(X_T[j - 1])) + 16 * ((X_T[j - 1] == 1) + (X_T[:j].count(X_T[j - 1])))
            with pe.Fori(0, NT // NB) as i:
                for j in range(NB):
                    t = i * NB + j
                    beside = lambda g: group(i * RING + (j * GA + g), j * GA + g, ps_win[g], i * 16 + 16, i * (2 * RING) + 2 * (j * GA + g))
                    pe.wait_ge(S["xTs_ready"], t + 1)
                    pe.wait_ge(S["kq_ready"], t + (2 if j == 0 else 1))
                    kq, x = ps_kq[j % 2], xTs[j % 2]
                    for k in range(KH):
                        pe.matmul(kq[:, 0:D], x[:, k, :], w_kv[:, k, 0:D], start=(k == 0), stop=(k == KH - 1))
                    for m in range(KH):
                        for k in range(KH):
                            ins = pe.matmul(kq[:, D + m * P:D + (m + 1) * P], w_q[:, k, m * P:(m + 1) * P], x[:, k, :], start=(k == 0), stop=(k == KH - 1))
                    ins.then_inc(S["pe_kq"], 1)
                    beside(0)
                    pe.wait_ge(S["kq_ready"], t + 2)
                    sum_kx(j, loads(i, j), t + 1)
                    beside(1)
            pe.wait_ge(S["kq_ready"], NT + 2)
            sum_kx(NB, 16 * (1 + NT // NB * X_T.count(1)), NT + 1)

            def transpose_kx():
                pe.wait_ge(S["kx_taken"], 1)
                for m in range(KH):
                    for c in range(KH):
                        ins = pe.transpose(ps_kxT[:, m * D + c * P:m * D + (c + 1) * P], kx[:, m * D + c * P:m * D + (c + 1) * P], ident[:, :])
                ins.then_inc(S["kx_T"], 1)

            def times_wv():
                pe.wait_ge(S["kxT_ready"], 1)
                for m in range(KH):
                    for c in range(KH):
                        ins = pe.matmul(ps_kvT[:, m * P:(m + 1) * P], w_kv[:, c, D + m * P:D + (m + 1) * P], kxT[:, m * D + c * P:m * D + (c + 1) * P],
                                        start=(c == 0), stop=(c == KH - 1))
                ins.then_inc(S["kvT_sum"], 1)

            def times_wm():
                pe.wait_ge(S["kvT_ready"], 1)
                for m in range(KH):
                    ins = pe.matmul(ps_kvm[:, m * D:(m + 1) * D], kvT[:, m, :], w_m[:, m, :], start=True, stop=True)
                ins.then_inc(S["kvm_sum"], 1)

            def step(i):
                def sums(*gs):
                    hots = 2 * NT * GA if isinstance(i, int) and i == 0 else (i - 1) * (2 * GM) + (2 * RING + 2 * NT * GA)
                    for g in gs:
                        group(first_group(i) + g, g, ps_win2[g], i * 16 + 16 * (NT // NB + 1), hots + 2 * g)

                if active(i, 4):
                    pe.wait_ge(S["hT_ready"], i - 3)
                    pe.wait_ge(S["m2_free"], i - 3)
                    for k in range(H1 // P):
                        ins = pe.matmul(ps_m2[:, 0:D], hT[:, k, :], w_2[:, k, :], start=(k == 0), stop=(k == H1 // P - 1))
                    ins.then_inc(S["m2_ready"], 1)
                between = isinstance(i, int) and i == 0
                sums(0)
                if between:
                    transpose_kx()
                if active(i, 3):
                    pe.wait_ge(S["mzT_ready"], i - 2)
                    for o in range(H1 // P):
                        for k in range(2 * KH):
                            rhs = xT[:, k, ds((i - 3) * P, P)] if k < KH else mzT[:, k - KH, :]
                            ins = pe.matmul(ps_hid[:, o * P:(o + 1) * P], w_1[:, k, o * P:(o + 1) * P], rhs, start=(k == 0), stop=(k == 2 * KH - 1))
                    ins.then_inc(S["h_ready"], 1)
                sums(1)
                if active(i, 2):
                    pe.wait_ge(S["z1_ready"], i - 1)
                    for m in range(KH):
                        ins = pe.transpose(ps_zT[:, m * P:(m + 1) * P], z1[:, m * P:(m + 1) * P], ident[:, :])
                    ins.then_inc(S["zT_ready"], 1)
                if between:
                    times_wv()
                sums(2)
                if active(i, 1):
                    pe.wait_ge(S["mT_ready"], i)
                    if isinstance(i, int) and i == 1:
                        pe.wait_ge(S["kvm_ready"], 1)
                    for k in range(KH):
                        ins = pe.matmul(ps_m[:, 0:D], mT[:, k, :], kvm[:, k, :], start=(k == 0), stop=(k == KH - 1))
                    ins.then_inc(S["m_ready"], 1)
                sums(3)
                if active(i, 0):
                    if between:
                        times_wm()
                        pe.wait_ge(S["bd_ready"], 1)
                    for m in range(KH):
                        ins = pe.matmul(ps_nd[:, m * P:(m + 1) * P], ks_bd[:, m, :], qT[:, m, ds(i * P, P)], start=True, stop=True)
                    ins.then_inc(S["den_sum"], 1)
                sums(*range(4, groups_at(i)))

            second_pass(pe, step)

        @block.vector
        def _(dve):
            def build(place, G):
                for h in range(2):
                    dve.tensor_scalar(onehot[:, 2 * place + h, :], iota_w[:, 0:WIN], c_loc[:, h, ds(G, 1)], c_w[:, h, ds(G, 1)],
                                      ALU.is_equal, ALU.mult).then_inc(S["onehots"], 1)

            def add(G, win, first, place=None, ahead=None):
                dve.wait_ge(S["win_ready"], G + (RING + 1))
                dve.sem_inc(S["dve_past"], 1)
                v = aggT[:, :, ds(first, WIN)]
                dve.tensor_tensor(v, v, win[:, 0:KH * WIN].rearrange("p (h n) -> p h n", h=KH), ALU.add).then_inc(S["win_added"], 1)
                if place is not None:
                    build(place, G + ahead)
                dve.wait_ge(S["win_added"], G + 3)


            dve.memset(kqe[:, :], 0.0)
            dve.memset(k_t[:, :], 0.0)
            dve.memset(x_t[X_T[-1]], 0.0).then_inc(S["kv_zero"], 1)
            for n in ("win_added", "kq_ready"):
                dve.sem_inc(S[n], 2)
            dve.wait_ge(S["edge_done"], 5)
            for g in range(RING):
                build(g, g)
            with dve.Fori(0, NT // NB) as i:
                r = load_values(mybir.EngineType.DVE, base_a[0:1, ds(i * RROW, RING)], N, "a group's first node is a dst, or N where the group is padding")
                for j in range(NB):
                    t = i * NB + j
                    G = i * RING + j * GA
                    dve.wait_ge(S["kx_acc"], t + 1)
                    dve.wait_ge(S["kq_ready"], t + 2)
                    dve.wait_ge(S["pe_kq"], t + 3)
                    dve.tensor_scalar(kqe[:, :], ps_kq[j % 2][:, :], 0.0, None, ALU.min).then_inc(S["kq_min"], 1)
                    add(G, ps_win[0], r[j * GA], j * GA, RING)
                    dve.wait_ge(S["kq_exp"], t + 1)
                    dve.wait_ge(S["kx_acc"], t + 2)
                    dve.scalar_tensor_tensor(out=k_t[:, :], in0=ps_kq[j % 2][:, 0:D], scalar=0.0, in1=kqe[:, 0:D], op0=ALU.max, op1=ALU.add)
                    dve.scalar_tensor_tensor(out=qT[:, :, ds(t * P, P)], in0=halves(ps_kq[j % 2][:, D:2 * D]), scalar=0.0, in1=halves(kqe[:, D:2 * D]),
                                             op0=ALU.max, op1=ALU.add).then_inc(S["kq_ready"], 1)
                    add(G + 1, ps_win[1], r[j * GA + 1], j * GA + 1, RING)
            dve.wait_ge(S["kx_acc"], NT + 2)
            for m in range(KH):
                dve.tensor_copy(kx[:, m * D:(m + 1) * D], ps_kx[m][:, 0:D])
                ins = dve.tensor_copy(ks[:, m:m + 1], ps_kx[m][:, D:D + 1])
            dve_link(dve, ins)
            dve.sem_inc(S["kx_taken"], 1)
            for m in range(KH):
                ins = dve.tensor_scalar(ks_bd[:, m, :], heads[:, :], ks[:, m:m + 1], None, ALU.mult)
            ins.then_inc(S["bd_ready"], 1)
            dve.sem_inc(S["m2_free"], 1)

            def copy_kxT():
                dve.wait_ge(S["kx_T"], 1)
                dve.tensor_copy(kxT[:, :], ps_kxT[:, :]).then_inc(S["kxT_ready"], 1)

            def diagonal():
                dve.wait_ge(S["kvT_sum"], 1)
                for m in range(KH):
                    ins = dve.scalar_tensor_tensor(out=kvT[:, m, :], in0=heads[:, :], scalar=1.0 / N, in1=ps_kvT[:, m * P:(m + 1) * P], op0=ALU.mult, op1=ALU.mult)
                ins.then_inc(S["kvT_ready"], 1)

            def copy_kvm():
                dve.wait_ge(S["kvm_sum"], 1)
                dve.tensor_copy(kvm[:, :, :], ps_kvm[:, :].rearrange("p (m n) -> p m n", m=KH)).then_inc(S["kvm_ready"], 1)

            def moments(src, n, ready):
                dve_link(dve, dve.bn_stats(st2[:, n, :], src))
                dve.sem_inc(S["dve_past"], 1)
                dve.bn_aggr(mv2[:, n, :], st2[:, n, :]).then_inc(S[ready], 1)

            def step(i):
                def sums(*gs):
                    for g in gs:
                        nxt = g if g < GM and (not isinstance(i, int) or i < LAST_STEP) else None
                        add(first_group(i) + g, ps_win2[g], r[g], nxt, groups_at(i))

                r = load_values(mybir.EngineType.DVE, base_m[0:1, ds(i * MROW, groups_at(i))], N, "a group's first node is a dst, or N where the group is padding")
                if active(i, 4):
                    dve.wait_ge(S["m2_ready"], i - 3)
                    moments(ps_m2[:, 0:D], 1, "mv2_ready")
                    dve.wait_ge(S["mv2_ready"], i - 3)
                    dve.scalar_tensor_tensor(out=z2, in0=ps_m2[:, 0:D], scalar=mv2[:, 1, 0:1], in1=row_g2[:, :], op0=ALU.subtract, op1=ALU.mult).then_inc(S["m2_free"], 1)
                between = isinstance(i, int) and i == 0
                sums(0)
                if between:
                    copy_kxT()
                if active(i, 4):
                    t = i - 4
                    dve.wait_ge(S["sd2_ready"], i - 3)
                    dve_link(dve, dve.reciprocal(rs2[:, 1:2], sd2[:, 1:2]))
                    dve.wait_ge(S["m2_free"], i - 2)
                    dve.sem_inc(S["dve_past"], 1)
                    v = xres[:, ds(t, 1), :].rearrange("p a d -> p (a d)")
                    dve_link(dve, dve.scalar_tensor_tensor(out=v, in0=z2, scalar=rs2[:, 1:2], in1=v, op0=ALU.mult, op1=ALU.add))
                sums(1)
                if between:
                    diagonal()
                sums(2)
                if active(i, 1):
                    dve.wait_ge(S["m_ready"], i)
                    moments(ps_m[:, 0:D], 0, "mv_ready")
                sums(3)
                if active(i, 1):
                    dve.wait_ge(S["sd_ready"], i)
                    dve_link(dve, dve.reciprocal(rs2[:, 0:1], sd2[:, 0:1]))
                    dve.tensor_scalar(z1, ps_m[:, 0:D], mv2[:, 0, 0:1], rs2[:, 0:1], ALU.subtract, ALU.mult).then_inc(S["z1_ready"], 1)
                if between:
                    copy_kvm()
                if active(i, 0):
                    dve.wait_ge(S["den_ready"], i + 1)
                    dve_link(dve, dve.reciprocal(den[:, :], den[:, :]))
                    dve.scalar_tensor_tensor(out=mT[:, :, :], in0=qT[:, :, ds(i * P, P)], scalar=float(N), in1=halves(den[:, :]),
                                             op0=ALU.mult, op1=ALU.mult).then_inc(S["mT_ready"], 1)
                sums(*range(4, groups_at(i)))
                if active(i, 0):
                    dve.wait_ge(S["mT_ready"], i + 1)
                if active(i, 1):
                    dve.wait_ge(S["z1_ready"], i)

            second_pass(dve, step, dve_steps)

        @block.scalar
        def _(act):
            def prepare(t, b, count):
                act.wait_ge(S["pe_kq"], count)
                act.sem_inc(S["act_past"], 1)
                act.activation(xTs[b][:, :, :], xT[:, :, ds(t * P, P)], ACT.Copy).then_inc(S["xTs_ready"], 1)

            act.sem_inc(S["marked"], 1)
            with act.Fori(0, NT // NB) as i:
                prepare(i * NB, 0, i * NB + 2)
                for j in range(NB):
                    t = i * NB + j
                    if j < NB - 1:
                        prepare(t + 1, (j + 1) % 2, t + 2)
                    act.wait_ge(S["kx_acc"], t + 1)
                    act.sem_inc(S["act_past"], 1)
                    act.activation(x_t[X_T[j]][:, D:D + 1], valid[:, ds(t, 1)], ACT.Copy).then_inc(S["marked"], 1)
                    act.wait_ge(S["kq_min"], t + 1)
                    act.activation(kqe[:, :], kqe[:, :], ACT.Exp).then_inc(S["kq_exp"], 1)

            def step(i):
                if active(i, 4):
                    act.wait_ge(S["mv2_ready"], i - 3)
                    act.activation(sd2[:, 1:2], mv2[:, 1, 1:2], ACT.Sqrt, bias=epsln[:, 0:1]).then_inc(S["sd2_ready"], 1)
                if active(i, 3):
                    act.wait_ge(S["h_ready"], i - 2)
                    act.activation(hT[:, :, :], ps_hid[:, :].rearrange("p (o n) -> p o n", n=P), ACT.Relu).then_inc(S["hT_ready"], 1)
                if active(i, 2):
                    act.wait_ge(S["zT_ready"], i - 1)
                    for m in range(KH):
                        ins = act.activation(mzT[:, m, :], ps_zT[:, m * P:(m + 1) * P], ACT.Identity, scale=m_g1[:, m:m + 1], bias=m_b1[:, m:m + 1])
                    ins.then_inc(S["mzT_ready"], 1)
                if active(i, 1):
                    act.wait_ge(S["mv_ready"], i)
                    act.activation(sd2[:, 0:1], mv2[:, 0, 1:2], ACT.Sqrt, bias=epsln[:, 0:1]).then_inc(S["sd_ready"], 1)
                if active(i, 0):
                    if not isinstance(i, int) or i > 0:
                        act.wait_ge(S["mT_ready"], i)
                    act.wait_ge(S["den_sum"], i + 1)
                    act.activation(den, ps_nd[:, 0:D], ACT.Identity, bias=epsatt[:, 0:1]).then_inc(S["den_ready"], 1)

            second_pass(act, step)

    for n in ("far_left", "far_free", "far_idx", "far_got", "far_scaled", "far_onehot", "far_sums", "far_added"):
        S[n] = sem(n)
    WIDES = NP // WIDE
    assert NP % WIDE == 0
    far_hot = early[:, 12 * EW:12 * EW + WIDE]
    with nc.Block() as block:

        @block.gpsimd
        def _(pool):
            taken, = load_values(mybir.EngineType.Pool, flag[0:1, 0:1], 1, "the outcome of a comparison")
            with pool.If(taken == 1):
                with pool.Fori(0, GROUPS) as g:
                    for h in range(2):
                        pool.wait_ge(S["far_free"], g * 2 + (h + 1))
                        pool.sem_inc(S["pool_past"], 1)
                        pool.tensor_copy(idx[:, 0:1], c_src[:, h, ds(g, 1)]).then_inc(S["far_idx"], 1)
                        pool.wait_ge(S["far_idx"], g * 2 + (h + 1))
                        pool.sem_inc(S["pool_past"], 1)
                        pool.indirect_dma_start(out=gath[0], out_offset=None, in_=xn_rows[:, :],
                                                in_offset=bass.IndirectOffsetOnAxis(ap=idx[:, 0:1], axis=0)).then_inc(S["far_got"], 16)

        @block.vector
        def _(dve):
            taken, = load_values(mybir.EngineType.DVE, flag[0:1, 0:1], 1, "the outcome of a comparison")
            with dve.If(taken == 1):
                v = c_w[:, :, :]
                dve.scalar_tensor_tensor(out=v, in0=c_loc[:, :, :], scalar=float(WIN), in1=v, op0=ALU.is_ge, op1=ALU.mult).then_inc(S["far_left"], 1)
                dve.wait_ge(S["far_left"], 1)
                dve.sem_inc(S["far_free"], 1)
                with dve.Fori(0, GROUPS) as g:
                    for h in range(2):
                        c = g * 2 + h
                        dve.wait_ge(S["far_got"], c * 16 + 16)
                        dve.sem_inc(S["dve_past"], 1)
                        dve.tensor_scalar(gath[0], gath[0], c_w[:, h, ds(g, 1)], None, ALU.mult).then_inc(S["far_scaled"], 1)
                        for w in range(WIDES):
                            k = c * WIDES + w
                            dve.tensor_scalar(far_hot[:, :], iota_w[:, :], c_dst[:, h, ds(g, 1)], float(-w * WIDE),
                                              ALU.subtract, ALU.is_equal).then_inc(S["far_onehot"], 1)
                            dve.wait_ge(S["far_sums"], k + 1)
                            for m in range(KH):
                                v = aggT[:, m, w * WIDE:(w + 1) * WIDE]
                                ins = dve.tensor_tensor(v, v, bank[m][:, 0:WIDE], ALU.add)
                            ins.then_inc(S["far_added"], 1)
                            dve.wait_ge(S["far_added"], k + 1)
                        dve.sem_inc(S["far_free"], 1)

        @block.tensor
        def _(pe):
            taken, = load_values(mybir.EngineType.PE, flag[0:1, 0:1], 1, "the outcome of a comparison")
            with pe.If(taken == 1):
                with pe.Fori(0, 2 * GROUPS) as c:
                    pe.wait_ge(S["far_scaled"], c + 1)
                    pe.sem_inc(S["pe_past"], 1)
                    for w in range(WIDES):
                        pe.wait_ge(S["far_onehot"], c * WIDES + (w + 1))
                        for m in range(KH):
                            ins = pe.matmul(bank[m][:, 0:WIDE], gath[0][:, m * P:(m + 1) * P], far_hot[:, :], start=True, stop=True)
                        ins.then_inc(S["far_sums"], 1)

    NB_TOK = NB * P
    PIECE = NB_TOK // 2
    g1T = w_1[:, :, :].rearrange("p k n -> p (k n)")[:, 0:KH * NB_TOK].rearrange("p (h n) -> p h n", h=KH)
    xn2 = spare[:, 0:NB * D].rearrange("p (j d) -> p j d", j=NB)
    pairs = ((0, 1), (2, 3), (4,))
    xn2T = [spare[:, NB * D:(NB + 2) * D], w_2[:, :, :].rearrange("p k n -> p (k n)")[:, 0:2 * D], spare[:, (NB + 2) * D:(NB + 3) * D]]
    TN = NT * NE
    TT = XT_TILES
    agg_flat = aggT[:, :, :].rearrange("p h n -> p (h n)")
    taken = [0]

    def late(*shape):
        n = 1
        for d in shape:
            n *= d
        taken[0] += n
        v = agg_flat[:, KH * NP - taken[0]:KH * NP - taken[0] + n]
        return v if len(shape) == 1 else v.rearrange("p (a b) -> p a b", b=shape[-1])

    probs, rtmp, chosen = (late(NT, NE) for _ in range(3))
    picks2 = late(2 * NT, NE)
    picks = picks2.rearrange("p (k t) e -> p k t e", k=2)
    run_in, run = late(NE, NT), late(NE, NT)
    past = late(TT, NE - 1)
    logits = sb("logits", [P, NT, NE])
    rev = sb("rev", [P, NE]); rmax = sb("rmax", [P, NT]); wts = sb("wts", [P, 2, NT]); slots = sb("slots", [P, 2, NT], I32)
    slot_f = sb("slot_f", [P, 2, NT])
    count = sb("count", [P, NE]); count_i = sb("count_i", [P, NE], I32); ntile = sb("ntile", [P, NE]); until = sb("until", [P, NE])
    shift = sb("shift", [P, NE])
    jt = sb("jt", [P, TT]); t_exp = sb("t_exp", [P, TT])
    ti_exp = sb("ti_exp", [P, TT], I32)
    stats5 = sb("stats5", [P, NB, 6]); mv5 = sb("mv5", [P, NB, 2]); std5 = sb("std5", [P, NB]); rstd5 = sb("rstd5", [P, NB])
    tile_nr = sb("tile_nr", [P, 2, NT]); in_tile = sb("in_tile", [P, 1]); no_row = sb("no_row", [P, TT])
    list_row = sb("list_row", [P, TT]); list_hit = sb("list_hit", [P, TT]); list_tmp = sb("list_tmp", [P, TT])
    from_row = sb("from_row", [P, TT], I32); to_row = sb("to_row", [P, TT], I32)
    for n in ("h0_ready", "g1_ready", "g1T_ready", "g2_ready", "g2_done", "var5", "std5", "n2_ready", "n2_stored", "n2_T", "n2T_ready",
              "logit_ready", "logits_done", "soft", "chosen_ready", "ranks_ready", "pool_consts", "hots_ready", "inverse",
              "rows_ready", "from_idx", "to_idx",
              "top_taken", "low_taken", "hots_used", "hits", "hots_ready_b", "xg_split", "he_split", "xg_split_top", "he_split_top", "xg_T", "xgT_ready", "he_ready", "hs_ready", "heT_ready", "gelu_ready", "ye_ready", "y_ready", "ye_free"):
        S[n] = sem(n)
    experts_loaded = [sem(f"experts_loaded{n}") for n in range(2 * KH + HC + 2)]
    SPLIT = HC - 1
    W1, W2 = NE * HE, NE * D
    top_w1 = [parts["xT"][:, 0:W1], parts["mix_w"][:, 0:W1]]
    top_w2 = [parts["xT"][:, W1:W1 + W2], parts["mix_w"][:, W1:W1 + W2], parts["spare"][:, 0:W2]]
    low_w1 = [parts["e_w1"][:, k * W1:(k + 1) * W1] for k in range(KH)]
    low_w2 = [parts["q_w2"][:, c * W2:(c + 1) * W2] for c in range(SPLIT)]
    splits = [(e_w1[:, 0, :], top_w1[0], low_w1[0]), (e_w2[:, 0, :], top_w2[0], low_w2[0]), (e_w1[:, 1, :], top_w1[1], low_w1[1]),
              (e_w2[:, 2, :], top_w2[2], low_w2[2]), (e_w2[:, 1, :], top_w2[1], low_w2[1])]
    EARLY_TOPS, EARLY_LOWS = 3, 2

    def take_top(dve, n):
        whole, top, _ = splits[n]
        dve.tensor_copy(top.bitcast(F32R), whole).then_inc(S["top_taken"], 1)

    def take_low(pool, n):
        whole, top, low = splits[n]
        pool.wait_ge(S["top_taken"], n + 1)
        pool.sem_inc(S["pool_past"], 1)
        pool.tensor_tensor(low.bitcast(F32R), whole, top, ALU.subtract).then_inc(S["low_taken"], 1)

    xg_loaded = [sem(f"xg_loaded{b}") for b in range(2)]
    y_stored = [sem(f"y_stored{b}") for b in range(2)]

    def chunk_pass(eng, step):
        step(0)
        with eng.Fori(1, CHUNKS) as i:
            step(i)
        step(CHUNKS)

    with nc.Block() as block:

        @block.sync
        def _(sp):
            half = NE // 2
            pieces = [(e_w1[:, k, h * half * HE:(h + 1) * half * HE].rearrange("p (e n) -> p e n", e=half),
                       a["L0_ffn_W1"][h * half:(h + 1) * half, k * P:(k + 1) * P, :].rearrange("e p n -> p e n")) for k in range(KH) for h in range(2)]
            pieces += [(e_w2[:, c, :].rearrange("p (e n) -> p e n", e=NE), a["L0_ffn_W2"][:, c * P:(c + 1) * P, :].rearrange("e p n -> p e n")) for c in range(HC)]
            pieces += [(e_b1[:, :], a["L0_ffn_b1"].rearrange("e (c p) -> p (e c)", p=P)),
                       (e_b2[:, :], a["L0_ffn_b2"].rearrange("e n -> (e n)").partition_broadcast(P))]
            share = -(-len(pieces) // CHUNKS)
            for c in range(CHUNKS):
                for n, (to, frm) in enumerate(pieces[c * share:(c + 1) * share], c * share):
                    sp.dma_start(to, frm, allow_slow_non_contiguous=True).then_inc(experts_loaded[n], 16)
                sp.wait_ge(S["n2_ready"], (c + 1) * NB)
                sp.dma_start(xn2_rows[c * NB_TOK:(c + 1) * NB_TOK, :].rearrange("(j p) d -> p j d", p=P), xn2[:, :, :]).then_inc(S["n2_stored"], 16)
            sp.wait_ge(S["n2_stored"], 16 * CHUNKS)
            for loaded in experts_loaded:
                sp.wait_ge(loaded, 16)

        @block.vector
        def _(dve):
            dve_link(dve, dve.tensor_scalar(eps1[:, :], eps1[:, :], 1.0, None, ALU.add))
            for i in range(CHUNKS):
                v = aggT[:, :, i * NB_TOK:(i + 1) * NB_TOK]
                dve.scalar_tensor_tensor(out=v, in0=xT[:, :, i * NB_TOK:(i + 1) * NB_TOK], scalar=eps1[:, 0:1], in1=v,
                                         op0=ALU.mult, op1=ALU.add).then_inc(S["h0_ready"], 1)
            dve.sem_inc(S["g2_done"], 4)
            dve_link(dve, dve.tensor_tensor(b2sum[:, :], row_b2[:, :], row_gb2[:, :], ALU.add))
            row = lambda t: xres[:, ds(t, 1), :].rearrange("p a d -> p (a d)")

            def moments(t, j):
                dve.wait_ge(S["g2_done"], t + 5)
                dve.sem_inc(S["dve_past"], 1)
                return dve.bn_stats(stats5[:, j, :], row(t))

            def step(i):
                if not isinstance(i, int) or i > 0:
                    dve.wait_ge(S["logit_ready"], i)
                    dve.sem_inc(S["dve_past"], 1)
                    dve.tensor_tensor(logits[:, ds((i - 1) * NB, NB), :], bank[7][:, 0:NB * NE].rearrange("p (j e) -> p j e", e=NE),
                                      gate_b[:, :].unsqueeze(1).to_broadcast([P, NB, NE]), ALU.add).then_inc(S["logits_done"], 1)
                if isinstance(i, int) and i == CHUNKS:
                    return
                v = xres[:, ds(i * NB, NB), :]
                dve_link(dve, dve.tensor_tensor(v, v, b2sum[:, :].unsqueeze(1).to_broadcast([P, NB, D]), ALU.add))
                for j in range(NB):
                    t = i * NB + j
                    dve.wait_ge(S["g2_ready"], t + 1)
                    dve.sem_inc(S["dve_past"], 1)
                    dve.tensor_tensor(row(t), row(t), bank[4 + j % 4][:, 0:D], ALU.add).then_inc(S["g2_done"], 1)
                    if j:
                        moments(t - 1, j - 1)
                dve_link(dve, moments(t, j))
                dve.sem_inc(S["dve_past"], 1)
                for j in range(NB):
                    ins = dve.bn_aggr(mv5[:, j, :], stats5[:, j, :])
                ins.then_inc(S["var5"], 1)
                dve.wait_ge(S["std5"], i + 1)
                dve_link(dve, dve.reciprocal(rstd5[:, :], std5[:, :]))
                if not isinstance(i, int) or i > 0:
                    dve.wait_ge(S["n2_T"], i * len(pairs))
                    dve.wait_ge(S["n2_stored"], i * 16)
                for j in range(NB):
                    dve.tensor_scalar(xn2[:, j, :], row(i * NB + j), mv5[:, j, 0:1], rstd5[:, j:j + 1], ALU.subtract, ALU.mult).then_inc(S["n2_ready"], 1)
                dve.wait_ge(S["n2_ready"], i * NB + NB)

            step(0)
            for n in range(2):
                dve.wait_ge(experts_loaded[n], 16)
            take_top(dve, 0)
            with dve.Fori(1, CHUNKS) as i:
                dve_steps.enter(i - 1, 3)
                step(i)
            dve_steps.leave(CHUNKS - 1)
            for n in (2 * KH, 2, 3):
                dve.wait_ge(experts_loaded[n], 16)
            for n in range(1, EARLY_TOPS):
                take_top(dve, n)
            step(CHUNKS)

        @block.tensor
        def _(pe):
            def step(i):
                if not isinstance(i, int) or i < CHUNKS:
                    pe.wait_ge(S["h0_ready"], i + 1)
                    for n in range(2):
                        for m in range(KH):
                            for k in range(KH):
                                ins = pe.matmul(bank[2 * n + m][:, 0:PIECE], g_w1[:, k, m * P:(m + 1) * P], aggT[:, k, ds(i * NB_TOK + n * PIECE, PIECE)],
                                                start=(k == 0), stop=(k == KH - 1))
                            ins.then_inc(S["g1_ready"], 1)
                if not isinstance(i, int) or i > 0:
                    pe.wait_ge(S["n2_ready"], i * NB)
                    for q, js in enumerate(pairs):
                        for j in js:
                            for h in range(KH):
                                lo = (j - js[0]) * D + h * P
                                ins = pe.transpose(bank[4 + q][:, lo:lo + P], xn2[:, j, h * P:(h + 1) * P], ident[:, :])
                        ins.then_inc(S["n2_T"], 1)
                    for q, js in enumerate(pairs):
                        pe.wait_ge(S["n2T_ready"], (i - 1) * len(pairs) + (q + 1))
                        for j in js:
                            for k in range(KH):
                                lo = (j - js[0]) * D + k * P
                                ins = pe.matmul(bank[7][:, j * NE:(j + 1) * NE], xn2T[q][:, lo:lo + P], gate_w[:, k, :], start=(k == 0), stop=(k == KH - 1))
                    ins.then_inc(S["logit_ready"], 1)
                if isinstance(i, int) and i == CHUNKS:
                    return
                for j in range(NB):
                    t = i * NB + j
                    pe.wait_ge(S["g1T_ready"], i * 4 + (2 if (j + 1) * P <= PIECE else 4))
                    if j == 3 and (not isinstance(i, int) or i > 0):
                        pe.wait_ge(S["logits_done"], i)
                    if j == 4:
                        pe.wait_ge(S["g2_done"], t + 1)
                    for k in range(KH):
                        ins = pe.matmul(bank[4 + j % 4][:, 0:D], g1T[:, k, j * P:(j + 1) * P], g_w2[:, k, :], start=(k == 0), stop=(k == KH - 1))
                    ins.then_inc(S["g2_ready"], 1)

            chunk_pass(pe, step)

        @block.scalar
        def _(act):
            def step(i):
                if not isinstance(i, int) or i < CHUNKS:
                    for n in range(2):
                        for m in range(KH):
                            act.wait_ge(S["g1_ready"], i * 4 + (2 * n + m + 1))
                            act.activation(g1T[:, m, n * PIECE:(n + 1) * PIECE], bank[2 * n + m][:, 0:PIECE], ACT.Relu, bias=g_b1[:, m:m + 1]).then_inc(S["g1T_ready"], 1)
                if not isinstance(i, int) or i > 0:
                    for q, js in enumerate(pairs):
                        act.wait_ge(S["n2_T"], (i - 1) * len(pairs) + (q + 1))
                        act.activation(xn2T[q], bank[4 + q][:, 0:len(js) * D], ACT.Copy).then_inc(S["n2T_ready"], 1)
                if not isinstance(i, int) or i < CHUNKS:
                    act.wait_ge(S["var5"], i + 1)
                    act.activation(std5[:, :], mv5[:, :, 1], ACT.Sqrt, bias=epsln[:, 0:1]).then_inc(S["std5"], 1)

            chunk_pass(act, step)

        @block.gpsimd
        def _(pool):
            def ramp(out, pattern, start, by_partition):
                pool.iota(out, pattern=pattern, base=start, channel_multiplier=by_partition, allow_small_or_imprecise_dtypes=True).then_inc(S["pool_consts"], 1)

            ramp(rev[:, :], [[-1, NE]], NE, 0)
            ramp(jt[:, :], [[1, TT]], 0, 0)
            ramp(tile_nr[:, :, :], [[NT, 2], [1, NT]], 1, 0)
            ramp(in_tile[:, :], [[0, 1]], 0, 1)
            ramp(no_row[:, :], [[P, TT]], 2 * NP + 1, 1)
            for n in range(EARLY_LOWS):
                take_low(pool, n)

    per_e = lambda v, n=NT: v.unsqueeze(2).to_broadcast([P, n, NE])
    per_t = lambda v, n=NT: v.unsqueeze(1).to_broadcast([P, n, NE])
    by_e = lambda v: v.rearrange("p (t e) -> p t e", e=NE)
    place_i = sb("place_i", [P, 2, 2, NT], I32); place = sb("place", [P, 2, 2, NT])
    hot_row = parts["aggT"][:, 0:2 * NB * P].rearrange("p (b n r) -> p b n r", b=2, r=P)
    hot_tile = parts["aggT"][:, 2 * NB * P:2 * NB * (P + 2 * TT)].rearrange("p (b n j) -> p b n j", b=2, j=2 * TT)
    hit = agg_flat[:, 2 * NB * (P + 2 * TT):2 * NB * (P + 3 * TT)].rearrange("p (b n j) -> p b n j", b=2, j=TT)
    assert 2 * NB * (P + 3 * TT) + taken[0] <= KH * NP

    with nc.Block() as block:

        @block.vector
        def _(dve):
            L = lambda ins: dve_link(dve, ins)
            tt, red = dve.tensor_tensor, dve.tensor_reduce
            L(red(rmax[:, :], logits[:, :, :], AX.X, ALU.max))
            tt(rtmp[:, :, :], logits[:, :, :], per_e(rmax[:, :]), ALU.subtract).then_inc(S["soft"], 1)
            dve.wait_ge(S["soft"], 2)
            L(red(rmax[:, :], probs[:, :, :], AX.X, ALU.add))
            L(dve.reciprocal(rmax[:, :], rmax[:, :]))
            L(tt(probs[:, :, :], probs[:, :, :], per_e(rmax[:, :]), ALU.mult))
            for k in range(2):
                L(red(wts[:, k, :], probs[:, :, :], AX.X, ALU.max))
                L(tt(rtmp[:, :, :], probs[:, :, :], per_e(wts[:, k, :]), ALU.is_equal))
                L(tt(rtmp[:, :, :], rtmp[:, :, :], per_t(rev[:, :]), ALU.mult))
                L(red(rmax[:, :], rtmp[:, :, :], AX.X, ALU.max))
                L(tt(picks[:, k, :, :], per_t(rev[:, :]), per_e(rmax[:, :]), ALU.is_equal))
                if k == 0:
                    L(dve.scalar_tensor_tensor(out=probs[:, :, :], in0=picks[:, 0, :, :], scalar=-2.0, in1=probs[:, :, :], op0=ALU.mult, op1=ALU.add))
            L(tt(chosen[:, :, :], picks[:, 0, :, :], picks[:, 1, :, :], ALU.add))
            tt(chosen[:, :, :], chosen[:, :, :], per_e(valid[:, :]), ALU.mult).then_inc(S["chosen_ready"], 1)
            for n in range(EARLY_TOPS, len(splits)):
                take_top(dve, n)
            dve.wait_ge(S["ranks_ready"], 1)
            L(dve.tensor_copy(run_in[:, :, :].rearrange("p e t -> p t e"), by_e(bank[1][:, 0:TN])))
            flat = lambda v: v[:, :, :].rearrange("p e t -> p (e t)")
            L(dve.tensor_tensor_scan(flat(run), flat(run_in), flat(run_in), 0.0, ALU.add, ALU.bypass))
            L(dve.tensor_copy(count[:, 0:1], run[:, 0, NT - 1:NT]))
            L(tt(count[:, 1:NE], run[:, 1:NE, NT - 1], run[:, 0:NE - 1, NT - 1], ALU.subtract))
            L(tt(run_in[:, :, :], run[:, :, :], run_in[:, :, :], ALU.subtract))
            L(tt(shift[:, :], run[:, :, NT - 1], count[:, :], ALU.subtract))
            L(dve.tensor_scalar(count[:, :], count[:, :], float(P - 1), None, ALU.add))
            L(dve.tensor_copy(count_i[:, :], count[:, :]))
            L(dve.tensor_scalar(count_i[:, :], count_i[:, :], 7, None, ALU.logical_shift_right))
            L(dve.tensor_copy(ntile[:, :], count_i[:, :]))
            L(dve.tensor_tensor_scan(until[:, :], ntile[:, :], ntile[:, :], 0.0, ALU.add, ALU.bypass))
            L(tt(ntile[:, :], until[:, :], ntile[:, :], ALU.subtract))
            L(dve.scalar_tensor_tensor(out=shift[:, :], in0=ntile[:, :], scalar=float(P), in1=shift[:, :], op0=ALU.mult, op1=ALU.subtract))
            L(tt(rtmp[:, :, :], by_e(bank[0][:, 0:TN]), run_in[:, :, :].rearrange("p e t -> p t e"), ALU.add))
            L(tt(rtmp[:, :, :], rtmp[:, :, :], per_t(shift[:, :]), ALU.add))
            for k in range(2):
                L(tt(probs[:, :, :], picks[:, k, :, :], rtmp[:, :, :], ALU.mult))
                L(red(slot_f[:, k, :], probs[:, :, :], AX.X, ALU.add))
            L(dve.tensor_copy(slots[:, :, :], slot_f[:, :, :]))
            L(dve.tensor_scalar(place_i[:, 0], slots[:, :, :], P - 1, None, ALU.bitwise_and))
            L(dve.tensor_scalar(place_i[:, 1], slots[:, :, :], P.bit_length() - 1, None, ALU.logical_shift_right))
            L(dve.tensor_copy(place[:, :], place_i[:, :]))
            L(dve.scalar_tensor_tensor(out=place[:, 1], in0=place[:, 1], scalar=1.0, in1=valid[:, :].unsqueeze(1).to_broadcast([P, 2, NT]), op0=ALU.add, op1=ALU.mult))
            for c in range(2 * CHUNKS):
                cut_, b = slice(c * NB, (c + 1) * NB), c % 2
                at = lambda v, n: v.rearrange("p k t -> p (k t)")[:, cut_].unsqueeze(2).to_broadcast([P, NB, n])
                along = lambda lo, n: iota_w[:, lo:lo + n].unsqueeze(1).to_broadcast([P, NB, n])
                if c >= 2:
                    dve.wait_ge(S["hots_used"], c - 1)
                tt(hit[:, b], at(place[:, 1], TT), along(1, TT), ALU.is_equal).then_inc(S["hits"], 1)
                tt(hot_row[:, b].bitcast(F32R), at(place[:, 0], P), along(0, P), ALU.is_equal)
                dve.wait_ge(S["hits"], c + 1)
                tt(hot_tile[:, b, :, 0:TT].bitcast(F32R), hit[:, b], at(tile_nr[:, :, :], TT), ALU.mult).then_inc(S["hots_ready"], 1)
            L(tt(past[:, :, :], jt[:, :].unsqueeze(2).to_broadcast([P, TT, NE - 1]), until[:, 0:NE - 1].unsqueeze(1).to_broadcast([P, TT, NE - 1]), ALU.is_ge))
            L(red(t_exp[:, :], past[:, :, :], AX.X, ALU.add))
            dve.tensor_copy(ti_exp[:, :], t_exp[:, :]).then_inc(S["rows_ready"], 1)
            dve.wait_ge(S["inverse"], 1)
            L(dve.tensor_scalar(list_tmp[:, :], bank[2][:, 0:TT], 0.0, float(1 - P), ALU.is_gt, ALU.mult))
            L(dve.scalar_tensor_tensor(out=list_tmp[:, :], in0=bank[2][:, 0:TT], scalar=float(P), in1=list_tmp[:, :], op0=ALU.mult, op1=ALU.add))
            L(tt(list_row[:, :], bank[2][:, TT:2 * TT], list_tmp[:, :], ALU.add))
            L(dve.tensor_scalar(list_hit[:, :], list_row[:, :], 0.0, None, ALU.is_equal))
            L(tt(list_hit[:, :], list_hit[:, :], no_row[:, :], ALU.mult))
            L(dve.scalar_tensor_tensor(out=list_hit[:, :], in0=list_row[:, :], scalar=-1.0, in1=list_hit[:, :], op0=ALU.add, op1=ALU.add))
            dve.tensor_copy(to_row[:, :], list_hit[:, :]).then_inc(S["rows_ready"], 1)
            L(dve.tensor_scalar(list_tmp[:, :], list_row[:, :], float(NP), float(-NP), ALU.is_gt, ALU.mult))
            L(dve.scalar_tensor_tensor(out=list_row[:, :], in0=list_row[:, :], scalar=-1.0, in1=list_tmp[:, :], op0=ALU.add, op1=ALU.add))
            L(dve.tensor_scalar(list_row[:, :], list_row[:, :], 0.0, None, ALU.max))
            dve.tensor_copy(from_row[:, :], list_row[:, :]).then_inc(S["rows_ready"], 1)

        @block.scalar
        def _(act):
            act.wait_ge(S["soft"], 1)
            act.activation(probs[:, :, :], rtmp[:, :, :], ACT.Exp).then_inc(S["soft"], 1)
            for c in range(2 * CHUNKS):
                act.wait_ge(S["hits"], c + 1)
                act.activation(hot_tile[:, c % 2, :, TT:2 * TT].bitcast(F32R), hit[:, c % 2], ACT.Copy, scale=in_tile[:, 0:1]).then_inc(S["hots_ready_b"], 1)

        @block.tensor
        def _(pe):
            pe.wait_ge(S["chosen_ready"], 1)
            c = chosen[:, :, :].rearrange("p t e -> p (t e)")
            pe.matmul(bank[0][:, 0:TN], before[:, :], c, start=True, stop=True)
            pe.matmul(bank[1][:, 0:TN], ones[:, :], c, start=True, stop=True).then_inc(S["ranks_ready"], 1)
            for n in range(2 * NT):
                if n % NB == 0:
                    pe.wait_ge(S["hots_ready"], n // NB + 1)
                    pe.wait_ge(S["hots_ready_b"], n // NB + 1)
                b = n // NB % 2
                ins = pe.matmul(bank[2][:, 0:2 * TT], hot_row[:, b, n % NB, :].bitcast(F32R), hot_tile[:, b, n % NB, :].bitcast(F32R), start=(n == 0), stop=(n == 2 * NT - 1))
                if n % NB == NB - 1 and n < 2 * NT - 1:
                    ins.then_inc(S["hots_used"], 1)
            ins.then_inc(S["inverse"], 1)

        @block.gpsimd
        def _(pool):
            for n in range(EARLY_LOWS, len(splits)):
                take_low(pool, n)

    work = aggT[:, :, :].rearrange("p h n -> p (h n)")
    cut = [0]

    def piece(n, part=False):
        cut[0] += 2 * n
        views = [v[:, cut[0] - 2 * n:cut[0]].rearrange("p (b n) -> p b n", b=2) for v in (work, parts["aggT"])]
        return views if part else views[0]

    xg, hs, ye = piece(D), piece(HE), piece(D)
    (xgT, xgT_low), (_, xgT_top) = piece(D, True), piece(D, True)
    (heT, heT_low), (_, heT_top) = piece(HE, True), piece(SPLIT * P, True)
    assert cut[0] <= KH * NP

    def split_product(pe, out, x_top, x_low, w_top, w_low, columns, first, last):
        parts = ((x_top, w_top), (x_top, w_low), (x_low, w_top))
        for n, (x, w) in enumerate(parts):
            ins = pe.matmul(out, x.bitcast(F32R), w[:, columns].bitcast(F32R), start=(first and n == 0), stop=(last and n == len(parts) - 1))
        return ins

    STEPS = XT_TILES // 2
    from_idx = sb("from_idx", [P, 2], I32); to_idx = sb("to_idx", [P, 2], I32)

    def busy(i, stage):
        return not isinstance(i, int) or 0 <= i - stage < STEPS

    def expert_pass(eng, step):
        for i in range(3):
            step(i)
        with eng.Fori(3, STEPS) as i:
            step(i)
        for i in range(STEPS, STEPS + 3):
            step(i)

    def experts_of(engine, i):
        return load_values(engine, ti_exp[0:1, ds(i * 2, 2)], NE - 1, "a count of NE - 1 comparisons")

    with nc.Block() as block:

        @block.gpsimd
        def _(pool):
            def gather(i):
                pool.tensor_copy(from_idx[:, :], from_row[:, ds(i * 2, 2)]).then_inc(S["from_idx"], 1)
                pool.wait_ge(S["from_idx"], i + 1)
                pool.sem_inc(S["pool_past"], 1)
                for b in range(2):
                    pool.indirect_dma_start(out=xg[:, b, :], out_offset=None, in_=xn2_rows[:, :],
                                            in_offset=bass.IndirectOffsetOnAxis(ap=from_idx[:, b:b + 1], axis=0)).then_inc(xg_loaded[b], 16)

            def step(i):
                if busy(i, 3):
                    if not isinstance(i, int) or i > 3:
                        for b in range(2):
                            pool.wait_ge(y_stored[b], (i - 3) * 16)
                        pool.sem_inc(S["pool_past"], 1)
                    pool.tensor_copy(to_idx[:, :], to_row[:, ds((i - 3) * 2, 2)]).then_inc(S["to_idx"], 1)
                    pool.wait_ge(S["to_idx"], i - 2)
                    for b in range(2):
                        pool.wait_ge(S["y_ready"], (i - 3) * 2 + (b + 1))
                        pool.sem_inc(S["pool_past"], 1)
                        pool.indirect_dma_start(out=results[:, :], out_offset=bass.IndirectOffsetOnAxis(ap=to_idx[:, b:b + 1], axis=0),
                                                in_=ye[:, b, :], in_offset=None).then_inc(y_stored[b], 16)
                if not isinstance(i, int) or i < STEPS - 1:
                    pool.wait_ge(S["xg_T"], i * 2 + 2)
                    pool.sem_inc(S["pool_past"], 1)
                    gather(i + 1)

            gather(0)
            for i in range(4):
                step(i)
            with pool.Fori(4, STEPS - 1) as i:
                step(i)
            for i in range(STEPS - 1, STEPS + 3):
                step(i)
            for b in range(2):
                pool.wait_ge(y_stored[b], 16 * STEPS)

        @block.tensor
        def _(pe):
            def step(i):
                if busy(i, 3):
                    e = experts_of(mybir.EngineType.PE, i - 3)
                    for b in range(2):
                        pe.wait_ge(S["he_split"], (i - 3) * 2 + (b + 1))
                        pe.wait_ge(S["ye_free"], (i - 3) * 2 + (b + 1))
                        for c in range(SPLIT):
                            rows_ = slice(c * P, (c + 1) * P)
                            split_product(pe, bank[6 + b][:, 0:D], heT_top[:, b, rows_], heT_low[:, b, rows_], top_w2[c], low_w2[c], ds(e[b] * D, D), c == 0, False)
                        ins = pe.matmul(bank[6 + b][:, 0:D], heT[:, b, SPLIT * P:HE], e_w2[:, SPLIT, ds(e[b] * D, D)], start=False, stop=True)
                        ins.then_inc(S["ye_ready"], 1)
                if busy(i, 2):
                    for b in range(2):
                        pe.wait_ge(S["hs_ready"], (i - 2) * 2 + (b + 1))
                        for c in range(HC):
                            ins = pe.transpose(bank[4 + b][:, c * P:(c + 1) * P], hs[:, b, c * P:(c + 1) * P], ident[:, :])
                        ins.then_inc(S["heT_ready"], 1)
                if busy(i, 1):
                    e = experts_of(mybir.EngineType.PE, i - 1)
                    for b in range(2):
                        pe.wait_ge(S["xg_split"], (i - 1) * 2 + (b + 1))
                        for k in range(KH):
                            rows_ = slice(k * P, (k + 1) * P)
                            ins = split_product(pe, bank[2 + b][:, 0:HE], xgT_top[:, b, rows_], xgT_low[:, b, rows_], top_w1[k], low_w1[k], ds(e[b] * HE, HE), k == 0, k == KH - 1)
                        ins.then_inc(S["he_ready"], 1)
                if busy(i, 0):
                    for b in range(2):
                        pe.wait_ge(xg_loaded[b], i * 16 + 16)
                        for h in range(KH):
                            ins = pe.transpose(bank[b][:, h * P:(h + 1) * P], xg[:, b, h * P:(h + 1) * P], ident[:, :])
                        ins.then_inc(S["xg_T"], 1)

            expert_pass(pe, step)

        @block.scalar
        def _(act):
            def step(i):
                if busy(i, 2):
                    e = experts_of(mybir.EngineType.Activation, i - 2)
                    for b in range(2):
                        act.wait_ge(S["heT_ready"], (i - 2) * 2 + (b + 1))
                        act.sem_inc(S["act_past"], 1)
                        for c in range(HC):
                            ins = act.activation(heT[:, b, c * P:(c + 1) * P], bank[4 + b][:, c * P:(c + 1) * P], ACT.Gelu, bias=e_b1[:, ds(e[b] * HC + c, 1)])
                        ins.then_inc(S["gelu_ready"], 1)
                if busy(i, 0):
                    for b in range(2):
                        act.wait_ge(S["xg_T"], i * 2 + (b + 1))
                        act.activation(xgT[:, b, :], bank[b][:, 0:D], ACT.Copy).then_inc(S["xgT_ready"], 1)

            expert_pass(act, step)

        @block.vector
        def _(dve):
            def split(whole, top, low, done, before_):
                dve.tensor_copy(top.bitcast(F32R), whole).then_inc(S[done + "_top"], 1)
                dve.wait_ge(S[done + "_top"], before_ + 1)
                dve.sem_inc(S["dve_past"], 1)
                dve.tensor_tensor(low.bitcast(F32R), whole, top, ALU.subtract).then_inc(S[done], 1)

            def step(i):
                if busy(i, 3):
                    e = experts_of(mybir.EngineType.DVE, i - 3)
                    for b in range(2):
                        if not isinstance(i, int) or i > 3:
                            dve.wait_ge(y_stored[b], (i - 3) * 16)
                        dve.wait_ge(S["ye_ready"], (i - 3) * 2 + (b + 1))
                        dve.sem_inc(S["dve_past"], 1)
                        dve.tensor_tensor(ye[:, b, :], bank[6 + b][:, 0:D], e_b2[:, ds(e[b] * D, D)], ALU.add).then_inc(S["y_ready"], 1)
                        dve.wait_ge(S["y_ready"], (i - 3) * 2 + (b + 1))
                        dve.sem_inc(S["ye_free"], 1)
                if busy(i, 2):
                    for b in range(2):
                        dve.wait_ge(S["gelu_ready"], (i - 2) * 2 + (b + 1))
                        split(heT[:, b, 0:SPLIT * P], heT_top[:, b, :], heT_low[:, b, 0:SPLIT * P], "he_split", (i - 2) * 2 + b)
                if busy(i, 1):
                    for b in range(2):
                        dve.wait_ge(S["he_ready"], (i - 1) * 2 + (b + 1))
                        dve.tensor_copy(hs[:, b, :], bank[2 + b][:, 0:HE]).then_inc(S["hs_ready"], 1)
                if busy(i, 0):
                    for b in range(2):
                        dve.wait_ge(S["xgT_ready"], i * 2 + (b + 1))
                        split(xgT[:, b, :], xgT_top[:, b, :], xgT_low[:, b, :], "xg_split", i * 2 + b)

            dve.sem_inc(S["ye_free"], 2)
            for i in range(3):
                step(i)
            step(3)
            with dve.Fori(4, STEPS) as i:
                step(i)
            for i in range(STEPS, STEPS + 3):
                step(i)

    NC, BUFS = 4, 3
    ROUNDS = (NT - 1) // (NC * BUFS)
    assert (NT - 1) % (NC * BUFS) == 0
    y_in = work[:, 0:BUFS * 2 * NC * D].rearrange("p (b k j d) -> p b k j d", b=BUFS, k=2, j=NC)
    y_last = spare[:, 0:2 * D].rearrange("p (k d) -> p k d", k=2)
    for n in ("comb", "o_ready", "last_loaded"):
        S[n] = sem(n)
    y_got = [sem(f"y_got{b}") for b in range(BUFS)]
    o_stored = [sem(f"o_stored{b}") for b in range(BUFS)]

    with nc.Block() as block:

        @block.sync
        def _(sp):
            def load(i, b):
                for k in range(2):
                    sp.dma_start(y_in[:, b, k, :, :], results[ds(i * (BUFS * NC * P) + (k * NP + b * NC * P), NC * P), :].rearrange("(j p) d -> p j d", p=P)).then_inc(y_got[b], 16)

            for b in range(BUFS):
                load(0, b)
            with sp.Fori(1, ROUNDS) as i:
                for b in range(BUFS):
                    sp.wait_ge(o_stored[b], i * 16)
                    sp.sem_inc(S["sp_past"], 1)
                    load(i, b)
            sp.dma_start(y_last[0:LAST, :, :], results[0:2 * NP, :].rearrange("(k n) d -> n k d", k=2)[(NT - 1) * P:N, :, :]).then_inc(S["last_loaded"], 16)
            sp.wait_ge(S["last_loaded"], 16)

        @block.vector
        def _(dve):
            def combine(n, y0, y1, res, w, wait):
                dve.scalar_tensor_tensor(out=y0, in0=y0, scalar=w[0], in1=res, op0=ALU.mult, op1=ALU.add).then_inc(S["comb"], 1)
                dve.wait_ge(S["comb"], wait)
                dve.sem_inc(S["dve_past"], 1)
                dve.scalar_tensor_tensor(out=y0, in0=y1, scalar=w[1], in1=y0, op0=ALU.mult, op1=ALU.add).then_inc(S["o_ready"], 1)

            with dve.Fori(0, ROUNDS) as i:
                for b in range(BUFS):
                    dve.wait_ge(y_got[b], i * 32 + 32)
                    for j in range(NC):
                        t = i * (BUFS * NC) + (b * NC + j)
                        combine(P, y_in[:, b, 0, j, :], y_in[:, b, 1, j, :], xres[:, ds(t, 1), :].rearrange("p a d -> p (a d)"),
                                [wts[:, k, ds(t, 1)] for k in range(2)], t + 1)
            dve.wait_ge(S["last_loaded"], 16)
            combine(LAST, y_last[0:LAST, 0, :], y_last[0:LAST, 1, :], xres[0:LAST, NT - 1, :], [wts[0:LAST, k, NT - 1:NT] for k in range(2)], NT)

        @block.scalar
        def _(act):
            with act.Fori(0, ROUNDS) as i:
                for b in range(BUFS):
                    act.wait_ge(S["o_ready"], i * (BUFS * NC) + (b + 1) * NC)
                    act.sem_inc(S["act_past"], 1)
                    act.dma_start(out[ds(i * (BUFS * NC * P) + b * NC * P, NC * P), :].rearrange("(j p) d -> p j d", p=P), y_in[:, b, 0, :, :]).then_inc(o_stored[b], 16)
            act.wait_ge(S["o_ready"], NT)
            act.dma_start(out[(NT - 1) * P:N, :], y_last[0:LAST, 0, :]).then_inc(o_stored[0], 16)
            for b in range(BUFS):
                act.wait_ge(o_stored[b], 16 * (ROUNDS + (b == 0)))

    ctx.close()


_OUTS = [((3125, 256), "float32")]


def kernel(**inputs):
    import numpy as _np
    import concourse.bacc as _bacc
    from concourse.bass_utils import run_bass_kernel_spmd as _run

    nc = _bacc.Bacc("TRN2", target_bir_lowering=False, num_devices=1)
    arrays, args = {}, {}
    for name, value in inputs.items():
        v = _np.ascontiguousarray(value)
        arrays[f"in_{name}"] = v
        args[name] = nc.dram_tensor(f"in_{name}", v.shape, mybir.dt.from_np(v.dtype), kind="ExternalInput").ap()
    shape, dtype = _OUTS[0]
    out = nc.dram_tensor("out_0", shape, mybir.dt.from_np(_np.dtype(dtype)), kind="ExternalOutput").ap()
    graph_layer(nc, args, out)
    r = _run(nc, [arrays], core_ids=[0])
    return r.results[0]["out_0"]
```
